# Optimizing a Trainium2 kernel written in Bass

```python
import numpy as np
import jax
import jax.numpy as jnp

def _softmax(x, axis=-1):
    return jax.nn.softmax(x, axis=axis)

def _gelu(x):
    return jax.nn.gelu(x, approximate=True)

def _silu(x):
    return jax.nn.silu(x)

def _sigmoid(x):
    return jax.nn.sigmoid(x)

def _layernorm(x, axis=-1, eps=1e-05):
    m = jnp.mean(x, axis=axis, keepdims=True)
    v = jnp.var(x, axis=axis, keepdims=True)
    return (x - m) / jnp.sqrt(v + eps)

def _scatter_add(tgt, idx, src, axis=0):
    return tgt.at[idx].add(src)

def _segment_sum(src, seg, n):
    return jax.ops.segment_sum(src, seg, n)
kernel_name = 'mk_gnn_ffn_d2_gnn_r32_024f51'

def setup_inputs(seed: int=0):
    np.random.seed(seed)
    _w = jnp.asarray

    def _rec_inputs():
        import jax
        import jax.numpy as jnp
        _gk = jax.random.key(seed)
        x = -0.0003713 + 1 * jax.random.normal(jax.random.fold_in(_gk, 1), (3125, 256), jnp.float32)
        src = jax.random.randint(jax.random.fold_in(_gk, 2), (50000,), 0, 3125, jnp.int32)
        dst = jax.random.randint(jax.random.fold_in(_gk, 3), (50000,), 0, 3125, jnp.int32)
        _o = jnp.argsort(dst, stable=True)
        src = src[_o]
        dst = dst[_o]
        edge_attr_32 = 0.000312547 + 1.00004 * jax.random.normal(jax.random.fold_in(_gk, 11), (50000, 32), jnp.float32)
        return (x, src, dst, edge_attr_32)
    x, src, dst, edge_attr_32 = _rec_inputs()

    def _L0_gnn_setup():
        import jax, jax.numpy as jnp
        import numpy as np
        N, E = (50000, 15625)
        D, HID, HEADS = (256, 256, 4)
        PH = HID // HEADS
        ED = 32

        def _add_self_loops(src, dst, ea, n):
            cnt = jax.ops.segment_sum(jnp.ones(src.shape[0], ea.dtype), dst, num_segments=n)
            sm = jax.ops.segment_sum(ea, dst, num_segments=n)
            loop = sm / jnp.maximum(cnt, 1.0)[:, None]
            idx = jnp.arange(n, dtype=src.dtype)
            return (jnp.concatenate([src, idx]), jnp.concatenate([dst, idx]), jnp.concatenate([ea, loop], axis=0))

        def _gat(x, src, dst, ea, Wg, a_s, a_d, Wge, a_e, b, n, h, f):
            hx = (x @ Wg).reshape(n, h, f)
            he = (ea @ Wge).reshape(-1, h, f)
            al = jax.nn.leaky_relu(jnp.einsum('nhf,hf->nh', hx, a_s)[src] + jnp.einsum('nhf,hf->nh', hx, a_d)[dst] + jnp.einsum('ehf,hf->eh', he, a_e), 0.2)
            m = jax.ops.segment_max(al, dst, num_segments=n)
            al = jnp.exp(al - m[dst])
            al = al / jax.ops.segment_sum(al, dst, num_segments=n)[dst]
            out = jax.ops.segment_sum(hx[src] * al[:, :, None], dst, num_segments=n)
            return out.reshape(n, h * f) + b

        def _forward(x, edge_index, edge_attr, We0, be0, We1, be1, Wo0, bo0, Wo1, bo1, Wg0, as0, ad0, Wge0, ae0, bg0, Wg1, as1, ad1, Wge1, ae1, bg1):
            n = x.shape[0]
            src, dst = (edge_index[0], edge_index[1])
            orig = x
            te = jax.nn.relu(edge_attr @ We0 + be0) * jnp.exp(x @ Wo0 + bo0)[src][:, None]
            s2, d2, ea2 = _add_self_loops(src, dst, te, n)
            x = jax.nn.relu(_gat(x, s2, d2, ea2, Wg0, as0, ad0, Wge0, ae0, bg0, n, HEADS, PH) + x)
            te = jax.nn.relu(edge_attr @ We1 + be1) * jnp.exp(x @ Wo1 + bo1)[src][:, None]
            s2, d2, ea2 = _add_self_loops(src, dst, te, n)
            x = _gat(x, s2, d2, ea2, Wg1, as1, ad1, Wge1, ae1, bg1, n, 1, D) + x
            return x + orig
        key = jax.random.key(seed)
        ks = jax.random.split(key, 20)
        r = lambda i, shape, s=1.0: jax.random.normal(ks[i], shape, jnp.float32) * s
        inv = lambda f: 1.0 / float(np.sqrt(f))
        return {'x': r(0, (N, D)), 'edge_index': jax.random.randint(ks[1], (2, E), 0, N, dtype=jnp.int32), 'edge_attr': r(2, (E, ED)), 'We0': r(3, (ED, PH), inv(ED)), 'be0': jnp.zeros((PH,), jnp.float32), 'We1': r(4, (ED, PH), inv(ED)), 'be1': jnp.zeros((PH,), jnp.float32), 'Wo0': r(5, (D,), 0.01), 'bo0': jnp.zeros((), jnp.float32), 'Wo1': r(6, (HID,), 0.01), 'bo1': jnp.zeros((), jnp.float32), 'Wg0': r(7, (D, HEADS * PH), inv(D)), 'as0': r(8, (HEADS, PH), 0.1), 'ad0': r(9, (HEADS, PH), 0.1), 'Wge0': r(10, (PH, HEADS * PH), inv(PH)), 'ae0': r(11, (HEADS, PH), 0.1), 'bg0': jnp.zeros((HEADS * PH,), jnp.float32), 'Wg1': r(12, (HID, D), inv(HID)), 'as1': r(13, (1, D), 0.1), 'ad1': r(14, (1, D), 0.1), 'Wge1': r(15, (PH, D), inv(PH)), 'ae1': r(16, (1, D), 0.1), 'bg1': jnp.zeros((D,), jnp.float32)}
    _L0_gnn_all = _L0_gnn_setup()
    _L0_gnn_in = {k: v for k, v in _L0_gnn_all.items() if k in ('We0', 'be0', 'We1', 'be1', 'Wo0', 'bo0', 'Wo1', 'bo1', 'Wg0', 'as0', 'ad0', 'Wge0', 'ae0', 'bg0', 'Wg1', 'as1', 'ad1', 'Wge1', 'ae1', 'bg1')}
    del _L0_gnn_all

    def _L0_ffn_setup():
        import math
        import jax, jax.numpy as jnp
        import numpy as np
        CAPACITY_FACTOR = 1.25
        key = jax.random.key(seed)
        ks = jax.random.split(key, 5)
        B, L, D, F, E = (8, 256, 256, 1024, 8)
        h = jax.random.normal(ks[0], (B, L, D), dtype=jnp.float32)
        gate_w = jax.random.normal(ks[1], (D, E), dtype=jnp.float32) * 0.02
        gate_b = jnp.zeros((E,), dtype=jnp.float32)
        w1 = jax.random.normal(ks[2], (E, D, F), dtype=jnp.float32) * (1.0 / math.sqrt(D))
        b1 = jnp.zeros((E, F), dtype=jnp.float32)
        w2 = jax.random.normal(ks[3], (E, F, D), dtype=jnp.float32) * (1.0 / math.sqrt(F))
        b2 = jnp.zeros((E, D), dtype=jnp.float32)
        return {'h': h, 'gate_w': gate_w, 'gate_b': gate_b, 'w1': w1, 'b1': b1, 'w2': w2, 'b2': b2}
    _L0_ffn_all = _L0_ffn_setup()
    _L0_ffn_in = {k: v for k, v in _L0_ffn_all.items() if k in ('gate_w', 'gate_b', 'w1', 'b1', 'w2', 'b2')}
    del _L0_ffn_all

    def _L1_gnn_setup():
        import jax, jax.numpy as jnp
        import numpy as np
        N = 3125
        M = 100000
        C = 256
        K = 5

        def _gcn_norm(edge_index, n):
            loop = jnp.arange(n, dtype=edge_index.dtype)
            row = jnp.concatenate([edge_index[0], loop])
            col = jnp.concatenate([edge_index[1], loop])
            w = jnp.ones(row.shape[0], dtype=jnp.float32)
            deg = jax.ops.segment_sum(w, col, num_segments=n)
            dis = jnp.where(deg > 0, jax.lax.rsqrt(deg), 0.0)
            norm = dis[row] * w * dis[col]
            return (row, col, norm)
        key = jax.random.key(seed)
        k1, k2, k3, k4 = jax.random.split(key, 4)
        x = jax.random.normal(k1, (N, C), dtype=jnp.float32)
        edge_index = jax.random.randint(k2, (2, M), 0, N, dtype=jnp.int64)
        lim = float(np.sqrt(6.0 / (C + 1)))
        lin_w = jax.random.uniform(k3, (1, C), dtype=jnp.float32, minval=-lim, maxval=lim)
        lin_b = jax.random.uniform(k4, (1,), dtype=jnp.float32, minval=-lim, maxval=lim)
        return {'x': x, 'edge_index': edge_index, 'lin_w': lin_w, 'lin_b': lin_b}
    _L1_gnn_all = _L1_gnn_setup()
    _L1_gnn_in = {k: v for k, v in _L1_gnn_all.items() if k in ('lin_w', 'lin_b')}
    del _L1_gnn_all

    def _L1_ffn_setup():
        import jax, jax.numpy as jnp
        import numpy as np
        DIM = 256
        H = 8
        D = 64
        G = 64
        INNER = H * D
        SCALE = D ** (-0.5)
        key = jax.random.key(seed)
        ks = jax.random.split(key, 12)
        B, N = (4, 512)
        x = jax.random.normal(ks[0], (B, N, DIM), dtype=jnp.float32)
        s = lambda fan_in: 1.0 / np.sqrt(fan_in)
        W_fx = jax.random.normal(ks[1], (DIM, INNER), dtype=jnp.float32) * s(DIM)
        b_fx = jnp.zeros((INNER,), dtype=jnp.float32)
        W_x = jax.random.normal(ks[2], (DIM, INNER), dtype=jnp.float32) * s(DIM)
        b_x = jnp.zeros((INNER,), dtype=jnp.float32)
        A = jax.random.normal(ks[3], (G, D), dtype=jnp.float32)
        Q, _ = jnp.linalg.qr(A.T)
        W_slice = Q[:, :G].astype(jnp.float32)
        b_slice = jnp.zeros((G,), dtype=jnp.float32)
        W_q = jax.random.normal(ks[4], (D, D), dtype=jnp.float32) * s(D)
        W_k = jax.random.normal(ks[5], (D, D), dtype=jnp.float32) * s(D)
        W_v = jax.random.normal(ks[6], (D, D), dtype=jnp.float32) * s(D)
        W_out = jax.random.normal(ks[7], (INNER, DIM), dtype=jnp.float32) * s(INNER)
        b_out = jnp.zeros((DIM,), dtype=jnp.float32)
        temperature = jnp.ones((1, H, 1, 1), dtype=jnp.float32) * 0.5
        return {'x': x, 'W_fx': W_fx, 'b_fx': b_fx, 'W_x': W_x, 'b_x': b_x, 'W_slice': W_slice, 'b_slice': b_slice, 'W_q': W_q, 'W_k': W_k, 'W_v': W_v, 'W_out': W_out, 'b_out': b_out, 'temperature': temperature}
    _L1_ffn_all = _L1_ffn_setup()
    _L1_ffn_in = {k: v for k, v in _L1_ffn_all.items() if k in ('W_fx', 'b_fx', 'W_x', 'b_x', 'W_slice', 'b_slice', 'W_q', 'W_k', 'W_v', 'W_out', 'b_out', 'temperature')}
    del _L1_ffn_all
    return {'x': x, 'src': src, 'dst': dst, 'edge_attr_32': edge_attr_32, 'L0_gnn_We0': _L0_gnn_in['We0'], 'L0_gnn_be0': _L0_gnn_in['be0'], 'L0_gnn_We1': _L0_gnn_in['We1'], 'L0_gnn_be1': _L0_gnn_in['be1'], 'L0_gnn_Wo0': _L0_gnn_in['Wo0'], 'L0_gnn_bo0': _L0_gnn_in['bo0'], 'L0_gnn_Wo1': _L0_gnn_in['Wo1'], 'L0_gnn_bo1': _L0_gnn_in['bo1'], 'L0_gnn_Wg0': _L0_gnn_in['Wg0'], 'L0_gnn_as0': _L0_gnn_in['as0'], 'L0_gnn_ad0': _L0_gnn_in['ad0'], 'L0_gnn_Wge0': _L0_gnn_in['Wge0'], 'L0_gnn_ae0': _L0_gnn_in['ae0'], 'L0_gnn_bg0': _L0_gnn_in['bg0'], 'L0_gnn_Wg1': _L0_gnn_in['Wg1'], 'L0_gnn_as1': _L0_gnn_in['as1'], 'L0_gnn_ad1': _L0_gnn_in['ad1'], 'L0_gnn_Wge1': _L0_gnn_in['Wge1'], 'L0_gnn_ae1': _L0_gnn_in['ae1'], 'L0_gnn_bg1': _L0_gnn_in['bg1'], 'L0_ffn_gate_w': _L0_ffn_in['gate_w'], 'L0_ffn_gate_b': _L0_ffn_in['gate_b'], 'L0_ffn_w1': _L0_ffn_in['w1'], 'L0_ffn_b1': _L0_ffn_in['b1'], 'L0_ffn_w2': _L0_ffn_in['w2'], 'L0_ffn_b2': _L0_ffn_in['b2'], 'L1_gnn_lin_w': _L1_gnn_in['lin_w'], 'L1_gnn_lin_b': _L1_gnn_in['lin_b'], 'L1_ffn_W_fx': _L1_ffn_in['W_fx'], 'L1_ffn_b_fx': _L1_ffn_in['b_fx'], 'L1_ffn_W_x': _L1_ffn_in['W_x'], 'L1_ffn_b_x': _L1_ffn_in['b_x'], 'L1_ffn_W_slice': _L1_ffn_in['W_slice'], 'L1_ffn_b_slice': _L1_ffn_in['b_slice'], 'L1_ffn_W_q': _L1_ffn_in['W_q'], 'L1_ffn_W_k': _L1_ffn_in['W_k'], 'L1_ffn_W_v': _L1_ffn_in['W_v'], 'L1_ffn_W_out': _L1_ffn_in['W_out'], 'L1_ffn_b_out': _L1_ffn_in['b_out'], 'L1_ffn_temperature': _L1_ffn_in['temperature']}

def reference(x, src, dst, edge_attr_32, L0_gnn_We0, L0_gnn_be0, L0_gnn_We1, L0_gnn_be1, L0_gnn_Wo0, L0_gnn_bo0, L0_gnn_Wo1, L0_gnn_bo1, L0_gnn_Wg0, L0_gnn_as0, L0_gnn_ad0, L0_gnn_Wge0, L0_gnn_ae0, L0_gnn_bg0, L0_gnn_Wg1, L0_gnn_as1, L0_gnn_ad1, L0_gnn_Wge1, L0_gnn_ae1, L0_gnn_bg1, L0_ffn_gate_w, L0_ffn_gate_b, L0_ffn_w1, L0_ffn_b1, L0_ffn_w2, L0_ffn_b2, L1_gnn_lin_w, L1_gnn_lin_b, L1_ffn_W_fx, L1_ffn_b_fx, L1_ffn_W_x, L1_ffn_b_x, L1_ffn_W_slice, L1_ffn_b_slice, L1_ffn_W_q, L1_ffn_W_k, L1_ffn_W_v, L1_ffn_W_out, L1_ffn_b_out, L1_ffn_temperature):
    import jax
    import jax.numpy as jnp

    def _L0_gnn_ref(x, edge_index, edge_attr, We0, be0, We1, be1, Wo0, bo0, Wo1, bo1, Wg0, as0, ad0, Wge0, ae0, bg0, Wg1, as1, ad1, Wge1, ae1, bg1):
        import jax, jax.numpy as jnp
        import numpy as np
        N, E = (50000, 15625)
        D, HID, HEADS = (256, 256, 4)
        PH = HID // HEADS
        ED = 32

        def _add_self_loops(src, dst, ea, n):
            cnt = jax.ops.segment_sum(jnp.ones(src.shape[0], ea.dtype), dst, num_segments=n)
            sm = jax.ops.segment_sum(ea, dst, num_segments=n)
            loop = sm / jnp.maximum(cnt, 1.0)[:, None]
            idx = jnp.arange(n, dtype=src.dtype)
            return (jnp.concatenate([src, idx]), jnp.concatenate([dst, idx]), jnp.concatenate([ea, loop], axis=0))

        def _gat(x, src, dst, ea, Wg, a_s, a_d, Wge, a_e, b, n, h, f):
            hx = (x @ Wg).reshape(n, h, f)
            he = (ea @ Wge).reshape(-1, h, f)
            al = jax.nn.leaky_relu(jnp.einsum('nhf,hf->nh', hx, a_s)[src] + jnp.einsum('nhf,hf->nh', hx, a_d)[dst] + jnp.einsum('ehf,hf->eh', he, a_e), 0.2)
            m = jax.ops.segment_max(al, dst, num_segments=n)
            al = jnp.exp(al - m[dst])
            al = al / jax.ops.segment_sum(al, dst, num_segments=n)[dst]
            out = jax.ops.segment_sum(hx[src] * al[:, :, None], dst, num_segments=n)
            return out.reshape(n, h * f) + b

        def _forward(x, edge_index, edge_attr, We0, be0, We1, be1, Wo0, bo0, Wo1, bo1, Wg0, as0, ad0, Wge0, ae0, bg0, Wg1, as1, ad1, Wge1, ae1, bg1):
            n = x.shape[0]
            src, dst = (edge_index[0], edge_index[1])
            orig = x
            te = jax.nn.relu(edge_attr @ We0 + be0) * jnp.exp(x @ Wo0 + bo0)[src][:, None]
            s2, d2, ea2 = _add_self_loops(src, dst, te, n)
            x = jax.nn.relu(_gat(x, s2, d2, ea2, Wg0, as0, ad0, Wge0, ae0, bg0, n, HEADS, PH) + x)
            te = jax.nn.relu(edge_attr @ We1 + be1) * jnp.exp(x @ Wo1 + bo1)[src][:, None]
            s2, d2, ea2 = _add_self_loops(src, dst, te, n)
            x = _gat(x, s2, d2, ea2, Wg1, as1, ad1, Wge1, ae1, bg1, n, 1, D) + x
            return x + orig
        return _forward(x, edge_index, edge_attr, We0, be0, We1, be1, Wo0, bo0, Wo1, bo1, Wg0, as0, ad0, Wge0, ae0, bg0, Wg1, as1, ad1, Wge1, ae1, bg1)

    def _L0_ffn_ref(h, gate_w, gate_b, w1, b1, w2, b2):
        import math
        import jax, jax.numpy as jnp
        import numpy as np
        CAPACITY_FACTOR = 1.25
        B, L, D = h.shape
        E = gate_w.shape[1]
        T = B * L
        C = max(1, math.ceil(CAPACITY_FACTOR * T / E))
        x = h.reshape(T, D)
        logits = x @ gate_w + gate_b
        probs = jax.nn.softmax(logits, axis=-1)
        idx = jnp.argmax(probs, axis=-1)
        prb = jnp.take_along_axis(probs, idx[:, None], axis=1)[:, 0]
        one_hot = jax.nn.one_hot(idx, E, dtype=jnp.float32)
        pos = (jnp.cumsum(one_hot, axis=0) * one_hot).sum(-1).astype(jnp.int32) - 1
        kept = pos < C
        pos_safe = jnp.where(kept, pos, C)
        buf = jnp.zeros((E, C, D), dtype=h.dtype).at[idx, pos_safe].set(x, mode='drop')
        hmid = jax.nn.relu(jnp.einsum('ecd,edf->ecf', buf, w1) + b1[:, None, :])
        ybuf = jnp.einsum('ecf,efd->ecd', hmid, w2) + b2[:, None, :]
        pos_g = jnp.minimum(pos, C - 1)
        y_tok = ybuf[idx, pos_g] * (prb * kept)[:, None]
        y = y_tok.reshape(B, L, D)
        y = jnp.nan_to_num(y, nan=0.0, posinf=10000.0, neginf=-10000.0)
        return y

    def _L1_gnn_ref(x, edge_index, lin_w, lin_b):
        import jax, jax.numpy as jnp
        import numpy as np
        N = 3125
        M = 100000
        C = 256
        K = 5

        def _gcn_norm(edge_index, n):
            loop = jnp.arange(n, dtype=edge_index.dtype)
            row = jnp.concatenate([edge_index[0], loop])
            col = jnp.concatenate([edge_index[1], loop])
            w = jnp.ones(row.shape[0], dtype=jnp.float32)
            deg = jax.ops.segment_sum(w, col, num_segments=n)
            dis = jnp.where(deg > 0, jax.lax.rsqrt(deg), 0.0)
            norm = dis[row] * w * dis[col]
            return (row, col, norm)
        n = x.shape[0]
        row, col, norm = _gcn_norm(edge_index, n)
        xs = [x]
        h = x
        for _ in range(K):
            h = jax.ops.segment_sum(norm[:, None] * h[col], row, num_segments=n)
            xs.append(h)
        H = jnp.stack(xs, axis=1)
        S = jax.nn.sigmoid(H @ lin_w.T + lin_b)
        out = jnp.sum(S * H, axis=1)
        return out

    def _L1_ffn_ref(x, W_fx, b_fx, W_x, b_x, W_slice, b_slice, W_q, W_k, W_v, W_out, b_out, temperature):
        import jax, jax.numpy as jnp
        import numpy as np
        DIM = 256
        H = 8
        D = 64
        G = 64
        INNER = H * D
        SCALE = D ** (-0.5)
        B, N, _ = x.shape
        fx_mid = (x @ W_fx + b_fx).reshape(B, N, H, D).transpose(0, 2, 1, 3)
        x_mid = (x @ W_x + b_x).reshape(B, N, H, D).transpose(0, 2, 1, 3)
        temp = jnp.clip(temperature, 0.1, 5.0)
        slice_weights = jax.nn.softmax((x_mid @ W_slice + b_slice) / temp, axis=-1)
        slice_norm = slice_weights.sum(axis=2)
        slice_token = jnp.einsum('bhnc,bhng->bhgc', fx_mid, slice_weights)
        slice_token = slice_token / (slice_norm[..., None] + 1e-05)
        q = slice_token @ W_q
        k = slice_token @ W_k
        v = slice_token @ W_v
        attn = jax.nn.softmax(jnp.einsum('bhgc,bhkc->bhgk', q, k) * SCALE, axis=-1)
        out_slice = jnp.einsum('bhgk,bhkc->bhgc', attn, v)
        out_x = jnp.einsum('bhgc,bhng->bhnc', out_slice, slice_weights)
        out_x = out_x.transpose(0, 2, 1, 3).reshape(B, N, INNER)
        return out_x @ W_out + b_out
    edge_index = jnp.stack([src, dst])
    x = x + _L0_gnn_ref(_layernorm(x, axis=-1), edge_index, edge_attr_32, L0_gnn_We0, L0_gnn_be0, L0_gnn_We1, L0_gnn_be1, L0_gnn_Wo0, L0_gnn_bo0, L0_gnn_Wo1, L0_gnn_bo1, L0_gnn_Wg0, L0_gnn_as0, L0_gnn_ad0, L0_gnn_Wge0, L0_gnn_ae0, L0_gnn_bg0, L0_gnn_Wg1, L0_gnn_as1, L0_gnn_ad1, L0_gnn_Wge1, L0_gnn_ae1, L0_gnn_bg1)
    x = x + _L0_ffn_ref(_layernorm(x, axis=-1)[None], L0_ffn_gate_w, L0_ffn_gate_b, L0_ffn_w1, L0_ffn_b1, L0_ffn_w2, L0_ffn_b2)[0]
    x = x + _L1_gnn_ref(_layernorm(x, axis=-1), edge_index, L1_gnn_lin_w, L1_gnn_lin_b)
    x = x + _L1_ffn_ref(_layernorm(x, axis=-1)[None], L1_ffn_W_fx, L1_ffn_b_fx, L1_ffn_W_x, L1_ffn_b_x, L1_ffn_W_slice, L1_ffn_b_slice, L1_ffn_W_q, L1_ffn_W_k, L1_ffn_W_v, L1_ffn_W_out, L1_ffn_b_out, L1_ffn_temperature)[0]
    return x

_drawn_inputs = setup_inputs


def setup_inputs(seed=0):
    import zlib

    import numpy as np

    out = dict(_drawn_inputs(seed))
    spreads = {'L0_gnn_be0': (0.0, 0.8),
     'L0_gnn_be1': (0.0, 0.8),
     'L0_gnn_bg0': (0.0, 0.1),
     'L0_gnn_bg1': (0.0, 0.1),
     'L0_ffn_gate_b': (0.0, 0.1),
     'L0_ffn_b1': (0.0, 0.8),
     'L0_ffn_b2': (0.0, 0.8),
     'L1_ffn_b_fx': (0.0, 0.1),
     'L1_ffn_b_x': (0.0, 0.8),
     'L1_ffn_b_slice': (0.0, 0.8),
     'L1_ffn_b_out': (0.0, 0.267),
     'L1_ffn_temperature': (0.5, 0.6)}
    factors = {'L0_gnn_Wo0': 5.382,
     'L0_gnn_Wo1': 8.0,
     'L0_gnn_ad0': 3.386,
     'L1_ffn_W_x': 8.0,
     'L1_ffn_W_slice': 8.0,
     'L1_ffn_W_q': 8.0,
     'L1_ffn_W_k': 8.0}
    for name, (base, spread) in spreads.items():
        noise = np.random.default_rng([zlib.crc32(name.encode()), seed]).standard_normal(out[name].shape)
        drawn = base * np.exp(spread * noise) if base else spread * noise
        out[name] = jnp.asarray(drawn.astype(out[name].dtype))
    for name, factor in factors.items():
        out[name] = (out[name] * factor).astype(out[name].dtype)
    return out
```

```python
from contextlib import ExitStack

import concourse.bass as bass
from concourse import mybir

P = 128
N, E, D = 3125, 50000, 256
NB = -(-N // P)
NP = NB * P
RING = 8
ET = -(-(-(-E // P)) // RING) * RING
EP = ET * P
ED, PH = 32, 64
HEADS = (4, 1)
SW = 8
ROW = 260
BIG = 1.0e30
LN_EPS = 1e-5
SLOPE = 0.2
NE, CAP, SLOTS, FF = 8, -(-5 * N // (4 * 8)), 512, 1024
HOPS = 5
SH, SD, SG = 8, 64, 64

ALU = mybir.AluOpType
ACT = mybir.ActivationFunctionType
AX = mybir.AxisListType.X
F32, I32, F16, BF16 = mybir.dt.float32, mybir.dt.int32, mybir.dt.float16, mybir.dt.bfloat16


class Linked:

    def __init__(self, eng, sem, base=0):
        self.eng, self.sem, self.base, self.n = eng, sem, base, 0

    def __call__(self, instruction):
        self.n += 1
        instruction.then_inc(self.sem, 1)
        self.eng.wait_ge(self.sem, self.base + self.n)


class Space:

    def __init__(self, nc, ctx, tag):
        self.nc, self.ctx, self.tag, self.sems = nc, ctx, tag, []
        ctx.callback(self.close)

    def close(self):
        self.nc.clear_and_free_semaphores(self.sems)
        self.nc.all_engine_barrier()

    def sb(self, name, shape, dt=F32):
        return self.ctx.enter_context(self.nc.sbuf_tensor(f"{self.tag}_{name}", shape, dt))

    def ps(self, name, shape=(P, 512), dt=F32):
        return self.ctx.enter_context(self.nc.psum_tensor(f"{self.tag}_{name}", list(shape), dt))

    def sem(self, name):
        self.sems.append(self.nc.alloc_semaphore(f"{self.tag}_{name}"))
        return self.sems[-1]


def at(ap, i):
    s = ap[:, bass.ds(i, 1)] if len(ap.shape) == 2 else ap[:, bass.ds(i, 1), :]
    return s if len(ap.shape) == 2 else s.rearrange("p a f -> p (a f)")


def across(row, width):
    return row.rearrange("(a n) -> a n", a=1).to_broadcast([P, width])


def constants(nc, g):
    with ExitStack() as ctx:
        s = Space(nc, ctx, "cst")
        zero = s.sb("zero", [P, 2048])
        made, filled = s.sem("made"), s.sem("filled")
        with nc.Block() as block:
            @block.gpsimd
            def _(pool):
                link = Linked(pool, made)
                link(pool.memset(g.ident[:, :], 0.0))
                link(pool.affine_select(out=g.ident[:, :], in_=g.ident[:, :], compare_op=ALU.not_equal,
                                        fill=1.0, base=0, pattern=[[-1, P]], channel_multiplier=1))
                for tri, base in ((g.tri_upto, 0), (g.tri_below, -1)):
                    link(pool.memset(tri[:, :], 1.0))
                    link(pool.affine_select(out=tri[:, :], in_=tri[:, :], compare_op=ALU.is_ge, fill=0.0,
                                            base=base, pattern=[[1, P]], channel_multiplier=-1))
                link(pool.iota(g.count[:, :], pattern=[[1, P]], base=0, channel_multiplier=0,
                               allow_small_or_imprecise_dtypes=True))

            @block.vector
            def _(dve):
                nc.vector.memset(g.ones[:, :], 1.0)
                nc.vector.memset(zero[:, :], 0.0).then_inc(filled, 1)

            @block.sync
            def _(sp):
                sp.wait_ge(filled, 1)
                sp.dma_start(g.edge_fill.rearrange("(p j) c -> p (j c)", p=P)[:, 0:2048], zero[:, :]).then_inc(filled, 16)
                sp.dma_start(g.edge_fill.rearrange("(p j) c -> p (j c)", p=P)[:, 2048:ET * SW],
                             zero[:, 0:ET * SW - 2048]).then_inc(filled, 16)
                per = NE * SLOTS * D // P // 2048
                for k in range(per):
                    sp.dma_start(g.expert_in.rearrange("(p j) c -> p (j c)", p=P)[:, k * 2048:(k + 1) * 2048],
                                 zero[:, :]).then_inc(filled, 16)
                sp.wait_ge(filled, 1 + 16 * (2 + per))


def graph_tables(nc, g, io):
    with ExitStack() as ctx:
        s = Space(nc, ctx, "grf")
        GRP = 8
        dst_i = s.sb("dst_i", [P, ET], I32)
        digit = s.sb("digit", [P, ET], I32)
        low, high = s.sb("low", [P, ET], F16), s.sb("high", [P, ET], F16)
        count16 = s.sb("count16", [P, P], F16)
        oh_low = s.sb("oh_low", [P, 2 * GRP, P], F16)
        oh_high = s.sb("oh_high", [P, 2 * GRP, NB], F16)
        zero16 = s.sb("zero16", [P, P], F16)
        total, upto = s.sb("total", [P, NB]), s.sb("upto", [P, NB])
        t0, t1 = s.sb("t0", [P, NB]), s.sb("t1", [P, NB])
        hist, prefix = s.ps("hist"), s.ps("prefix")
        loaded, linked, hot, used = s.sem("loaded"), s.sem("linked"), s.sem("hot"), s.sem("used")
        counted, summed, table, rooted = s.sem("counted"), s.sem("summed"), s.sem("table"), s.sem("rooted")
        have = s.sem("have")
        with nc.Block() as block:
            @block.sync
            def _(sp):
                sp.dma_start(dst_i[:, :], io["dst_cols"]).then_inc(loaded, 16)
                sp.dma_start(g.src_i[:, :], io["src_cols"]).then_inc(loaded, 16)

            @block.vector
            def _(dve):
                link = Linked(dve, linked)
                dve.wait_ge(loaded, 32)
                link(nc.vector.memset(zero16[:, :], 0.0))
                link(nc.vector.tensor_copy(count16[:, :], g.count[:, :]))
                link(nc.vector.tensor_copy(g.dst_f[:, :], dst_i[:, :]))
                link(nc.vector.tensor_scalar(digit[:, :], dst_i[:, :], P - 1, None, ALU.bitwise_and))
                link(nc.vector.tensor_copy(low[:, :], digit[:, :]))
                link(nc.vector.tensor_scalar(digit[:, :], dst_i[:, :], 7, None, ALU.logical_shift_right))
                link(nc.vector.tensor_copy(high[:, :], digit[:, :]))
                nc.vector.memset(zero16[:, 0:1], 0.0).then_inc(used, 1)
                with dve.Fori(0, ET // GRP) as i:
                    dve.wait_ge(used, i)
                    nc.vector.tensor_tensor(
                        oh_low[:, bass.ds((i % 2) * GRP, GRP), :], count16[:, :].unsqueeze(1).to_broadcast([P, GRP, P]),
                        low[:, bass.ds(i * GRP, GRP)].unsqueeze(2).to_broadcast([P, GRP, P]), ALU.is_equal)
                    nc.vector.tensor_tensor(
                        oh_high[:, bass.ds((i % 2) * GRP, GRP), :],
                        count16[:, 0:NB].unsqueeze(1).to_broadcast([P, GRP, NB]),
                        high[:, bass.ds(i * GRP, GRP)].unsqueeze(2).to_broadcast([P, GRP, NB]),
                        ALU.is_equal).then_inc(hot, 1)
                dve.wait_ge(counted, 1)
                nc.vector.tensor_copy(g.indeg[:, :], hist[:, 0:NB]).then_inc(have, 1)
                dve.wait_ge(summed, 1)
                link(nc.vector.tensor_copy(total[:, :], prefix[:, 64:64 + NB]))
                link(nc.vector.memset(t0[:, :], 0.0))
                link(nc.vector.tensor_tensor_scan(upto[:, :], total[:, :], t0[:, :], 0.0, ALU.add, ALU.add))
                link(nc.vector.tensor_tensor(t0[:, :], upto[:, :], total[:, :], ALU.subtract))
                link(nc.vector.tensor_tensor(t0[:, :], t0[:, :], prefix[:, 0:NB], ALU.add))
                link(nc.vector.tensor_scalar(t1[:, :], g.indeg[:, :], 0.0, float(2 * EP), ALU.is_equal, ALU.mult))
                link(nc.vector.tensor_tensor(t1[:, :], t1[:, :], t0[:, :], ALU.add))
                link(nc.vector.tensor_copy(g.seg_start[:, :], t1[:, :]))
                link(nc.vector.tensor_tensor(t0[:, :], t0[:, :], g.indeg[:, :], ALU.add))
                link(nc.vector.tensor_scalar(t0[:, :], t0[:, :], -1.0, 0.0, ALU.add, ALU.max))
                link(nc.vector.tensor_copy(g.seg_end[:, :], t0[:, :]))
                link(nc.vector.tensor_copy(g.tiles[:, 1:NB + 1], upto[:, :]))
                link(nc.vector.tensor_scalar(g.tiles[:, 1:NB + 1], g.tiles[:, 1:NB + 1], 7, None,
                                             ALU.logical_shift_right))
                link(nc.vector.tensor_scalar(g.tiles[:, 1:NB + 1], g.tiles[:, 1:NB + 1], float(ET - 1), None, ALU.min))
                link(nc.vector.memset(g.tiles[:, 0:1], 0))
                link(nc.vector.tensor_scalar(g.minus_base[:, :], g.count[:, 0:NB], float(-P), None, ALU.mult))
                link(nc.vector.tensor_scalar(g.has[:, :], g.indeg[:, :], 1.0, None, ALU.min))
                link(nc.vector.tensor_scalar(t0[:, :], g.indeg[:, :], 1.0, None, ALU.max))
                link(nc.vector.reciprocal(g.inv_deg[:, :], t0[:, :]))
                nc.vector.tensor_scalar(t1[:, :], g.indeg[:, :], 1.0, None, ALU.add).then_inc(table, 1)
                dve.wait_ge(rooted, 1)
                nc.vector.reciprocal(g.dis[:, :], t1[:, :]).then_inc(table, 1)

            @block.scalar
            def _(act):
                act.wait_ge(table, 1)
                nc.scalar.activation(t1[:, :], t1[:, :], ACT.Sqrt).then_inc(rooted, 1)

            @block.tensor
            def _(pe):
                pe.wait_ge(hot, 1)
                nc.tensor.matmul(hist[:, 0:NB], zero16[:, :], oh_high[:, 0, :], start=True, stop=False,
                                 skip_group_check=True)
                with pe.Fori(0, ET // GRP) as i:
                    pe.wait_ge(hot, i + 1)
                    for k in range(GRP):
                        mm = nc.tensor.matmul(hist[:, 0:NB], at(oh_low, (i % 2) * GRP + k), at(oh_high, (i % 2) * GRP + k),
                                              start=False, stop=False, skip_group_check=True)
                    mm.then_inc(used, 1)
                nc.tensor.matmul(hist[:, 0:NB], zero16[:, :], oh_high[:, 0, :], start=False, stop=True,
                                 skip_group_check=True).then_inc(counted, 1)
                pe.wait_ge(have, 1)
                nc.tensor.matmul(prefix[:, 0:NB], g.tri_below[:, :], g.indeg[:, :], start=True, stop=True)
                nc.tensor.matmul(prefix[:, 64:64 + NB], g.ones[:, :], g.indeg[:, :], start=True,
                                 stop=True).then_inc(summed, 1)


def inverse_root(dve, link, out, var, root, half):
    link(dve.reciprocal(out, root))
    link(dve.tensor_tensor(half, out, out, ALU.mult))
    link(dve.tensor_tensor(half, half, var, ALU.mult))
    link(dve.tensor_scalar(half, half, -0.5, 1.5, ALU.mult, ALU.add))
    link(dve.tensor_tensor(out, out, half, ALU.mult))


class Norm:

    def __init__(self, s):
        self.stats, self.pair = s.sb("stats", [P, NB, 6]), s.sb("pair", [P, NB, 2])
        self.mean, self.var = s.sb("mean", [P, NB]), s.sb("var", [P, NB])
        self.root, self.half, self.rstd = (s.sb(n, [P, NB]) for n in ("root", "half", "rstd"))
        self.varied, self.rooted = s.sem("varied"), s.sem("rooted")

    def on_vector(self, dve, sem, x):
        with dve.Fori(0, NB) as b:
            dve.bn_stats(at(self.stats, b), at(x, b)).then_inc(sem, 1)
        dve.wait_ge(sem, NB)
        link = Linked(dve, sem, NB)
        for b in range(NB):
            last = dve.bn_aggr(self.pair[:, b, :], self.stats[:, b, :])
        link(last)
        link(dve.tensor_scalar(self.var[:, :], self.pair[:, :, 1], LN_EPS, None, ALU.add))
        link(dve.tensor_copy(self.mean[:, :], self.pair[:, :, 0]))
        dve.sem_inc(self.varied, 1)
        dve.wait_ge(self.rooted, 1)
        inverse_root(dve, link, self.rstd[:, :], self.var[:, :], self.root[:, :], self.half[:, :])

    def block(self, dve, out, x, b):
        return dve.tensor_scalar(out, at(x, b), at(self.mean, b), at(self.rstd, b), ALU.subtract, ALU.mult)

    def on_scalar(self, act):
        act.wait_ge(self.varied, 1)
        act.activation(self.root[:, :], self.var[:, :], ACT.Sqrt).then_inc(self.rooted, 1)


def pairs(eng, body):
    with eng.Fori(0, NB // 2) as j:
        body(((2 * j, 0, j), (2 * j + 1, 1, j)))
    if NB % 2:
        body(((NB - 1, 0, NB // 2),))


def project_nodes(nc, g, io, layer, x_in, normalise):
    H = HEADS[layer]
    F = D // H
    W = D + 2 * H + 1
    with ExitStack() as ctx:
        s = Space(nc, ctx, f"prj{layer}")
        x = s.sb("x", [P, NB, D])
        w = s.sb("w", [P, 2, W])
        wo = s.sb("wo", [P, 2])
        a_row = s.sb("a_row", [P, 2, D])
        prod = s.sb("prod", [P, D])
        bo = s.sb("bo", [P, 1])
        xs = [s.sb(f"xs{i}", [P, D]) for i in range(2)]
        xt = [s.sb(f"xt{i}", [P, 2, P]) for i in range(2)]
        full = [s.sb(f"row{i}", [P, ROW]) for i in range(2)]
        row = [r[:, 0:H * (F + 1)].rearrange("p (h f) -> p h f", h=H) for r in full]
        sums = s.sb("sums", [P, NB, 2 * H + 1])
        norm = Norm(s) if normalise else None
        turned = [s.ps(f"turned{i}") for i in range(2)]
        prod_ps = [s.ps(f"prod_ps{i}") for i in range(2)]
        loaded, wts, linked, link2, wready = (s.sem(n) for n in ("loaded", "wts", "linked", "link2", "wready"))
        fed, t_done, t_copied, m_done, m_read, stored, kept = (
            [s.sem(f"{n}{i}") for i in range(2)]
            for n in ("fed", "t_done", "t_copied", "m_done", "m_read", "stored", "kept"))
        summed, expd, tabled, out_done = (s.sem(n) for n in ("summed", "expd", "tabled", "out_done"))
        nm = lambda n: io[f"L0_gnn_{n}{layer}"]
        with nc.Block() as block:
            @block.sync
            def _(sp):
                sp.dma_start(x[:, :, :], x_in.rearrange("(b p) d -> p b d", p=P)).then_inc(loaded, 16)
                sp.dma_start(w[:, :, 0:D], nm("Wg").rearrange("(p k) n -> p k n", p=P)).then_inc(wts, 16)
                sp.dma_start(wo[:, :], nm("Wo").rearrange("(p k) -> p k", p=P)).then_inc(wts, 16)
                sp.dma_start(a_row[:, 0, :], across(nm("as").rearrange("h f -> (h f)"), D)).then_inc(wts, 16)
                sp.dma_start(a_row[:, 1, :], across(nm("ad").rearrange("h f -> (h f)"), D)).then_inc(wts, 16)
                sp.dma_start(bo[:, :], across(nm("bo"), 1)).then_inc(wts, 16)

                def body(blocks):
                    if normalise:
                        for b, i, j in blocks:
                            sp.wait_ge(fed[i], j + 1)
                            sp.dma_start(g.x_norm[bass.ds(b * P, P), :], xs[i][:, :]).then_inc(kept[i], 16)
                    for b, i, j in blocks:
                        sp.wait_ge(m_read[i], j + 1)
                        sp.dma_start(g.hx_rows[bass.ds(b * P, P), :], full[i][:, :]).then_inc(stored[i], 16)
                pairs(sp, body)
                sp.wait_ge(tabled, 1)
                sp.dma_start(g.small.rearrange("(b p) c -> p b c", p=P), g.small_sb[:, :, :]).then_inc(out_done, 16)
                sp.wait_ge(out_done, 16)
                for i, turns in ((0, -(-NB // 2)), (1, NB // 2)):
                    sp.wait_ge(stored[i], 16 * turns)
                    if normalise:
                        sp.wait_ge(kept[i], 16 * turns)

            @block.vector
            def _(dve):
                dve.wait_ge(loaded, 16)
                if normalise:
                    norm.on_vector(dve, linked, x)
                dve.wait_ge(wts, 80)
                link = Linked(dve, link2)
                for k in range(2):
                    for c in range(2):
                        link(dve.tensor_tensor(prod[:, :], w[:, k, 0:D], a_row[:, c, :], ALU.mult))
                        link(dve.tensor_reduce(w[:, k, D + c * H:D + (c + 1) * H],
                                               prod[:, :].rearrange("p (h f) -> p h f", h=H), AX, ALU.add))
                link(dve.tensor_copy(w[:, :, W - 1], wo[:, :]))
                link(dve.memset(full[0][:, :], 1.0))
                link(dve.memset(full[1][:, :], 1.0))
                dve.sem_inc(wready, 1)

                def body(blocks):
                    for b, i, j in blocks:
                        dve.wait_ge(t_done[i], j)
                        if normalise:
                            dve.wait_ge(kept[i], 16 * j)
                            norm.block(dve, xs[i][:, :], x, b).then_inc(fed[i], 1)
                        else:
                            dve.tensor_copy(xs[i][:, :], at(x, b)).then_inc(fed[i], 1)
                    for b, i, j in blocks:
                        dve.wait_ge(m_done[i], j + 1)
                        dve.wait_ge(stored[i], 16 * j)
                        dve.tensor_copy(row[i][:, :, 0:F], prod_ps[i][:, 0:D].rearrange("p (h f) -> p h f", h=H))
                        dve.tensor_copy(at(sums, b), prod_ps[i][:, D:W]).then_inc(m_read[i], 1)
                pairs(dve, body)
                dve.wait_ge(m_read[0], -(-NB // 2))
                dve.wait_ge(m_read[1], NB // 2)
                link(dve.memset(g.small_sb[:, :, :], 0.0))
                link(dve.tensor_copy(g.small_sb[:, :, 0:H], sums[:, :, 0:H]))
                dve.tensor_copy(g.node_d[:, :, 0:H], sums[:, :, H:2 * H]).then_inc(summed, 1)

            @block.scalar
            def _(act):
                if normalise:
                    norm.on_scalar(act)

                def body(blocks):
                    for b, i, j in blocks:
                        act.wait_ge(t_done[i], j + 1)
                        act.wait_ge(m_done[i], j)
                        act.activation(xt[i][:, :, :].rearrange("p k n -> p (k n)"), turned[i][:, 0:2 * P],
                                       ACT.Copy).then_inc(t_copied[i], 1)
                pairs(act, body)
                act.wait_ge(summed, 1)
                act.activation(g.small_sb[:, :, 4], sums[:, :, 2 * H], ACT.Exp, bias=bo[:, 0:1]).then_inc(tabled, 1)

            @block.tensor
            def _(pe):
                pe.wait_ge(loaded, 16)
                pe.wait_ge(wready, 1)

                def body(blocks):
                    for b, i, j in blocks:
                        pe.wait_ge(fed[i], j + 1)
                        pe.wait_ge(t_copied[i], j)
                        for k in range(2):
                            mm = pe.transpose(turned[i][:, k * P:(k + 1) * P], xs[i][:, k:D:2], g.ident[:, :])
                        mm.then_inc(t_done[i], 1)
                    for b, i, j in blocks:
                        pe.wait_ge(t_copied[i], j + 1)
                        pe.wait_ge(m_read[i], j)
                        for k in range(2):
                            mm = pe.matmul(prod_ps[i][:, 0:W], xt[i][:, k, :], w[:, k, :], start=(k == 0), stop=(k == 1))
                        mm.then_inc(m_done[i], 1)
                pairs(pe, body)


def edge_terms(nc, g, io):
    with ExitStack() as ctx:
        s = Space(nc, ctx, "edg")
        COLS = 8
        WIDE = COLS * P // 2
        HT = sum(HEADS)
        ea = s.sb("ea", [ED, 2, COLS * P])
        we = s.sb("we", [ED, 2 * PH])
        be = s.sb("be", [2 * PH, 1])
        wge, ae = s.sb("wge", [P, D]), s.sb("ae", [P, D])
        v = s.sb("v", [P, HT])
        hid = [s.sb(f"hid{i}", [P, WIDE]) for i in range(2)]
        terms = s.sb("terms", [P, HT, ET])
        up = [s.ps(f"up{i}") for i in range(2)]
        down = s.ps("down")
        wts, linked, ready, out_done = (s.sem(n) for n in ("wts", "linked", "ready", "out_done"))
        came = [s.sem(f"came{i}") for i in range(2)]
        upped, activated, downed, copied = (s.sem(n) for n in ("upped", "activated", "downed", "copied"))
        turns = ET // COLS
        with nc.Block() as block:
            @block.sync
            def _(sp):
                for n in range(2):
                    lo, hi = n * PH, (n + 1) * PH
                    sp.dma_start(we[:, lo:hi], io[f"L0_gnn_We{n}"]).then_inc(wts, 16)
                    sp.dma_start(be[lo:hi, :], io[f"L0_gnn_be{n}"].rearrange("(p a) -> p a", a=1)).then_inc(wts, 16)
                    sp.dma_start(wge[lo:hi, :], io[f"L0_gnn_Wge{n}"]).then_inc(wts, 16)
                    sp.dma_start(ae[lo:hi, :], io[f"L0_gnn_ae{n}"].rearrange("h f -> (h f)").rearrange(
                        "(a n) -> a n", a=1).to_broadcast([PH, D])).then_inc(wts, 16)

                def load(j, i):
                    sp.dma_start(ea[:, i, :], io["edge_attr"][:, bass.ds(j * COLS, COLS), :].rearrange(
                        "f j p -> f (j p)")).then_inc(came[i], 16)

                with sp.Fori(0, turns // 2) as j:
                    sp.wait_ge(upped, 4 * j)
                    load(2 * j, 0)
                    sp.wait_ge(upped, 4 * j + 1)
                    load(2 * j + 1, 1)
                sp.wait_ge(upped, 2 * (turns - 1))
                load(turns - 1, 0)
                sp.wait_ge(copied, turns)
                sp.dma_start(g.edge_terms, terms[:, :, :]).then_inc(out_done, 16)
                sp.wait_ge(out_done, 16)

            @block.vector
            def _(dve):
                link = Linked(dve, linked)
                dve.wait_ge(wts, 16 * 8)
                link(dve.memset(v[:, :], 0.0))
                link(dve.tensor_tensor(wge[:, :], wge[:, :], ae[:, :], ALU.mult))
                for n, lo in ((0, 0), (1, HEADS[0])):
                    link(dve.tensor_reduce(v[n * PH:(n + 1) * PH, lo:lo + HEADS[n]],
                                           wge[n * PH:(n + 1) * PH, :].rearrange("p (h f) -> p h f", h=HEADS[n]),
                                           AX, ALU.add))
                dve.sem_inc(ready, 1)
                with dve.Fori(0, turns) as j:
                    dve.wait_ge(downed, 2 * j + 2)
                    dve.tensor_copy(terms[:, :, bass.ds(j * COLS, COLS)],
                                    down[:, 0:COLS * HT].rearrange("p (c h) -> p h c", h=HT)).then_inc(copied, 1)

            @block.scalar
            def _(act):
                with act.Fori(0, turns) as j:
                    for i in range(2):
                        act.wait_ge(upped, 2 * j + i + 1)
                        act.wait_ge(downed, 2 * j + i)
                        act.activation(hid[i][:, :], up[i][:, :], ACT.Relu, bias=be[:, 0:1]).then_inc(activated, 1)

            @block.tensor
            def _(pe):
                pe.wait_ge(ready, 1)

                def turn(j, i, nth):
                    pe.wait_ge(came[i], 16 * nth)
                    pe.wait_ge(activated, 2 * j)
                    for k in range(2):
                        pe.matmul(up[k][:, :], we[:, :], ea[:, i, k * WIDE:(k + 1) * WIDE], start=True,
                                  stop=True).then_inc(upped, 1)
                    pe.wait_ge(copied, j)
                    for k in range(2):
                        pe.wait_ge(activated, 2 * j + k + 1)
                        for c in range(COLS // 2):
                            col = (k * (COLS // 2) + c) * HT
                            mm = pe.matmul(down[:, col:col + HT], hid[k][:, c * P:(c + 1) * P], v[:, :],
                                           start=True, stop=True)
                        mm.then_inc(downed, 1)

                with pe.Fori(0, turns // 2) as j:
                    turn(2 * j, 0, j + 1)
                    turn(2 * j + 1, 1, j + 1)
                turn(turns - 1, 0, turns // 2 + 1)


def gather_small(s, g, io):
    half = RING // 2
    ring = s.sb("ring", [P, RING, SW])
    ids = s.sb("ids", [P, ET], I32)
    now = [s.sb(f"now{i}", [P, half], I32) for i in range(2)]
    came = [s.sem(f"came{k}") for k in range(RING)]
    listed, picked, taken, gate = (s.sem(n) for n in ("listed", "picked", "taken", "gate"))

    def on_pool(pool):
        def issue(j, i):
            pool.tensor_copy(now[i][:, :], ids[:, bass.ds(j * RING + i * half, half)]).then_inc(picked, 1)
            pool.wait_ge(picked, 2 * j + i + 1)
            pool.sem_inc(gate, 1)
            for k in range(half):
                pool.indirect_dma_start(
                    out=ring[:, i * half + k, :], out_offset=None, in_=g.small,
                    in_offset=bass.IndirectOffsetOnAxis(ap=now[i][:, k:k + 1], axis=0)
                ).then_inc(came[i * half + k], 16)

        def take(j, i):
            for k in range(half):
                pool.wait_ge(came[i * half + k], 16 * (j + 1))
            pool.tensor_copy(g.per_edge[:, bass.ds(j * RING + i * half, half), :],
                             ring[:, i * half:(i + 1) * half, :]).then_inc(taken, 1)
            pool.wait_ge(taken, 2 * j + i + 1)

        pool.dma_start(ids[:, :], io["src_rows"]).then_inc(listed, 16)
        pool.wait_ge(listed, 16)
        issue(0, 0)
        issue(0, 1)
        with pool.Fori(1, ET // RING) as j:
            for i in range(2):
                take(j - 1, i)
                issue(j, i)
        take(ET // RING - 1, 0)
        take(ET // RING - 1, 1)

    return on_pool


def counts_and_gather(nc, g, io):
    with ExitStack() as ctx:
        s = Space(nc, ctx, "cnt")
        BANK = 512
        banks = [(c, min(BANK, NP - c)) for c in range(0, NP, BANK)]
        n_act = (len(banks) + 1) // 2
        n_dve = len(banks) // 2
        HALF = NP // 2
        src_f = s.sb("src_f", [P, ET])
        number = s.sb("number", [P, NP], F16)
        oh_src = s.sb("oh_src", [P, 2, NP], F16)
        oh_dst = s.sb("oh_dst", [P, 2, P], F16)
        count16 = s.sb("count16", [P, P], F16)
        zero16 = s.sb("zero16", [P, BANK], F16)
        acc = [s.ps(f"acc{i}") for i in range(len(banks))]
        numbered, linked, ready, hot, used = (s.sem(n) for n in ("numbered", "linked", "ready", "hot", "used"))
        summed, act_read, dve_read, diag = (s.sem(n) for n in ("summed", "act_read", "dve_read", "diag"))
        gather_on_pool = gather_small(s, g, io)
        with nc.Block() as block:
            @block.gpsimd
            def _(pool):
                pool.iota(number[:, :], pattern=[[1, NP]], base=-HALF, channel_multiplier=0,
                          allow_small_or_imprecise_dtypes=True).then_inc(numbered, 1)
                gather_on_pool(pool)

            def bounds(eng, b):
                return (eng.value_load(g.tiles[0:1, bass.ds(b, 1)], min_val=0, max_val=ET - 1),
                        eng.value_load(g.tiles[0:1, bass.ds(b + 1, 1)], min_val=0, max_val=ET - 1))

            @block.vector
            def _(dve):
                link = Linked(dve, linked)
                link(dve.memset(zero16[:, :], 0.0))
                link(dve.tensor_copy(count16[:, :], g.count[:, :]))
                link(dve.tensor_scalar(src_f[:, :], g.src_i[:, :], float(-HALF), None, ALU.add))
                dve.sem_inc(ready, 1)
                dve.sem_inc(dve_read, n_dve)
                dve.wait_ge(numbered, 1)
                with dve.Fori(0, NB) as b:
                    first, last = bounds(dve, b)
                    with dve.Fori(first, last + 1) as t:
                        dve.wait_ge(used, t + b)
                        dve.tensor_scalar(at(oh_dst, (t + b) % 2), count16[:, :], at(g.dst_f, t), at(g.minus_base, b),
                                          ALU.subtract, ALU.is_equal)
                        dve.tensor_scalar(at(oh_src, (t + b) % 2), number[:, :], at(src_f, t), None,
                                          ALU.is_equal).then_inc(hot, 1)
                    dve.wait_ge(summed, b + 1)
                    for n, (c, width) in enumerate(banks):
                        if n % 2:
                            dve.tensor_copy(g.counts[:, bass.ds(b, 1), c:c + width].rearrange("p a f -> p (a f)"),
                                            acc[n][:, 0:width]).then_inc(dve_read, 1)
                dve.wait_ge(act_read, (NB + 1) * n_act)
                dve.wait_ge(dve_read, (NB + 1) * n_dve)
                for b in range(NB):
                    own = g.counts[:, b, b * P:(b + 1) * P]
                    dve.tensor_tensor(own, own, g.ident[:, :], ALU.add).then_inc(diag, 1)

            @block.scalar
            def _(act):
                act.sem_inc(act_read, n_act)
                with act.Fori(0, NB) as b:
                    act.wait_ge(summed, b + 1)
                    for n, (c, width) in enumerate(banks):
                        if n % 2 == 0:
                            act.activation(g.counts[:, bass.ds(b, 1), c:c + width].rearrange("p a f -> p (a f)"),
                                           acc[n][:, 0:width], ACT.Copy).then_inc(act_read, 1)

            @block.tensor
            def _(pe):
                pe.sem_inc(used, 1)
                pe.wait_ge(ready, 1)
                with pe.Fori(0, NB) as b:
                    first, last = bounds(pe, b)
                    for n, (c, width) in enumerate(banks):
                        if n % 2:
                            pe.wait_ge(dve_read, b * n_dve + n // 2 + 1)
                        else:
                            pe.wait_ge(act_read, b * n_act + n // 2 + 1)
                        pe.matmul(acc[n][:, 0:width], zero16[:, 0:P], zero16[:, 0:width], start=True, stop=False,
                                  skip_group_check=True)
                    with pe.Fori(first, last + 1) as t:
                        pe.wait_ge(hot, t + b + 1)
                        for n, (c, width) in enumerate(banks):
                            mm = pe.matmul(acc[n][:, 0:width], at(oh_dst, (t + b) % 2),
                                           oh_src[:, bass.ds((t + b) % 2, 1), c:c + width].rearrange("p a f -> p (a f)"),
                                           start=False, stop=False, skip_group_check=True)
                        mm.then_inc(used, 1)
                    for n, (c, width) in enumerate(banks):
                        mm = pe.matmul(acc[n][:, 0:width], zero16[:, 0:P], zero16[:, 0:width], start=False, stop=True,
                                       skip_group_check=True)
                    mm.then_inc(summed, 1)


def edge_weights(nc, g, io, layer):
    H = HEADS[layer]
    first_head = sum(HEADS[:layer])
    chunks = [(c, min(P, ET - c)) for c in range(0, ET, P)]
    with ExitStack() as ctx:
        s = Space(nc, ctx, f"wts{layer}")
        u, v = s.sb("u", [P, H * ET]), s.sb("v", [P, H * ET])
        uh, vh = (x[:, :].rearrange("p (h j) -> p h j", h=H) for x in (u, v))
        dsts = s.sb("dsts", [P, 2 * ET], I32)
        before, here, tail = dsts[:, 0:ET], dsts[:, ET:], dsts[:, :].bitcast(F32)
        same, fresh = s.sb("same", [P, ET]), s.sb("fresh", [P, ET])
        rows = s.sb("rows", [P, 4, 2 * H])
        turned = s.sb("turned", [2 * H, 4, P])
        chain = s.sb("chain", [2 * H, 2, P + 1])
        carry = s.sb("carry", [P, 2, 2 * H])
        ends, fill = s.sb("ends", [P, NB, SW]), s.sb("fill", [P, NB, SW])
        self_v, top = s.sb("self_v", [P, NB, H]), s.sb("top", [P, NB, H])
        turn_ps, back_ps = s.ps("turn_ps"), s.ps("back_ps")
        cols_ps = [s.ps(f"cols_ps{i}") for i in range(2)]
        loaded, linked = s.sem("loaded"), s.sem("linked")
        summed_up, transposed, chained, returned = (s.sem(n) for n in ("summed_up", "transposed", "chained", "returned"))
        scanned, stored, gathered, node_done, scattered, spread = (
            s.sem(n) for n in ("scanned", "stored", "gathered", "node_done", "scattered", "spread"))
        weighed, exp_done, w_stored, turned_cols, copied_cols = (
            s.sem(n) for n in ("weighed", "exp_done", "w_stored", "turned_cols", "copied_cols"))
        w_loaded = [s.sem(f"w_loaded{i}") for i in range(len(chunks))]
        by_tile = [u[0:n, i * P * H:(i + 1) * P * H] if i < len(chunks) - 1 else tail[0:n, 0:P * H]
                   for i, (_, n) in enumerate(chunks)]
        pe_all = g.per_edge
        per_node = lambda x: x[:, :].unsqueeze(2).to_broadcast([P, NB, H])
        with nc.Block() as block:
            @block.sync
            def _(sp):
                sp.dma_start(before, io["dst_after"][0:EP].rearrange("(p j) -> p j", p=P)).then_inc(loaded, 16)
                sp.dma_start(here, io["dst_after"][1:EP + 1].rearrange("(p j) -> p j", p=P)).then_inc(loaded, 16)
                sp.dma_start(uh, g.edge_terms[:, first_head:first_head + H, :]).then_inc(loaded, 16)
                sp.wait_ge(scanned, 1)
                sp.dma_start(g.edge_scan.rearrange("(p j) c -> p j c", p=P), pe_all[:, :, :]).then_inc(stored, 16)
                sp.wait_ge(scattered, 16 * NB)
                sp.dma_start(pe_all[:, :, :], g.edge_fill.rearrange("(p j) c -> p j c", p=P)).then_inc(spread, 16)
                sp.wait_ge(exp_done, 2)
                w_dram = g.edge_w[0:EP * H]
                sp.dma_start(w_dram.rearrange("(p c) -> p c", p=P), v[:, :]).then_inc(w_stored, 16)
                sp.wait_ge(w_stored, 16)
                for i, (c, n) in enumerate(chunks):
                    sp.dma_start(by_tile[i], w_dram.rearrange("(t c) -> t c", t=ET)[c:c + n, :]).then_inc(w_loaded[i], 16)

            @block.gpsimd
            def _(pool):
                pool.wait_ge(stored, 16)
                for b in range(NB):
                    pool.indirect_dma_start(
                        out=ends[:, b, :], out_offset=None, in_=g.edge_scan,
                        in_offset=bass.IndirectOffsetOnAxis(ap=g.seg_end[:, b:b + 1], axis=0)).then_inc(gathered, 16)
                pool.wait_ge(node_done, 1)
                for b in range(NB):
                    pool.indirect_dma_start(
                        out=g.edge_fill, out_offset=bass.IndirectOffsetOnAxis(ap=g.seg_start[:, b:b + 1], axis=0),
                        in_=fill[:, b, :], in_offset=None, bounds_check=EP - 1, oob_is_err=False).then_inc(scattered, 16)

            @block.vector
            def _(dve):
                link = Linked(dve, linked)
                events = [0]

                def scan_sum(out, data, start):
                    link(dve.tensor_tensor_scan(out, same[:, :], data, start, ALU.mult, ALU.add))

                def scan_max(out, data, start):
                    link(dve.tensor_tensor_scan(out, fresh[:, :], data, start, ALU.add, ALU.max))

                def carries(n_sum, n_max):
                    n = max(n_sum, n_max)
                    events[0] += 1
                    dve.sem_inc(summed_up, 1)
                    dve.wait_ge(transposed, events[0])
                    link(dve.tensor_copy(turned[0:n, :, :].rearrange("h k p -> h (k p)"), turn_ps[0:n, :]))
                    link(dve.memset(chain[0:n, 0, 0:1], 0.0))
                    link(dve.memset(chain[0:n, 1, 0:1], -BIG))
                    link(dve.tensor_tensor_scan(chain[0:n, 0, 1:P + 1], turned[0:n, 2, :], turned[0:n, 0, :], 0.0,
                                                ALU.mult, ALU.add))
                    link(dve.tensor_tensor_scan(chain[0:n, 1, 1:P + 1], turned[0:n, 3, :], turned[0:n, 1, :], -BIG,
                                                ALU.add, ALU.max))
                    dve.sem_inc(chained, 1)
                    dve.wait_ge(returned, events[0])
                    link(dve.tensor_copy(carry[:, :, 0:n], back_ps[:, 0:2 * n].rearrange("p (k h) -> p k h", k=2)))

                dve.wait_ge(loaded, 48)
                link(dve.tensor_tensor(same[:, :], before, here, ALU.is_equal))
                link(dve.tensor_scalar(fresh[:, :], same[:, :], -1.0, BIG, ALU.add, ALU.mult))
                link(dve.memset(rows[:, :, :], 0.0))
                link(dve.tensor_reduce(rows[:, 2, 0:1], same[:, :], AX, ALU.min))
                link(dve.tensor_copy(rows[:, 2, 1:2 * H], rows[:, 2, 0:1].to_broadcast([P, 2 * H - 1])))
                link(dve.tensor_scalar(rows[:, 3, :], rows[:, 2, :], -1.0, BIG, ALU.add, ALU.mult))
                link(dve.tensor_tensor(uh, uh, pe_all[:, :, 4:5].rearrange("p j a -> p a j").to_broadcast([P, H, ET]),
                                       ALU.mult))
                link(dve.tensor_tensor(vh, uh, pe_all[:, :, 0:H].rearrange("p j h -> p h j"), ALU.add))
                for h in range(H):
                    scan_sum(pe_all[:, :, h], uh[:, h, :], 0.0)
                    scan_max(pe_all[:, :, H + h], vh[:, h, :], -BIG)
                link(dve.tensor_copy(rows[:, 0, 0:H], pe_all[:, ET - 1, 0:H]))
                link(dve.tensor_copy(rows[:, 1, 0:H], pe_all[:, ET - 1, H:2 * H]))
                carries(2 * H, 2 * H)
                for h in range(H):
                    scan_sum(pe_all[:, :, h], uh[:, h, :], carry[:, 0, h:h + 1])
                    scan_max(pe_all[:, :, H + h], vh[:, h, :], carry[:, 1, h:h + 1])
                dve.sem_inc(scanned, 1)

                dve.wait_ge(gathered, 16 * NB)
                link(dve.memset(fill[:, :, :], 0.0))
                total, peak = ends[:, :, 0:H], ends[:, :, H:2 * H]
                link(dve.tensor_tensor(self_v[:, :, :], total, per_node(g.inv_deg), ALU.mult))
                link(dve.tensor_tensor(self_v[:, :, :], self_v[:, :, :], per_node(g.has), ALU.mult))
                link(dve.tensor_tensor(self_v[:, :, :], self_v[:, :, :], g.small_sb[:, :, 0:H], ALU.add))
                link(dve.tensor_tensor(top[:, :, :], peak, per_node(g.has), ALU.mult))
                link(dve.tensor_scalar(ends[:, :, 0], g.has[:, :], -1.0, BIG, ALU.add, ALU.mult))
                link(dve.tensor_tensor(top[:, :, :], top[:, :, :], ends[:, :, 0:1].to_broadcast([P, NB, H]), ALU.add))
                link(dve.tensor_tensor(top[:, :, :], top[:, :, :], self_v[:, :, :], ALU.max))
                link(dve.tensor_tensor(top[:, :, :], top[:, :, :], g.node_d[:, :, 0:H], ALU.add))
                link(dve.scalar_tensor_tensor(fill[:, :, H:2 * H], top[:, :, :], SLOPE, top[:, :, :], ALU.mult, ALU.max))
                link(dve.tensor_copy(fill[:, :, 0:H], g.node_d[:, :, 0:H]))
                dve.sem_inc(node_done, 1)
                link(dve.tensor_tensor(self_v[:, :, :], self_v[:, :, :], g.node_d[:, :, 0:H], ALU.add))
                link(dve.scalar_tensor_tensor(self_v[:, :, :], self_v[:, :, :], SLOPE, self_v[:, :, :], ALU.mult, ALU.max))
                link(dve.tensor_tensor(self_v[:, :, :], self_v[:, :, :], fill[:, :, H:2 * H], ALU.subtract))
                dve.sem_inc(weighed, 1)

                dve.wait_ge(spread, 16)
                for c in range(2 * H):
                    scan_sum(uh[:, 0, :], pe_all[:, :, c], 0.0)
                    link(dve.tensor_copy(rows[:, 0, c:c + 1], uh[:, 0, ET - 1:ET]))
                carries(2 * H, 2 * H)
                for c in range(2 * H):
                    scan_sum(pe_all[:, :, c], pe_all[:, :, c], carry[:, 0, c:c + 1])
                link(dve.tensor_tensor(uh, vh, pe_all[:, :, 0:H].rearrange("p j h -> p h j"), ALU.add))
                link(dve.scalar_tensor_tensor(u[:, :], u[:, :], SLOPE, u[:, :], ALU.mult, ALU.max))
                link(dve.tensor_tensor(uh, uh, pe_all[:, :, H:2 * H].rearrange("p j h -> p h j"), ALU.subtract))
                dve.sem_inc(weighed, 1)
                for i, (c, n) in enumerate(chunks):
                    for h in range(H):
                        k = i * H + h
                        dve.wait_ge(turned_cols, k + 1)
                        dve.tensor_copy(g.w_cols[:, c:c + n, h], cols_ps[k % 2][:, 0:n]).then_inc(copied_cols, 1)

            @block.scalar
            def _(act):
                act.wait_ge(weighed, 1)
                act.activation(g.w_self[:, :, 0:H], self_v[:, :, :], ACT.Exp).then_inc(exp_done, 1)
                act.wait_ge(weighed, 2)
                act.activation(v[:, :].rearrange("p (j h) -> p h j", h=H), uh, ACT.Exp).then_inc(exp_done, 1)

            @block.tensor
            def _(pe):
                for n in range(2):
                    pe.wait_ge(summed_up, n + 1)
                    for k in range(4):
                        mm = pe.transpose(turn_ps[0:2 * H, k * P:(k + 1) * P], rows[:, k, :], g.ident[:, :])
                    mm.then_inc(transposed, 1)
                    pe.wait_ge(chained, n + 1)
                    for k in range(2):
                        mm = pe.transpose(back_ps[:, k * 2 * H:(k + 1) * 2 * H], chain[:, k, 0:P],
                                          g.ident[0:2 * H, 0:2 * H])
                    mm.then_inc(returned, 1)
                for i, (c, n) in enumerate(chunks):
                    pe.wait_ge(w_loaded[i], 16)
                    for h in range(H):
                        k = i * H + h
                        if k >= 2:
                            pe.wait_ge(copied_cols, k - 1)
                        pe.transpose(cols_ps[k % 2][:, 0:n], by_tile[i][:, h:P * H:H],
                                     g.ident[0:n, 0:n]).then_inc(turned_cols, 1)


def aggregate(nc, g, io, layer, out_dram):
    H = HEADS[layer]
    F = D // H
    R = H * (F + 1)
    half = RING // 2
    with ExitStack() as ctx:
        s = Space(nc, ctx, f"agg{layer}")
        ring = s.sb("ring", [P, RING, ROW])
        now = [s.sb(f"now{i}", [P, half], I32) for i in range(2)]
        oh = s.sb("oh", [P, P])
        msg = s.sb("msg", [P, 2, R])
        own, res = s.sb("own", [P, ROW]), s.sb("res", [P, 3, D])
        y, inv = s.sb("y", [P, R]), s.sb("inv", [P, H])
        bias = s.sb("bias", [P, D])
        zero = s.sb("zero", [P, P])
        acc = s.ps("acc")
        yh = y[:, :].rearrange("p (h f) -> p h f", h=H)
        came = [s.sem(f"came{k}") for k in range(RING)]
        (listed, picked, gate, in_order, freed, hot, used, scaled, summed, read, loaded, finished, stored, consts, linked,
         left) = (s.sem(n) for n in (
             "listed", "picked", "gate", "in_order", "freed", "hot", "used", "scaled", "summed", "read", "loaded",
             "finished", "stored", "consts", "linked", "left"))
        residuals = [g.x_norm] if layer == 0 else [g.x_mid, g.x_norm, io["x"]]
        n_loads = 1 + len(residuals)

        def bounds(eng, b):
            return (eng.value_load(g.tiles[0:1, bass.ds(b, 1)], min_val=0, max_val=ET - 1),
                    eng.value_load(g.tiles[0:1, bass.ds(b + 1, 1)], min_val=0, max_val=ET - 1))

        with nc.Block() as block:
            @block.gpsimd
            def _(pool):
                with pool.Fori(0, ET // RING) as j:
                    for i in range(2):
                        pool.wait_ge(freed, j * RING + i * half + half)
                        pool.tensor_copy(now[i][:, :], g.src_i[:, bass.ds(j * RING + i * half, half)]).then_inc(picked, 1)
                        pool.wait_ge(picked, 2 * j + i + 1)
                        pool.sem_inc(gate, 1)
                        for k in range(half):
                            pool.indirect_dma_start(
                                out=ring[:, i * half + k, :], out_offset=None, in_=g.hx_rows,
                                in_offset=bass.IndirectOffsetOnAxis(ap=now[i][:, k:k + 1], axis=0)
                            ).then_inc(came[i * half + k], 16)

            @block.scalar
            def _(act):
                with act.Fori(0, ET // RING) as j:
                    for k in range(RING):
                        act.wait_ge(came[k], 16 * (j + 1))
                        act.sem_inc(in_order, 1)

            @block.sync
            def _(sp):
                sp.sem_inc(freed, RING)
                sp.dma_start(bias[:, :], across(io[f"L0_gnn_bg{layer}"], D)).then_inc(consts, 16)
                with sp.Fori(0, NB) as b:
                    first, last = bounds(sp, b)
                    sp.wait_ge(finished, b)
                    sp.dma_start(own[:, :], g.hx_rows[bass.ds(b * P, P), :]).then_inc(loaded, 16)
                    for n, src in enumerate(residuals):
                        sp.dma_start(res[:, n, :], src[bass.ds(b * P, P), :]).then_inc(loaded, 16)
                    with sp.If(last > first):
                        with sp.Fori(first, last) as t:
                            sp.wait_ge(scaled, t + b + 1)
                            sp.sem_inc(freed, 1)
                    sp.wait_ge(finished, b + 1)
                    sp.dma_start(out_dram[bass.ds(b * P, P), :], y[:, 0:D]).then_inc(stored, 16)
                    sp.wait_ge(stored, 16 * (b + 1))
                    sp.sem_inc(left, 1)

            @block.vector
            def _(dve):
                dve.memset(zero[:, :], 0.0).then_inc(linked, 1)
                dve.wait_ge(consts, 16)
                with dve.Fori(0, NB) as b:
                    first, last = bounds(dve, b)
                    with dve.Fori(first, last + 1) as t:
                        dve.wait_ge(in_order, t + 1)
                        dve.wait_ge(used, t + b)
                        row = ring[:, bass.ds(t % RING, 1), 0:R].rearrange("p a (h f) -> p (a h) f", h=H)
                        dve.tensor_tensor(msg[:, bass.ds((t + b) % 2, 1), :].rearrange("p a (h f) -> p (a h) f", h=H), row,
                                          g.w_cols[:, bass.ds(t, 1), 0:H].rearrange("p a h -> p (a h)").unsqueeze(2)
                                          .to_broadcast([P, H, F + 1]), ALU.mult).then_inc(scaled, 1)
                        dve.wait_ge(used, t + b + 1)
                        dve.tensor_scalar(oh[:, :], g.count[:, :], at(g.dst_f, t), at(g.minus_base, b), ALU.subtract,
                                          ALU.is_equal).then_inc(hot, 1)
                    link = Linked(dve, linked, 1 + (H + (5 if layer == 0 else 6)) * b)
                    dve.wait_ge(summed, b + 1)
                    dve.wait_ge(loaded, 16 * n_loads * (b + 1))
                    dve.wait_ge(left, b)
                    for h in range(H):
                        ins = dve.scalar_tensor_tensor(
                            yh[:, h, :], own[:, h * (F + 1):(h + 1) * (F + 1)],
                            g.w_self[:, bass.ds(b, 1), h:h + 1].rearrange("p a f -> p (a f)"),
                            acc[:, h * (F + 1):(h + 1) * (F + 1)], ALU.mult, ALU.add)
                        link(ins)
                    dve.sem_inc(read, 1)
                    link(dve.reciprocal(inv[:, :], yh[:, :, F]))
                    link(dve.tensor_tensor(own[:, 0:D].rearrange("p (h f) -> p h f", h=H), yh[:, :, 0:F],
                                           inv[:, :].unsqueeze(2).to_broadcast([P, H, F]), ALU.mult))
                    link(dve.tensor_tensor(own[:, 0:D], own[:, 0:D], bias[:, :], ALU.add))
                    for n in range(len(residuals) - 1):
                        link(dve.tensor_tensor(own[:, 0:D], own[:, 0:D], res[:, n, :], ALU.add))
                    if layer == 0:
                        link(dve.tensor_tensor(own[:, 0:D], own[:, 0:D], res[:, 0, :], ALU.add))
                        link(dve.tensor_scalar(y[:, 0:D], own[:, 0:D], 0.0, None, ALU.max))
                    else:
                        link(dve.tensor_tensor(y[:, 0:D], own[:, 0:D], res[:, len(residuals) - 1, :], ALU.add))
                    dve.sem_inc(finished, 1)

            @block.tensor
            def _(pe):
                pe.sem_inc(used, 1)
                pe.wait_ge(linked, 1)
                with pe.Fori(0, NB) as b:
                    first, last = bounds(pe, b)
                    pe.wait_ge(read, b)
                    pe.matmul(acc[:, 0:P], zero[:, :], zero[:, :], start=True, stop=False, skip_group_check=True)
                    with pe.Fori(first, last + 1) as t:
                        pe.wait_ge(hot, t + b + 1)
                        pe.matmul(acc[:, 0:R], oh[:, :], at(msg, (t + b) % 2), start=False, stop=False,
                                  skip_group_check=True).then_inc(used, 1)
                    pe.matmul(acc[:, 0:P], zero[:, :], zero[:, :], start=False, stop=True,
                              skip_group_check=True).then_inc(summed, 1)


def gather_alone(nc, g, io):
    with ExitStack() as ctx:
        on_pool = gather_small(Space(nc, ctx, "gth"), g, io)
        with nc.Block() as block:
            @block.gpsimd
            def _(pool):
                on_pool(pool)


def route(nc, g, io):
    with ExitStack() as ctx:
        s = Space(nc, ctx, "rte")
        x = s.sb("x", [P, NB, D])
        gw, gb = s.sb("gw", [P, 2, NE]), s.sb("gb", [P, NE])
        xs = [s.sb(f"xs{i}", [P, D]) for i in range(2)]
        xt = [s.sb(f"xt{i}", [P, 2, P]) for i in range(2)]
        cube = lambda n: s.sb(n, [P, NB, NE])
        logits, hot, number, work, before = (cube(n) for n in ("logits", "hot", "number", "work", "before"))
        top, choice, place, kept_f = (s.sb(n, [P, NB]) for n in ("top", "choice", "place", "kept_f"))
        zero = s.sb("zero", [P, NB])
        norm = Norm(s)
        turned = [s.ps(f"turned{i}") for i in range(2)]
        lg = [s.ps(f"lg{i}") for i in range(2)]
        sums = s.ps("sums")
        loaded, linked, link2, numbered, shifted, expd, hotted, cumulated, placed, sent = (
            s.sem(n) for n in ("loaded", "linked", "link2", "numbered", "shifted", "expd", "hotted", "cumulated",
                               "placed", "sent"))
        fed, t_done, t_copied, m_done, m_read, kept = ([s.sem(f"{n}{i}") for i in range(2)] for n in (
            "fed", "t_done", "t_copied", "m_done", "m_read", "kept"))
        flat = lambda c: c[:, :, :].rearrange("p b e -> p (b e)")
        with nc.Block() as block:
            @block.sync
            def _(sp):
                sp.dma_start(x[:, :, :], g.x_gnn.rearrange("(b p) d -> p b d", p=P)).then_inc(loaded, 16)
                sp.dma_start(gw[:, :, :], io["L0_ffn_gate_w"].rearrange("(p k) e -> p k e", p=P)).then_inc(loaded, 16)
                sp.dma_start(gb[:, :], across(io["L0_ffn_gate_b"], NE)).then_inc(loaded, 16)

            @block.gpsimd
            def _(pool):
                pool.iota(number[:, :, :], pattern=[[0, NB], [1, NE]], base=0, channel_multiplier=0,
                          allow_small_or_imprecise_dtypes=True).then_inc(numbered, 1)
                pool.wait_ge(placed, 1)
                for b in range(NB):
                    pool.indirect_dma_start(
                        out=g.expert_in, out_offset=bass.IndirectOffsetOnAxis(ap=g.slot_in[:, b:b + 1], axis=0),
                        in_=x[:, b, :], in_offset=None, bounds_check=NE * SLOTS - 1, oob_is_err=False).then_inc(sent, 16)
                pool.wait_ge(sent, 16 * NB)

            @block.vector
            def _(dve):
                dve.wait_ge(loaded, 48)
                norm.on_vector(dve, linked, x)
                link = Linked(dve, link2)

                def body(blocks):
                    for b, i, j in blocks:
                        dve.wait_ge(t_done[i], j)
                        dve.wait_ge(kept[i], j)
                        norm.block(dve, xs[i][:, :], x, b).then_inc(fed[i], 1)
                    for b, i, j in blocks:
                        dve.wait_ge(m_done[i], j + 1)
                        dve.tensor_tensor(at(logits, b), lg[i][:, 0:NE], gb[:, :], ALU.add).then_inc(m_read[i], 1)
                pairs(dve, body)
                wide = lambda t: t[:, :].unsqueeze(2).to_broadcast([P, NB, NE])
                dve.wait_ge(m_read[0], -(-NB // 2))
                dve.wait_ge(m_read[1], NB // 2)
                dve.wait_ge(numbered, 1)
                link(dve.tensor_reduce(top[:, :], logits[:, :, :], AX, ALU.max))
                link(dve.tensor_tensor(work[:, :, :], logits[:, :, :], wide(top), ALU.subtract))
                dve.sem_inc(shifted, 1)
                link(dve.tensor_tensor(hot[:, :, :], logits[:, :, :], wide(top), ALU.is_lt))
                link(dve.scalar_tensor_tensor(hot[:, :, :], hot[:, :, :], float(NE), number[:, :, :], ALU.mult, ALU.add))
                link(dve.tensor_reduce(choice[:, :], hot[:, :, :], AX, ALU.min))
                link(dve.tensor_tensor(hot[:, :, :], number[:, :, :], wide(choice), ALU.is_equal))
                dve.sem_inc(hotted, 1)
                dve.wait_ge(expd, 1)
                link(dve.tensor_reduce(top[:, :], work[:, :, :], AX, ALU.add))
                link(dve.reciprocal(top[:, :], top[:, :]))
                dve.wait_ge(cumulated, 1)
                W = NB * NE
                link(dve.tensor_copy(flat(work), sums[:, 256:256 + W]))
                link(dve.memset(zero[:, :], 0.0))
                for e in range(NE):
                    link(dve.tensor_tensor_scan(before[:, :, e], work[:, :, e], zero[:, :], 0.0, ALU.add, ALU.add))
                link(dve.tensor_tensor(before[:, :, :], before[:, :, :], work[:, :, :], ALU.subtract))
                link(dve.tensor_tensor(flat(before), flat(before), sums[:, 0:W], ALU.add))
                link(dve.tensor_tensor(before[:, :, :], before[:, :, :], hot[:, :, :], ALU.mult))
                link(dve.tensor_reduce(place[:, :], before[:, :, :], AX, ALU.add))
                link(dve.tensor_scalar(place[:, :], place[:, :], -1.0, None, ALU.add))
                link(dve.tensor_scalar(kept_f[:, :], place[:, :], float(CAP), None, ALU.is_lt))
                link(dve.tensor_tensor(g.share[:, :], top[:, :], kept_f[:, :], ALU.mult))
                link(dve.tensor_scalar(place[:, :], place[:, :], float(CAP - 1), None, ALU.min))
                link(dve.scalar_tensor_tensor(place[:, :], choice[:, :], float(SLOTS), place[:, :], ALU.mult, ALU.add))
                link(dve.tensor_copy(g.slot_out[:, :], place[:, :]))
                link(dve.tensor_scalar(kept_f[:, :], kept_f[:, :], -1.0, float(-NE * SLOTS), ALU.add, ALU.mult))
                link(dve.tensor_tensor(place[:, :], place[:, :], kept_f[:, :], ALU.add))
                link(dve.tensor_copy(g.slot_in[:, :], place[:, :]))
                dve.wait_ge(kept[0], -(-NB // 2))
                dve.wait_ge(kept[1], NB // 2)
                dve.sem_inc(placed, 1)

            @block.scalar
            def _(act):
                norm.on_scalar(act)

                def body(blocks):
                    for b, i, j in blocks:
                        act.wait_ge(t_done[i], j + 1)
                        act.wait_ge(m_done[i], j)
                        act.activation(xt[i][:, :, :].rearrange("p k n -> p (k n)"), turned[i][:, 0:2 * P],
                                       ACT.Copy).then_inc(t_copied[i], 1)
                    for b, i, j in blocks:
                        act.activation(at(x, b), xs[i][:, :], ACT.Copy).then_inc(kept[i], 1)
                pairs(act, body)
                act.wait_ge(shifted, 1)
                act.activation(flat(work), flat(work), ACT.Exp).then_inc(expd, 1)

            @block.tensor
            def _(pe):
                pe.wait_ge(loaded, 48)

                def body(blocks):
                    for b, i, j in blocks:
                        pe.wait_ge(fed[i], j + 1)
                        pe.wait_ge(t_copied[i], j)
                        for k in range(2):
                            mm = pe.transpose(turned[i][:, k * P:(k + 1) * P], xs[i][:, k:D:2], g.ident[:, :])
                        mm.then_inc(t_done[i], 1)
                    for b, i, j in blocks:
                        pe.wait_ge(t_copied[i], j + 1)
                        pe.wait_ge(m_read[i], j)
                        for k in range(2):
                            mm = pe.matmul(lg[i][:, 0:NE], xt[i][:, k, :], gw[:, k, :], start=(k == 0), stop=(k == 1))
                        mm.then_inc(m_done[i], 1)
                pairs(pe, body)
                pe.wait_ge(hotted, 1)
                W = NB * NE
                pe.matmul(sums[:, 0:W], g.tri_upto[:, :], flat(hot), start=True, stop=True)
                pe.matmul(sums[:, 256:256 + W], g.ones[:, :], flat(hot), start=True, stop=True).then_inc(cumulated, 1)


def experts(nc, g, io):
    KF = FF // P
    Q = SLOTS // P
    with ExitStack() as ctx:
        s = Space(nc, ctx, "exp")
        w1 = [s.sb(f"w1_{i}", [P, 2, FF]) for i in range(2)]
        w2 = s.sb("w2", [P, KF, D])
        b1, b2 = s.sb("b1", [P, NE, KF]), s.sb("b2", [P, D])
        rows = s.sb("rows", [P, Q, D])
        xt = s.sb("xt", [P, 2, SLOTS])
        hid = [s.sb(f"hid{i}", [P, SLOTS]) for i in range(2)]
        y = s.sb("y", [P, Q, D])
        up = [s.ps(f"up{i}") for i in range(2)]
        turned = [s.ps(f"turned{i}") for i in range(2)]
        down = [s.ps(f"down{q}") for q in range(Q)]
        w1_in = [s.sem(f"w1_in{i}") for i in range(2)]
        w2_in, rows_in, b_in, t_done, t_copied, u_done, act_done, d_chunk, d_read, y_out = (
            s.sem(n) for n in ("w2_in", "rows_in", "b_in", "t_done", "t_copied", "u_done", "act_done", "d_chunk",
                               "d_read", "y_out"))
        w1_d = io["L0_ffn_w1"].rearrange("e (p k) f -> e p k f", p=P)
        w2_d = io["L0_ffn_w2"].rearrange("e (p c) d -> e p c d", p=P)
        in_d = g.expert_in.rearrange("(e q p) d -> e p q d", e=NE, p=P)
        out_d = g.expert_out.rearrange("(e q p) d -> e p q d", e=NE, p=P)
        b2_d = io["L0_ffn_b2"]
        one = lambda ap, e: ap[bass.ds(e, 1)].rearrange("a p k f -> (a p) k f")

        def by_parity(eng, body):
            with eng.Fori(0, NE // 2) as j:
                body(2 * j, 0, j)
                body(2 * j + 1, 1, j)

        with nc.Block() as block:
            @block.sync
            def _(sp):
                sp.dma_start(b1[:, :, :], io["L0_ffn_b1"].rearrange("e (p c) -> p e c", p=P)).then_inc(b_in, 16)
                sp.wait_ge(b_in, 16)

                def body(e, i, j):
                    sp.wait_ge(t_done, 2 * Q * e)
                    sp.dma_start(rows[:, :, :], one(in_d, e)).then_inc(rows_in, 16)
                    sp.wait_ge(u_done, KF * e)
                    sp.dma_start(w1[i][:, :, :], one(w1_d, e)).then_inc(w1_in[i], 16)
                    sp.wait_ge(d_chunk, KF * e)
                    sp.dma_start(w2[:, :, :], one(w2_d, e)).then_inc(w2_in, 16)
                    sp.wait_ge(d_read, Q * e)
                    sp.dma_start(b2[:, :], b2_d[bass.ds(e, 1), :].to_broadcast([P, D])).then_inc(b_in, 16)
                by_parity(sp, body)

            @block.gpsimd
            def _(pool):
                with pool.Fori(0, NE) as e:
                    pool.wait_ge(d_read, Q * (e + 1))
                    pool.dma_start(one(out_d, e), y[:, :, :]).then_inc(y_out, 16)
                pool.wait_ge(y_out, 16 * NE)

            @block.vector
            def _(dve):
                with dve.Fori(0, NE) as e:
                    dve.wait_ge(b_in, 16 * (e + 2))
                    dve.wait_ge(y_out, 16 * e)
                    for q in range(Q):
                        dve.wait_ge(d_chunk, KF * (e + 1))
                        dve.tensor_tensor(y[:, q, :], down[q][:, 0:D], b2[:, :], ALU.add).then_inc(d_read, 1)

            @block.scalar
            def _(act):
                act.wait_ge(b_in, 16)
                with act.Fori(0, NE) as e:
                    act.wait_ge(u_done, KF * e + KF)
                    for n in range(2 * Q // 4):
                        act.wait_ge(t_done, 2 * Q * e + 4 * (n + 1))
                        act.activation(xt[:, n, :], turned[n][:, :], ACT.Copy).then_inc(t_copied, 1)
                    for c in range(KF):
                        act.wait_ge(u_done, KF * e + KF + c + 1)
                        if c >= 2:
                            act.wait_ge(d_chunk, KF * e + c - 1)
                        else:
                            act.wait_ge(d_chunk, KF * e)
                        act.activation(hid[c % 2][:, :], up[c % 2][:, :], ACT.Relu,
                                       bias=b1[:, bass.ds(e, 1), c:c + 1].rearrange("p a f -> p (a f)")).then_inc(act_done, 1)

            @block.tensor
            def _(pe):
                pe.sem_inc(u_done, KF)

                def body(e, i, j):
                    pe.wait_ge(rows_in, 16 * (e + 1))
                    pe.wait_ge(t_copied, 2 * e)
                    for k in range(2):
                        for q in range(Q):
                            pe.transpose(turned[k][:, q * P:(q + 1) * P], rows[:, q, k:D:2], g.ident[:, :]).then_inc(t_done, 1)

                    def first(c):
                        pe.wait_ge(act_done, KF * e + c - 1 if c >= 2 else KF * e)
                        for k in range(2):
                            mm = pe.matmul(up[c % 2][:, :], w1[i][:, k, c:FF:KF], xt[:, k, :], start=(k == 0), stop=(k == 1))
                        mm.then_inc(u_done, 1)

                    pe.wait_ge(t_copied, 2 * (e + 1))
                    pe.wait_ge(w1_in[i], 16 * (j + 1))
                    first(0)
                    for c in range(KF):
                        if c + 1 < KF:
                            first(c + 1)
                        if c == 0:
                            pe.wait_ge(w2_in, 16 * (e + 1))
                            pe.wait_ge(d_read, Q * e)
                        pe.wait_ge(act_done, KF * e + c + 1)
                        for q in range(Q):
                            mm = pe.matmul(down[q][:, 0:D], hid[c % 2][:, q * P:(q + 1) * P], w2[:, c, :],
                                           start=(c == 0), stop=(c == KF - 1), skip_group_check=True)
                        mm.then_inc(d_chunk, 1)
                by_parity(pe, body)


def combine(nc, g, io):
    PART = 5
    parts = NB // PART
    MAX32 = 3.4028234663852886e38
    with ExitStack() as ctx:
        s = Space(nc, ctx, "cmb")
        y, x, z = ([s.sb(f"{n}{i}", [P, PART, D]) for i in range(2)] for n in ("y", "x", "z"))
        mask = s.sb("mask", [P, PART, D])
        edge = s.sb("edge", [P, 2, D])
        loaded, stored, linked, done = (s.sem(n) for n in ("loaded", "stored", "linked", "done"))
        came_by = [s.sem(f"came{c}") for c in range(parts)]
        view = lambda d, c: d.rearrange("(b p) d -> p b d", p=P)[:, c * PART:(c + 1) * PART, :]
        with nc.Block() as block:
            @block.sync
            def _(sp):
                for c in range(parts):
                    if c >= 2:
                        sp.wait_ge(stored, 16 * (c - 1))
                    if c >= 1:
                        sp.wait_ge(loaded, 16 * c)
                    sp.dma_start(x[c % 2][:, :, :], view(g.x_gnn, c)).then_inc(loaded, 16)
                    if c >= 1:
                        sp.wait_ge(done, c)
                        sp.dma_start(view(g.x_moe, c - 1), x[(c - 1) % 2][:, :, :]).then_inc(stored, 16)
                sp.wait_ge(done, parts)
                sp.dma_start(view(g.x_moe, parts - 1), x[(parts - 1) % 2][:, :, :]).then_inc(stored, 16)
                sp.wait_ge(stored, 16 * parts)

            @block.gpsimd
            def _(pool):
                for c in range(parts):
                    if c >= 2:
                        pool.wait_ge(done, c - 1)
                    for b in range(PART):
                        col = c * PART + b
                        pool.indirect_dma_start(
                            out=y[c % 2][:, b, :], out_offset=None, in_=g.expert_out,
                            in_offset=bass.IndirectOffsetOnAxis(ap=g.slot_out[:, col:col + 1], axis=0)
                        ).then_inc(came_by[c], 16)

            @block.vector
            def _(dve):
                link = Linked(dve, linked)
                link(dve.memset(edge[:, 0, :], 1.0e4))
                link(dve.memset(edge[:, 1, :], -1.0e4))
                flat = lambda t: t[:, :, :].rearrange("p b d -> p (b d)")
                for c in range(parts):
                    yc, xc, zc = y[c % 2], x[c % 2], z[c % 2]
                    dve.wait_ge(came_by[c], 16 * PART)
                    link(dve.tensor_tensor(yc[:, :, :], yc[:, :, :],
                                           g.share[:, c * PART:(c + 1) * PART].unsqueeze(2).to_broadcast([P, PART, D]),
                                           ALU.mult))
                    link(dve.memset(zc[:, :, :], 0.0))
                    link(dve.tensor_tensor(mask[:, :, :], yc[:, :, :], yc[:, :, :], ALU.is_equal))
                    link(dve.copy_predicated(flat(zc), flat(mask).bitcast(I32), flat(yc)))
                    for n, (limit, op) in enumerate(((MAX32, ALU.is_gt), (-MAX32, ALU.is_lt))):
                        link(dve.tensor_scalar(mask[:, :, :], yc[:, :, :], limit, None, op))
                        for b in range(PART):
                            link(dve.copy_predicated(zc[:, b, :], mask[:, b, :].bitcast(I32), edge[:, n, :]))
                    dve.wait_ge(loaded, 16 * (c + 1))
                    link(dve.tensor_tensor(xc[:, :, :], xc[:, :, :], zc[:, :, :], ALU.add))
                    dve.sem_inc(done, 1)


class Gate:

    def __init__(self, s):
        self.w, self.bias, self.junk = s.sb("w", [P, D]), s.sb("bias", [P, 1]), s.sb("junk", [P, D])
        self.h, self.rest = s.sb("h", [P, D]), s.sb("rest", [P, D])
        self.parts = [s.sb(f"parts{i}", [P, 3, D], BF16) for i in range(2)]
        self.dot, self.gate = s.sb("dot", [P, 2]), s.sb("gate", [P, 2])
        self.given, self.linked = s.sem("given"), s.sem("linked")
        self.dotted, self.gated, self.split, self.added = (
            [s.sem(f"{n}{i}") for i in range(2)] for n in ("dotted", "gated", "split", "added"))

    def load(self, sp, io):
        sp.dma_start(self.w[:, :], across(io["L1_gnn_lin_w"].rearrange("a n -> (a n)"), D)).then_inc(self.given, 16)
        sp.dma_start(self.bias[:, :], across(io["L1_gnn_lin_b"], 1)).then_inc(self.given, 16)

    LINKS = 7

    def on_vector(self, dve, link, i, turn, dis, acc_out, acc_in):
        link(dve.tensor_tensor_reduce(self.junk[:, :], self.h[:, :], self.w[:, :], 1.0, 0.0, ALU.mult, ALU.add,
                                      self.dot[:, i:i + 1]))
        dve.sem_inc(self.dotted[i], 1)
        hi, mid, low = (self.parts[i][:, n, :] for n in range(3))
        link(dve.tensor_scalar(self.rest[:, :], self.h[:, :], dis, None, ALU.mult))
        link(dve.tensor_copy(hi, self.rest[:, :]))
        link(dve.tensor_tensor(self.rest[:, :], self.rest[:, :], hi, ALU.subtract))
        link(dve.tensor_copy(mid, self.rest[:, :]))
        link(dve.tensor_tensor(self.rest[:, :], self.rest[:, :], mid, ALU.subtract))
        dve.tensor_copy(low, self.rest[:, :]).then_inc(self.split[i], 1)
        dve.wait_ge(self.gated[i], turn + 1)
        link(dve.scalar_tensor_tensor(acc_out, self.h[:, :], self.gate[:, i:i + 1], acc_in, ALU.mult, ALU.add))
        dve.sem_inc(self.added[i], 1)

    def on_scalar(self, act, i, turn):
        act.wait_ge(self.dotted[i], turn + 1)
        act.activation(self.gate[:, i:i + 1], self.dot[:, i:i + 1], ACT.Sigmoid,
                       bias=self.bias[:, 0:1]).then_inc(self.gated[i], 1)


TURNS = (-(-NB // 2), NB // 2)


def hop_parts(g, parity, b):
    return g.hop_parts[bass.ds(parity * NP + b * P, P), :]


def hops_start(nc, g, io):
    with ExitStack() as ctx:
        s = Space(nc, ctx, "hp0")
        x = s.sb("x", [P, NB, D])
        acc = [s.sb(f"acc{i}", [P, D]) for i in range(2)]
        norm, gate = Norm(s), Gate(s)
        loaded, bn = s.sem("loaded"), s.sem("bn")
        kept, saved = ([s.sem(f"{n}{i}") for i in range(2)] for n in ("kept", "saved"))
        with nc.Block() as block:
            @block.sync
            def _(sp):
                sp.dma_start(x[:, :, :], g.x_moe.rearrange("(b p) d -> p b d", p=P)).then_inc(loaded, 16)
                gate.load(sp, io)

                def body(blocks):
                    for b, i, j in blocks:
                        sp.wait_ge(gate.split[i], j + 1)
                        sp.dma_start(hop_parts(g, 0, b), gate.parts[i][:, :, :].rearrange("p n d -> p (n d)")
                                     ).then_inc(kept[i], 16)
                        sp.wait_ge(gate.added[i], j + 1)
                        sp.dma_start(g.x_gcn[bass.ds(b * P, P), :], acc[i][:, :]).then_inc(saved[i], 16)
                pairs(sp, body)
                for i in range(2):
                    sp.wait_ge(kept[i], 16 * TURNS[i])
                    sp.wait_ge(saved[i], 16 * TURNS[i])

            @block.vector
            def _(dve):
                dve.wait_ge(loaded, 16)
                norm.on_vector(dve, bn, x)
                dve.wait_ge(gate.given, 32)

                def body(blocks):
                    for b, i, j in blocks:
                        link = Linked(dve, gate.linked, (Gate.LINKS + 1) * b)
                        dve.wait_ge(kept[i], 16 * j)
                        dve.wait_ge(saved[i], 16 * j)
                        link(norm.block(dve, gate.h[:, :], x, b))
                        gate.on_vector(dve, link, i, j, at(g.dis, b), acc[i][:, :], at(x, b))
                pairs(dve, body)

            @block.scalar
            def _(act):
                norm.on_scalar(act)
                act.wait_ge(gate.given, 32)
                pairs(act, lambda blocks: [gate.on_scalar(act, i, j) for b, i, j in blocks])


def hops(nc, g, io):
    CHUNK = 5
    with ExitStack() as ctx:
        s = Space(nc, ctx, "hop")
        hs = s.sb("hs", [P, NB, 3 * D], BF16)
        acc = [s.sb(f"acc{i}", [P, D]) for i in range(2)]
        gate = Gate(s)
        wide, narrow = ([s.ps(f"{n}{i}") for i in range(2)] for n in ("wide", "narrow"))
        here, passed = [s.sem(f"here{c}") for c in range(NB // CHUNK)], s.sem("passed")
        kept, saved, came, summed, read = ([s.sem(f"{n}{i}") for i in range(2)] for n in (
            "kept", "saved", "came", "summed", "read"))
        with nc.Block() as block:
            @block.sync
            def _(sp):
                gate.load(sp, io)
                with sp.Fori(0, HOPS) as k:
                    for i in range(2):
                        for done, count in ((kept[i], 16 * TURNS[i] * k), (saved[i], 16 * TURNS[i] * k),
                                            (summed[i], TURNS[i] * k)):
                            sp.wait_ge(done, count)
                            sp.sem_inc(passed, 1)
                    for c in range(NB // CHUNK):
                        sp.dma_start(hs[:, c * CHUNK:(c + 1) * CHUNK, :],
                                     g.hop_parts[bass.ds((k % 2) * NP + c * CHUNK * P, CHUNK * P), :].rearrange(
                                         "(b p) d -> p b d", p=P)).then_inc(here[c], 16)

                    def body(blocks):
                        for b, i, j in blocks:
                            turn = k * TURNS[i] + j
                            sp.wait_ge(saved[i], 16 * turn)
                            sp.dma_start(acc[i][:, :], g.x_gcn[bass.ds(b * P, P), :]).then_inc(came[i], 16)
                        for b, i, j in blocks:
                            turn = k * TURNS[i] + j
                            sp.wait_ge(gate.split[i], turn + 1)
                            sp.dma_start(hop_parts(g, (k + 1) % 2, b),
                                         gate.parts[i][:, :, :].rearrange("p n d -> p (n d)")).then_inc(kept[i], 16)
                            sp.wait_ge(gate.added[i], turn + 1)
                            sp.dma_start(g.x_gcn[bass.ds(b * P, P), :], acc[i][:, :]).then_inc(saved[i], 16)
                    pairs(sp, body)
                for i in range(2):
                    sp.wait_ge(kept[i], 16 * TURNS[i] * HOPS)
                    sp.wait_ge(saved[i], 16 * TURNS[i] * HOPS)

            @block.vector
            def _(dve):
                dve.wait_ge(gate.given, 32)
                with dve.Fori(0, HOPS) as k:
                    def body(blocks):
                        for b, i, j in blocks:
                            turn = k * TURNS[i] + j
                            link = Linked(dve, gate.linked, (Gate.LINKS + 3) * (k * NB + b))
                            dis = at(g.dis, b)
                            dve.wait_ge(summed[i], turn + 1)
                            link(dve.tensor_scalar(gate.h[:, :], narrow[i][:, 0:D], dis, None, ALU.mult))
                            for n in (1, 0):
                                link(dve.scalar_tensor_tensor(gate.h[:, :], wide[i][:, n * D:(n + 1) * D], dis,
                                                              gate.h[:, :], ALU.mult, ALU.add))
                            dve.sem_inc(read[i], 1)
                            dve.wait_ge(kept[i], 16 * turn)
                            dve.wait_ge(came[i], 16 * (turn + 1))
                            gate.on_vector(dve, link, i, turn, dis, acc[i][:, :], acc[i][:, :])
                    pairs(dve, body)

            @block.scalar
            def _(act):
                act.wait_ge(gate.given, 32)
                with act.Fori(0, HOPS) as k:
                    pairs(act, lambda blocks: [gate.on_scalar(act, i, k * TURNS[i] + j) for b, i, j in blocks])

            @block.tensor
            def _(pe):
                with pe.Fori(0, HOPS) as k:
                    def body(blocks):
                        for b, i, j in blocks:
                            pe.wait_ge(read[i], k * TURNS[i] + j)
                            for t in range(NB):
                                if t % CHUNK == 0:
                                    pe.wait_ge(here[t // CHUNK], 16 * (k + 1))
                                count = g.counts[:, t, bass.ds(b * P, P)]
                                pe.matmul(wide[i][:, :], count, hs[:, t, 0:2 * D], start=(t == 0), stop=(t == NB - 1))
                                mm = pe.matmul(narrow[i][:, 0:D], count, hs[:, t, 2 * D:3 * D], start=(t == 0),
                                               stop=(t == NB - 1))
                            mm.then_inc(summed[i], 1)
                    pairs(pe, body)


def slice_weights(nc, g, a, io):
    HW = SH * SD
    with ExitStack() as ctx:
        s = Space(nc, ctx, "swt")
        wx, wxt = s.sb("wx", [P, 2, HW]), s.sb("wxt", [P, 2, 4, P])
        wsl = s.sb("wsl", [P, SG])
        bx, bxw = s.sb("bx", [SD, SH]), s.sb("bxw", [SD, SH, P])
        bsl, inv_t = s.sb("bsl", [P, SG]), s.sb("inv_t", [P, SH])
        turn = [s.ps(f"turn{k}") for k in range(2)]
        both = [s.ps(f"both{o}") for o in range(2)]
        bias_ps = s.ps("bias_ps")
        loaded, linked, turned, copied, ready, folded = (
            s.sem(n) for n in ("loaded", "linked", "turned", "copied", "ready", "folded"))
        nm = lambda n: io[f"L1_ffn_{n}"]
        with nc.Block() as block:
            @block.sync
            def _(sp):
                sp.dma_start(a.x[:, :, :], g.x_gcn.rearrange("(b p) d -> p b d", p=P)).then_inc(loaded, 16)
                sp.dma_start(wx[:, :, :], nm("W_x").rearrange("(p k) n -> p k n", p=P)).then_inc(loaded, 16)
                for o in range(2):
                    sp.dma_start(wsl[o * SD:(o + 1) * SD, :], nm("W_slice")).then_inc(loaded, 16)
                with nc.allow_non_contiguous_dma(reason="512 numbers"):
                    sp.dma_start(bx[:, :], nm("b_x").rearrange("(h d) -> d h", h=SH)).then_inc(loaded, 16)
                sp.dma_start(bsl[:, :], across(nm("b_slice"), SG)).then_inc(loaded, 16)
                sp.dma_start(inv_t[:, :], across(nm("temperature").rearrange("a h b c -> (a h b c)"), SH)).then_inc(loaded, 16)

            @block.gpsimd
            def _(pool):
                pool.iota(a.valid[:, :], pattern=[[P, NB]], base=0, channel_multiplier=1,
                          allow_small_or_imprecise_dtypes=True).then_inc(ready, 1)

            @block.vector
            def _(dve):
                link = Linked(dve, linked)
                dve.wait_ge(loaded, 16 * 7)
                dve.wait_ge(ready, 1)
                link(dve.tensor_scalar(a.valid[:, :], a.valid[:, :], float(N), None, ALU.is_lt))
                link(dve.tensor_scalar(inv_t[:, :], inv_t[:, :], 0.1, 5.0, ALU.max, ALU.min))
                link(dve.reciprocal(inv_t[:, :], inv_t[:, :]))
                link(dve.tensor_copy(bxw[:, :, :], bx[:, :].unsqueeze(2).to_broadcast([SD, SH, P])))
                dve.sem_inc(ready, 1)
                dve.wait_ge(turned, 2)
                for k in range(2):
                    link(dve.tensor_copy(wxt[:, k, :, :].rearrange("p m n -> p (m n)"), turn[k][:, :]))
                dve.sem_inc(copied, 1)
                dve.wait_ge(folded, 1)
                for o in range(2):
                    for k in range(2):
                        link(dve.tensor_tensor(
                            a.wxs[:, k, :].rearrange("p (m o s) -> p m o s", o=2, s=SG)[:, :, o, :],
                            both[o][:, k * 256:(k + 1) * 256].rearrange("p (m s) -> p m s", s=SG),
                            inv_t[:, o:SH:2].unsqueeze(2).to_broadcast([P, 4, SG]), ALU.mult))
                heads = lambda t: t.rearrange("p (h s) -> p h s", h=SH)
                link(dve.tensor_tensor(heads(a.bias[:, :]), heads(bias_ps[:, :]),
                                       bsl[:, :].unsqueeze(1).to_broadcast([P, SH, SG]), ALU.add))
                link(dve.tensor_tensor(heads(a.bias[:, :]), heads(a.bias[:, :]),
                                       inv_t[:, :].unsqueeze(2).to_broadcast([P, SH, SG]), ALU.mult))

            @block.tensor
            def _(pe):
                pe.wait_ge(loaded, 16 * 7)
                for k in range(2):
                    for m in range(4):
                        mm = pe.transpose(turn[k][:, m * P:(m + 1) * P], wx[:, k, m * P:(m + 1) * P], g.ident[:, :])
                    mm.then_inc(turned, 1)
                pe.wait_ge(ready, 2)
                for h in range(SH):
                    pe.matmul(bias_ps[:, h * SG:(h + 1) * SG], bxw[:, h, :], wsl[0:SD, :], start=True, stop=True)
                pe.wait_ge(copied, 1)
                for o in range(2):
                    half = slice(o * SD, (o + 1) * SD)
                    for k in range(2):
                        for m in range(4):
                            c = (k * 4 + m) * SG
                            mm = pe.matmul(both[o][:, c:c + SG], wxt[half, k, m, :], wsl[half, :], start=True, stop=True)
                mm.then_inc(folded, 1)


def slice_tokens(nc, g, a, io):
    HW = SH * SG
    with ExitStack() as ctx:
        s = Space(nc, ctx, "tok")
        xs = [s.sb(f"xs{i}", [P, D + 1]) for i in range(2)]
        xt = [s.sb(f"xt{i}", [P, 2, P]) for i in range(2)]
        sw = [s.sb(f"sw{i}", [P, HW]) for i in range(2)]
        peak, total = s.sb("peak", [P, SH]), s.sb("total", [P, SH])
        zero = s.sb("zero", [P, P])
        norm = Norm(s)
        turned, flipped = s.ps("turned"), s.ps("flipped")
        lg = [s.ps(f"lg{i}") for i in range(2)]
        tok = [s.ps(f"tok{m}") for m in range(4)]
        bn, linked, summed, zeroed = s.sem("bn"), s.sem("linked"), s.sem("summed"), s.sem("zeroed")
        fed, t_done, t_copied, m_done, m_read, shifted, expd, soft, tok_done = (
            [s.sem(f"{n}{i}") for i in range(2)] for n in (
                "fed", "t_done", "t_copied", "m_done", "m_read", "shifted", "expd", "soft", "tok_done"))
        f_done, f_copied = s.sem("f_done"), s.sem("f_copied")
        heads = lambda t: t.rearrange("p (h s) -> p h s", h=SH)
        wide = lambda t: t[:, :].unsqueeze(2).to_broadcast([P, SH, SG])
        with nc.Block() as block:
            @block.vector
            def _(dve):
                norm.on_vector(dve, bn, a.x)
                dve.tensor_tensor(norm.rstd[:, :], norm.rstd[:, :], a.valid[:, :], ALU.mult).then_inc(zeroed, 1)
                dve.memset(zero[:, :], 0.0).then_inc(zeroed, 1)
                dve.wait_ge(zeroed, 2)

                def body(blocks):
                    for b, i, j in blocks:
                        dve.wait_ge(tok_done[i], j)
                        dve.tensor_copy(xs[i][:, D:D + 1], at(a.valid, b))
                        norm.block(dve, xs[i][:, 0:D], a.x, b).then_inc(fed[i], 1)
                    for b, i, j in blocks:
                        link = Linked(dve, linked, 6 * b)
                        w = heads(sw[i][:, :])
                        dve.wait_ge(m_done[i], j + 1)
                        link(dve.tensor_tensor(sw[i][:, :], lg[i][:, :], a.bias[:, :], ALU.add))
                        dve.sem_inc(m_read[i], 1)
                        link(dve.tensor_reduce(peak[:, :], w, AX, ALU.max))
                        link(dve.tensor_tensor(w, w, wide(peak), ALU.subtract))
                        dve.sem_inc(shifted[i], 1)
                        dve.wait_ge(expd[i], j + 1)
                        link(dve.tensor_reduce(total[:, :], w, AX, ALU.add))
                        link(dve.reciprocal(total[:, :], total[:, :]))
                        link(dve.tensor_tensor(w, w, wide(total), ALU.mult))
                        dve.sem_inc(soft[i], 1)
                pairs(dve, body)
                dve.wait_ge(summed, 1)
                for m in range(4):
                    dve.tensor_copy(a.tok[:, m, 0:D + 1], tok[m][:, 0:D + 1])

            @block.scalar
            def _(act):
                norm.on_scalar(act)

                def body(blocks):
                    for b, i, j in blocks:
                        act.wait_ge(t_done[i], j + 1)
                        act.wait_ge(m_done[i], j)
                        act.activation(xt[i][:, :, :].rearrange("p k n -> p (k n)"),
                                       turned[:, i * D:(i + 1) * D], ACT.Copy).then_inc(t_copied[i], 1)
                    for b, i, j in blocks:
                        act.wait_ge(shifted[i], j + 1)
                        act.activation(sw[i][:, :], sw[i][:, :], ACT.Exp).then_inc(expd[i], 1)
                    for b, i, j in blocks:
                        act.wait_ge(f_done, b + 1)
                        act.activation(at(a.swt, b), flipped[:, :], ACT.Copy).then_inc(f_copied, 1)
                pairs(act, body)

            @block.tensor
            def _(pe):
                pe.wait_ge(zeroed, 2)
                for m in range(4):
                    pe.matmul(tok[m][:, 0:D + 1], zero[:, :], a.x[:, 0:2, :].rearrange("p b d -> p (b d)")[:, 0:D + 1],
                              start=True, stop=False, skip_group_check=True)

                def body(blocks):
                    for b, i, j in blocks:
                        pe.wait_ge(fed[i], j + 1)
                        pe.wait_ge(t_copied[1 - i], j + i)
                        for k in range(2):
                            mm = pe.transpose(turned[:, i * D + k * P:i * D + (k + 1) * P], xs[i][:, k:D:2], g.ident[:, :])
                        mm.then_inc(t_done[i], 1)
                    for b, i, j in blocks:
                        pe.wait_ge(t_copied[i], j + 1)
                        pe.wait_ge(m_read[i], j)
                        for k in range(2):
                            mm = pe.matmul(lg[i][:, :], xt[i][:, k, :], a.wxs[:, k, :], start=(k == 0), stop=(k == 1))
                        mm.then_inc(m_done[i], 1)
                    for b, i, j in blocks:
                        pe.wait_ge(soft[i], j + 1)
                        pe.wait_ge(f_copied, b)
                        for m in range(4):
                            mm = pe.transpose(flipped[:, m * P:(m + 1) * P], sw[i][:, m * P:(m + 1) * P], g.ident[:, :])
                        mm.then_inc(f_done, 1)
                        for m in range(4):
                            mm = pe.matmul(tok[m][:, 0:D + 1], sw[i][:, m * P:(m + 1) * P], xs[i][:, :], start=False,
                                           stop=False, skip_group_check=True)
                        mm.then_inc(tok_done[i], 1)
                pairs(pe, body)
                for m in range(4):
                    mm = pe.matmul(tok[m][:, 0:P], zero[:, :], zero[:, :], start=False, stop=True, skip_group_check=True)
                mm.then_inc(summed, 1)


def slice_attention(nc, g, a, io):
    with ExitStack() as ctx:
        s = Space(nc, ctx, "att")
        HW = SH * SD
        wfx, bfx = s.sb("wfx", [P, 2, HW]), s.sb("bfx", [1, HW])
        wq, wk, wv = (s.sb(n, [SD, SD]) for n in ("wq", "wk", "wv"))
        wo = s.sb("wo", [SD, SH, D])
        inv = s.sb("inv", [P, 4])
        tokt, normt = s.sb("tokt", [P, 2, 4 * P]), s.sb("normt", [1, 4 * P])
        st, qt, kt, v, at_, att, ot = (s.sb(n, [SD, SH, SG]) for n in ("st", "qt", "kt", "v", "at", "att", "ot"))
        peak = s.sb("peak", [SG, SH])
        A, B, C, Dd = (s.ps(n) for n in "ABCD")
        O = [s.ps(f"O{m}") for m in range(4)]
        loaded, linked, vec, ten, expd = (s.sem(n) for n in ("loaded", "linked", "vec", "ten", "expd"))
        nm = lambda n: io[f"L1_ffn_{n}"]
        fl = lambda t: t[:, :, :].rearrange("p h g -> p (h g)")
        wide = lambda t: t[:, :].unsqueeze(2).to_broadcast([SG, SH, SG])
        with nc.Block() as block:
            @block.sync
            def _(sp):
                sp.dma_start(wfx[:, :, :], nm("W_fx").rearrange("(k p) n -> p k n", p=P)).then_inc(loaded, 16)
                sp.dma_start(bfx[:, :], nm("b_fx").rearrange("(a n) -> a n", a=1)).then_inc(loaded, 16)
                for w, n in ((wq, "W_q"), (wk, "W_k"), (wv, "W_v")):
                    sp.dma_start(w[:, :], nm(n)).then_inc(loaded, 16)
                sp.dma_start(wo[:, :, :], nm("W_out").rearrange("(h c) d -> c h d", h=SH)).then_inc(loaded, 16)

            @block.vector
            def _(dve):
                link = Linked(dve, linked)
                link(dve.tensor_scalar(inv[:, :], a.tok[:, :, D], 1e-5, None, ALU.add))
                link(dve.reciprocal(inv[:, :], inv[:, :]))
                link(dve.tensor_tensor(a.tok[:, :, 0:D + 1], a.tok[:, :, 0:D + 1],
                                       inv[:, :].unsqueeze(2).to_broadcast([P, 4, D + 1]), ALU.mult))
                dve.sem_inc(vec, 1)
                dve.wait_ge(ten, 1)
                for k, src in enumerate((A, B)):
                    link(dve.tensor_copy(tokt[:, k, :], src[:, :]))
                link(dve.tensor_copy(normt[:, :], C[0:1, :]))
                dve.sem_inc(vec, 1)
                dve.wait_ge(ten, 2)
                for h in range(SH):
                    m, o = h // 2, h % 2
                    link(dve.tensor_copy(st[:, h, :], Dd[o * SD:(o + 1) * SD, m * P + o * SG:m * P + (o + 1) * SG]))
                dve.sem_inc(vec, 1)
                dve.wait_ge(ten, 3)
                for dst, src in ((qt, A), (kt, B), (v, C)):
                    link(dve.tensor_copy(fl(dst), src[0:SD, :]))
                dve.sem_inc(vec, 1)
                dve.wait_ge(ten, 4)
                link(dve.tensor_copy(fl(at_), Dd[0:SD, :]))
                link(dve.tensor_reduce(peak[:, :], at_[:, :, :], AX, ALU.max))
                link(dve.tensor_tensor(at_[:, :, :], at_[:, :, :], wide(peak), ALU.subtract))
                dve.sem_inc(vec, 1)
                dve.wait_ge(expd, 1)
                link(dve.tensor_reduce(peak[:, :], at_[:, :, :], AX, ALU.add))
                link(dve.reciprocal(peak[:, :], peak[:, :]))
                link(dve.tensor_tensor(at_[:, :, :], at_[:, :, :], wide(peak), ALU.mult))
                dve.sem_inc(vec, 1)
                dve.wait_ge(ten, 5)
                link(dve.tensor_copy(fl(att), A[0:SD, :]))
                dve.sem_inc(vec, 1)
                dve.wait_ge(ten, 6)
                link(dve.tensor_copy(fl(ot), B[0:SD, :]))
                dve.sem_inc(vec, 1)
                dve.wait_ge(ten, 7)
                for h in range(SH):
                    m, o = h // 2, h % 2
                    link(dve.tensor_copy(a.v2[o * SG:(o + 1) * SG, m, :], O[m][0:SG, o * D:(o + 1) * D]))

            @block.scalar
            def _(act):
                act.wait_ge(vec, 5)
                act.activation(fl(at_), fl(at_), ACT.Exp, scale=float(SD) ** -0.5).then_inc(expd, 1)

            @block.tensor
            def _(pe):
                pe.wait_ge(loaded, 16 * 6)
                pe.wait_ge(vec, 1)
                for m in range(4):
                    for k, dst in enumerate((A, B)):
                        pe.transpose(dst[:, m * P:(m + 1) * P], a.tok[:, m, k * P:(k + 1) * P], g.ident[:, :])
                    mm = pe.transpose(C[0:1, m * P:(m + 1) * P], a.tok[:, m, D:D + 1], g.ident[:, :])
                mm.then_inc(ten, 1)
                pe.wait_ge(vec, 2)
                for m in range(4):
                    cols = slice(m * P, (m + 1) * P)
                    for k in range(2):
                        pe.matmul(Dd[:, cols], wfx[:, k, cols], tokt[:, k, cols], start=(k == 0), stop=False)
                    mm = pe.matmul(Dd[:, cols], bfx[0:1, cols], normt[0:1, cols], start=False, stop=True)
                mm.then_inc(ten, 1)
                pe.wait_ge(vec, 3)
                pe.matmul(A[0:SD, :], wq[:, :], fl(st), start=True, stop=True)
                pe.matmul(B[0:SD, :], wk[:, :], fl(st), start=True, stop=True)
                each = lambda dst, lhs, rhs: [pe.matmul(dst[0:SD, h * SG:(h + 1) * SG], lhs(h), rhs(h), start=True,
                                                        stop=True) for h in range(SH)][-1]
                each(C, lambda h: st[:, h, :], lambda h: wv[:, :]).then_inc(ten, 1)
                pe.wait_ge(vec, 4)
                each(Dd, lambda h: qt[:, h, :], lambda h: kt[:, h, :]).then_inc(ten, 1)
                pe.wait_ge(vec, 6)
                for h in range(SH):
                    mm = pe.transpose(A[0:SD, h * SG:(h + 1) * SG], at_[:, h, :], g.ident[0:SG, 0:SG])
                mm.then_inc(ten, 1)
                pe.wait_ge(vec, 7)
                each(B, lambda h: v[:, h, :], lambda h: att[:, h, :]).then_inc(ten, 1)
                pe.wait_ge(vec, 8)
                for h in range(SH):
                    m, o = h // 2, h % 2
                    mm = pe.matmul(O[m][0:SG, o * D:(o + 1) * D], ot[:, h, :], wo[:, h, :], start=True, stop=True)
                mm.then_inc(ten, 1)


def slice_output(nc, g, a, io, out):
    with ExitStack() as ctx:
        s = Space(nc, ctx, "out")
        now = [s.sb(f"now{i}", [P, SH * SG]) for i in range(2)]
        y = [s.sb(f"y{i}", [P, D]) for i in range(2)]
        bias = s.sb("bias", [P, D])
        acc = [s.ps(f"acc{i}") for i in range(2)]
        loaded, linked = s.sem("loaded"), s.sem("linked")
        copied, done, made, stored = ([s.sem(f"{n}{i}") for i in range(2)] for n in ("copied", "done", "made", "stored"))
        with nc.Block() as block:
            @block.sync
            def _(sp):
                sp.dma_start(bias[:, :], across(io["L1_ffn_b_out"], D)).then_inc(loaded, 16)

                def body(blocks):
                    for b, i, j in blocks:
                        sp.wait_ge(made[i], j + 1)
                        sp.dma_start(out[bass.ds(b * P, P), :], y[i][:, :]).then_inc(stored[i], 16)
                pairs(sp, body)
                for i in range(2):
                    sp.wait_ge(stored[i], 16 * TURNS[i])

            @block.scalar
            def _(act):
                def body(blocks):
                    for b, i, j in blocks:
                        act.wait_ge(done[i], j)
                        act.activation(now[i][:, :], at(a.swt, b), ACT.Copy).then_inc(copied[i], 1)
                pairs(act, body)

            @block.tensor
            def _(pe):
                def body(blocks):
                    for b, i, j in blocks:
                        pe.wait_ge(copied[i], j + 1)
                        pe.wait_ge(made[i], j)
                        for m in range(4):
                            mm = pe.matmul(acc[i][:, 0:D], now[i][:, m * P:(m + 1) * P], a.v2[:, m, :], start=(m == 0),
                                           stop=(m == 3))
                        mm.then_inc(done[i], 1)
                pairs(pe, body)

            @block.vector
            def _(dve):
                dve.wait_ge(loaded, 16)

                def body(blocks):
                    for b, i, j in blocks:
                        link = Linked(dve, linked, b)
                        dve.wait_ge(done[i], j + 1)
                        dve.wait_ge(stored[i], 16 * j)
                        link(dve.tensor_tensor(y[i][:, :], acc[i][:, 0:D], bias[:, :], ALU.add))
                        dve.tensor_tensor(y[i][:, :], y[i][:, :], at(a.x, b), ALU.add).then_inc(made[i], 1)
                pairs(dve, body)


def main_program(nc, io, out):
    with ExitStack() as whole:
        g = Space(nc, whole, "all")
        dram = lambda name, shape, dt=F32: nc.dram_tensor(name, shape, dt, kind="Internal").ap()
        g.edge_fill, g.edge_scan, g.edge_w = dram("edge_fill", [EP, SW]), dram("edge_scan", [EP, SW]), dram("edge_w", [EP * 4])
        g.edge_terms = dram("edge_terms", [P, sum(HEADS), ET])
        g.hx_rows, g.small = dram("hx_rows", [NP, ROW]), dram("small", [NP, SW])
        g.expert_in, g.expert_out = dram("expert_in", [NE * SLOTS, D]), dram("expert_out", [NE * SLOTS, D])
        g.x_norm, g.x_mid, g.x_gnn, g.x_moe, g.x_gcn = (
            dram(n, [NP, D]) for n in ("x_norm", "x_mid", "x_gnn", "x_moe", "x_gcn"))
        g.hop_parts = dram("hop_parts", [2 * NP, 3 * D], BF16)
        g.ident, g.count, g.ones = g.sb("ident", [P, P]), g.sb("count", [P, P]), g.sb("ones", [P, P])
        g.tri_upto, g.tri_below = g.sb("tri_upto", [P, P]), g.sb("tri_below", [P, P])
        g.dis, g.share = g.sb("dis", [P, NB]), g.sb("share", [P, NB])
        g.slot_in, g.slot_out = g.sb("slot_in", [P, NB], I32), g.sb("slot_out", [P, NB], I32)
        constants(nc, g)
        with ExitStack() as counted:
            g.counts = counted.enter_context(nc.sbuf_tensor("counts", [P, NB, NP], F16))
            with ExitStack() as graph:
                sb = lambda n, shape, dt=F32: graph.enter_context(nc.sbuf_tensor(n, shape, dt))
                g.src_i, g.dst_f = sb("src_i", [P, ET], I32), sb("dst_f", [P, ET])
                g.indeg, g.inv_deg, g.has, g.minus_base = (sb(n, [P, NB]) for n in ("indeg", "inv_deg", "has", "minus_base"))
                g.seg_start, g.seg_end = sb("seg_start", [P, NB], I32), sb("seg_end", [P, NB], I32)
                g.tiles = sb("tiles", [P, NB + 1], I32)
                g.small_sb, g.node_d, g.w_self = sb("small_sb", [P, NB, SW]), sb("node_d", [P, NB, 4]), sb("w_self", [P, NB, 4])
                graph_tables(nc, g, io)
                project_nodes(nc, g, io, 0, io["x"], True)
                edge_terms(nc, g, io)
                for layer, target in enumerate((g.x_mid, g.x_gnn)):
                    if layer:
                        project_nodes(nc, g, io, layer, g.x_mid, False)
                    with ExitStack() as held:
                        g.per_edge = held.enter_context(nc.sbuf_tensor(f"per_edge{layer}", [P, ET, SW], F32))
                        g.w_cols = held.enter_context(nc.sbuf_tensor(f"w_cols{layer}", [P, ET, 4], F32))
                        if layer:
                            gather_alone(nc, g, io)
                        else:
                            counts_and_gather(nc, g, io)
                        edge_weights(nc, g, io, layer)
                        aggregate(nc, g, io, layer, target)
            route(nc, g, io)
            experts(nc, g, io)
            combine(nc, g, io)
            hops_start(nc, g, io)
            hops(nc, g, io)
        with ExitStack() as slices:
            a = Space(nc, slices, "slc")
            a.x, a.swt = a.sb("x", [P, NB, D]), a.sb("swt", [P, NB, SH * SG])
            a.wxs, a.bias, a.valid = a.sb("wxs", [P, 2, SH * SG]), a.sb("bias", [P, SH * SG]), a.sb("valid", [P, NB])
            a.tok, a.v2 = a.sb("tok", [P, 4, D + 1]), a.sb("v2", [P, 4, D])
            slice_weights(nc, g, a, io)
            slice_tokens(nc, g, a, io)
            slice_attention(nc, g, a, io)
            slice_output(nc, g, a, io, out)


def kernel(**inputs):
    import numpy as np
    import concourse.bacc as bacc
    from concourse.bass_utils import run_bass_kernel_spmd

    a = {k: np.ascontiguousarray(v) for k, v in inputs.items()}
    pad = lambda v, n, fill=0: np.concatenate([v, np.full((n - len(v), *v.shape[1:]), fill, v.dtype)])
    x, src, dst, ea = a.pop("x"), a.pop("src"), a.pop("dst"), a.pop("edge_attr_32")
    src, dst, ea = pad(src, EP, NP - 1), pad(dst, EP, NP - 1), pad(ea, EP)
    arrays = {
        "x": pad(x, NP),
        "src_cols": src.reshape(ET, P).T, "dst_cols": dst.reshape(ET, P).T,
        "src_rows": src.reshape(P, ET),
        "dst_after": np.concatenate([np.full(1, -1, dst.dtype), dst]),
        "edge_attr": ea.reshape(P, ET, ED).transpose(2, 1, 0),
        **a,
    }
    arrays = {"in_" + k: np.ascontiguousarray(v).reshape(v.shape or (1,)) for k, v in arrays.items()}
    nc = bacc.Bacc("TRN2", target_bir_lowering=False, num_devices=1)
    io = {k[3:]: nc.dram_tensor(k, v.shape, mybir.dt.from_np(v.dtype), kind="ExternalInput").ap()
          for k, v in arrays.items()}
    out = nc.dram_tensor("out_0_dram", (NP, D), F32, kind="ExternalOutput").ap()
    main_program(nc, io, out)
    r = run_bass_kernel_spmd(nc, [arrays], core_ids=[0])
    return r.results[0]["out_0_dram"][:N]
```

```python
from contextlib import ExitStack

import concourse.bass as bass
from concourse import mybir

P = 128
N, E, D = 3125, 50000, 256
NB = -(-N // P)
NP = NB * P
RING = 14
ET = -(-(-(-E // P)) // RING) * RING
EP = ET * P
SPLIT = 4
ED, PH = 32, 64
HEADS = (4, 1)
SW = 8
ROW = 260
BIG = 1.0e30
LN_EPS = 1e-5
SLOPE = 0.2
NE, CAP, SLOTS, FF = 8, -(-5 * N // (4 * 8)), 512, 1024
HOPS = 5
SH, SD, SG = 8, 64, 64

ALU = mybir.AluOpType
ACT = mybir.ActivationFunctionType
AX = mybir.AxisListType.X
F32, I32, F16, BF16 = mybir.dt.float32, mybir.dt.int32, mybir.dt.float16, mybir.dt.bfloat16


def after(count):
    return count + 1


class Linked:

    def __init__(self, eng, sem, base=0):
        self.eng, self.sem, self.base, self.n = eng, sem, base, 0

    def __call__(self, instruction):
        self.n += 1
        instruction.then_inc(self.sem, 1)
        self.eng.wait_ge(self.sem, after(self.base + self.n))


class Space:

    def __init__(self, nc, ctx, tag):
        self.nc, self.ctx, self.tag, self.sems, self.from_zero = nc, ctx, tag, [], []
        ctx.callback(self.close)

    def close(self):
        self.nc.clear_and_free_semaphores(self.sems + self.from_zero)

    def block(self):
        self.arm()
        self.nc.all_engine_barrier()
        return self.nc.Block()

    def arm(self):
        for sem in self.sems:
            self.nc.gpsimd.sem_inc(sem, 1)

    def sb(self, name, shape, dt=F32):
        return self.ctx.enter_context(self.nc.sbuf_tensor(f"{self.tag}_{name}", shape, dt))

    def ps(self, name, shape=(P, 512), dt=F32):
        return self.ctx.enter_context(self.nc.psum_tensor(f"{self.tag}_{name}", list(shape), dt))

    def sem(self, name):
        self.sems.append(self.nc.alloc_semaphore(f"{self.tag}_{name}"))
        return self.sems[-1]

    def pool_sem(self, name):
        self.from_zero.append(self.nc.alloc_semaphore(f"{self.tag}_{name}"))
        return self.from_zero[-1]


def at(ap, i):
    s = ap[:, bass.ds(i, 1)] if len(ap.shape) == 2 else ap[:, bass.ds(i, 1), :]
    return s if len(ap.shape) == 2 else s.rearrange("p a f -> p (a f)")


def across(row, width):
    return row.rearrange("(a n) -> a n", a=1).to_broadcast([P, width])


def constants(nc, g):
    with ExitStack() as ctx:
        s = Space(nc, ctx, "cst")
        zero = s.sb("zero", [P, 2048])
        made, filled = s.sem("made"), s.sem("filled")
        with s.block() as block:
            @block.gpsimd
            def _(pool):
                link = Linked(pool, made)
                link(pool.memset(g.ident[:, :], 0.0))
                link(pool.affine_select(out=g.ident[:, :], in_=g.ident[:, :], compare_op=ALU.not_equal,
                                        fill=1.0, base=0, pattern=[[-1, P]], channel_multiplier=1))
                for tri, base in ((g.tri_upto, 0), (g.tri_below, -1)):
                    link(pool.memset(tri[:, :], 1.0))
                    link(pool.affine_select(out=tri[:, :], in_=tri[:, :], compare_op=ALU.is_ge, fill=0.0,
                                            base=base, pattern=[[1, P]], channel_multiplier=-1))
                link(pool.iota(g.count[:, :], pattern=[[1, P]], base=0, channel_multiplier=0,
                               allow_small_or_imprecise_dtypes=True))

            @block.vector
            def _(dve):
                nc.vector.memset(g.ones[:, :], 1.0)
                nc.vector.memset(zero[:, :], 0.0).then_inc(filled, 1)

            @block.sync
            def _(sp):
                sp.wait_ge(filled, after(1))
                sp.dma_start(g.edge_fill.rearrange("(p j) c -> p (j c)", p=P)[:, 0:2048], zero[:, :]).then_inc(filled, 16)
                sp.dma_start(g.edge_fill.rearrange("(p j) c -> p (j c)", p=P)[:, 2048:ET * SW],
                             zero[:, 0:ET * SW - 2048]).then_inc(filled, 16)
                per = NE * SLOTS * D // P // 2048
                for k in range(per):
                    sp.dma_start(g.expert_in.rearrange("(p j) c -> p (j c)", p=P)[:, k * 2048:(k + 1) * 2048],
                                 zero[:, :]).then_inc(filled, 16)
                sp.wait_ge(filled, after(1 + 16 * (2 + per)))


def graph_tables(nc, g, io):
    with ExitStack() as ctx:
        s = Space(nc, ctx, "grf")
        GRP = 8
        dst_i = s.sb("dst_i", [P, ET], I32)
        digit = s.sb("digit", [P, ET], I32)
        low, high = s.sb("low", [P, ET], F16), s.sb("high", [P, ET], F16)
        count16 = s.sb("count16", [P, P], F16)
        oh_low = s.sb("oh_low", [P, 2 * GRP, P], F16)
        oh_high = s.sb("oh_high", [P, 2 * GRP, NB], F16)
        zero16 = s.sb("zero16", [P, P], F16)
        total, upto = s.sb("total", [P, NB]), s.sb("upto", [P, NB])
        t0, t1 = s.sb("t0", [P, NB]), s.sb("t1", [P, NB])
        hist, prefix = s.ps("hist"), s.ps("prefix")
        loaded, linked, hot, used = s.sem("loaded"), s.sem("linked"), s.sem("hot"), s.sem("used")
        counted, summed, table, rooted = s.sem("counted"), s.sem("summed"), s.sem("table"), s.sem("rooted")
        have = s.sem("have")
        with s.block() as block:
            @block.sync
            def _(sp):
                sp.dma_start(dst_i[:, :], io["dst_cols"]).then_inc(loaded, 16)
                sp.dma_start(g.src_i[:, :], io["src_cols"]).then_inc(loaded, 16)

            @block.vector
            def _(dve):
                link = Linked(dve, linked)
                dve.wait_ge(loaded, after(32))
                link(nc.vector.memset(zero16[:, :], 0.0))
                link(nc.vector.tensor_copy(count16[:, :], g.count[:, :]))
                link(nc.vector.tensor_copy(g.dst_f[:, :], dst_i[:, :]))
                link(nc.vector.tensor_scalar(digit[:, :], dst_i[:, :], P - 1, None, ALU.bitwise_and))
                link(nc.vector.tensor_copy(low[:, :], digit[:, :]))
                link(nc.vector.tensor_scalar(digit[:, :], dst_i[:, :], 7, None, ALU.logical_shift_right))
                link(nc.vector.tensor_copy(high[:, :], digit[:, :]))
                nc.vector.memset(zero16[:, 0:1], 0.0).then_inc(used, 1)
                with dve.Fori(0, ET // GRP) as i:
                    dve.wait_ge(used, after(i))
                    nc.vector.tensor_tensor(
                        oh_low[:, bass.ds((i % 2) * GRP, GRP), :], count16[:, :].unsqueeze(1).to_broadcast([P, GRP, P]),
                        low[:, bass.ds(i * GRP, GRP)].unsqueeze(2).to_broadcast([P, GRP, P]), ALU.is_equal)
                    nc.vector.tensor_tensor(
                        oh_high[:, bass.ds((i % 2) * GRP, GRP), :],
                        count16[:, 0:NB].unsqueeze(1).to_broadcast([P, GRP, NB]),
                        high[:, bass.ds(i * GRP, GRP)].unsqueeze(2).to_broadcast([P, GRP, NB]),
                        ALU.is_equal).then_inc(hot, 1)
                dve.wait_ge(counted, after(1))
                nc.vector.tensor_copy(g.indeg[:, :], hist[:, 0:NB]).then_inc(have, 1)
                dve.wait_ge(summed, after(1))
                link(nc.vector.tensor_copy(total[:, :], prefix[:, 64:64 + NB]))
                link(nc.vector.memset(t0[:, :], 0.0))
                link(nc.vector.tensor_tensor_scan(upto[:, :], total[:, :], t0[:, :], 0.0, ALU.add, ALU.add))
                link(nc.vector.tensor_tensor(t0[:, :], upto[:, :], total[:, :], ALU.subtract))
                link(nc.vector.tensor_tensor(t0[:, :], t0[:, :], prefix[:, 0:NB], ALU.add))
                link(nc.vector.tensor_scalar(t1[:, :], g.indeg[:, :], 0.0, float(2 * EP), ALU.is_equal, ALU.mult))
                link(nc.vector.tensor_tensor(t1[:, :], t1[:, :], t0[:, :], ALU.add))
                link(nc.vector.tensor_copy(g.seg_start[:, :], t1[:, :]))
                link(nc.vector.tensor_tensor(t0[:, :], t0[:, :], g.indeg[:, :], ALU.add))
                link(nc.vector.tensor_scalar(t0[:, :], t0[:, :], -1.0, 0.0, ALU.add, ALU.max))
                link(nc.vector.tensor_copy(g.seg_end[:, :], t0[:, :]))
                link(nc.vector.tensor_copy(g.tiles[:, 1:NB + 1], upto[:, :]))
                link(nc.vector.tensor_scalar(g.tiles[:, 1:NB + 1], g.tiles[:, 1:NB + 1], 7, None,
                                             ALU.logical_shift_right))
                link(nc.vector.tensor_scalar(g.tiles[:, 1:NB + 1], g.tiles[:, 1:NB + 1], float(ET - 1), None, ALU.min))
                link(nc.vector.memset(g.tiles[:, 0:1], 0))
                link(nc.vector.tensor_scalar(g.tile_pairs[:, :], g.tiles[:, :], 1, None, ALU.logical_shift_right))
                link(nc.vector.tensor_scalar(g.minus_base[:, :], g.count[:, 0:NB], float(-P), None, ALU.mult))
                link(nc.vector.tensor_scalar(g.has[:, :], g.indeg[:, :], 1.0, None, ALU.min))
                link(nc.vector.tensor_scalar(t0[:, :], g.indeg[:, :], 1.0, None, ALU.max))
                link(nc.vector.reciprocal(g.inv_deg[:, :], t0[:, :]))
                nc.vector.tensor_scalar(t1[:, :], g.indeg[:, :], 1.0, None, ALU.add).then_inc(table, 1)
                dve.wait_ge(rooted, after(1))
                nc.vector.reciprocal(g.dis[:, :], t1[:, :]).then_inc(table, 1)

            @block.scalar
            def _(act):
                act.wait_ge(table, after(1))
                nc.scalar.activation(t1[:, :], t1[:, :], ACT.Sqrt).then_inc(rooted, 1)

            @block.tensor
            def _(pe):
                pe.wait_ge(hot, after(1))
                nc.tensor.matmul(hist[:, 0:NB], zero16[:, :], oh_high[:, 0, :], start=True, stop=False,
                                 skip_group_check=True)
                with pe.Fori(0, ET // GRP) as i:
                    pe.wait_ge(hot, after(i + 1))
                    for k in range(GRP):
                        mm = nc.tensor.matmul(hist[:, 0:NB], at(oh_low, (i % 2) * GRP + k), at(oh_high, (i % 2) * GRP + k),
                                              start=False, stop=False, skip_group_check=True)
                    mm.then_inc(used, 1)
                nc.tensor.matmul(hist[:, 0:NB], zero16[:, :], oh_high[:, 0, :], start=False, stop=True,
                                 skip_group_check=True).then_inc(counted, 1)
                pe.wait_ge(have, after(1))
                nc.tensor.matmul(prefix[:, 0:NB], g.tri_below[:, :], g.indeg[:, :], start=True, stop=True)
                nc.tensor.matmul(prefix[:, 64:64 + NB], g.ones[:, :], g.indeg[:, :], start=True,
                                 stop=True).then_inc(summed, 1)


def inverse_root(dve, link, out, var, root, half):
    link(dve.reciprocal(out, root))
    link(dve.tensor_tensor(half, out, out, ALU.mult))
    link(dve.tensor_tensor(half, half, var, ALU.mult))
    link(dve.tensor_scalar(half, half, -0.5, 1.5, ALU.mult, ALU.add))
    link(dve.tensor_tensor(out, out, half, ALU.mult))


class Norm:

    def __init__(self, s):
        self.stats, self.pair = s.sb("stats", [P, NB, 6]), s.sb("pair", [P, NB, 2])
        self.mean, self.var = s.sb("mean", [P, NB]), s.sb("var", [P, NB])
        self.root, self.half, self.rstd = (s.sb(n, [P, NB]) for n in ("root", "half", "rstd"))
        self.varied, self.rooted = s.sem("varied"), s.sem("rooted")

    def on_vector(self, dve, sem, x):
        with dve.Fori(0, NB) as b:
            dve.bn_stats(at(self.stats, b), at(x, b)).then_inc(sem, 1)
        dve.wait_ge(sem, after(NB))
        link = Linked(dve, sem, NB)
        for b in range(NB):
            last = dve.bn_aggr(self.pair[:, b, :], self.stats[:, b, :])
        link(last)
        link(dve.tensor_scalar(self.var[:, :], self.pair[:, :, 1], LN_EPS, None, ALU.add))
        link(dve.tensor_copy(self.mean[:, :], self.pair[:, :, 0]))
        dve.sem_inc(self.varied, 1)
        dve.wait_ge(self.rooted, after(1))
        inverse_root(dve, link, self.rstd[:, :], self.var[:, :], self.root[:, :], self.half[:, :])

    def block(self, dve, out, x, b):
        return dve.tensor_scalar(out, at(x, b), at(self.mean, b), at(self.rstd, b), ALU.subtract, ALU.mult)

    def on_scalar(self, act):
        act.wait_ge(self.varied, after(1))
        act.activation(self.root[:, :], self.var[:, :], ACT.Sqrt).then_inc(self.rooted, 1)


def pairs(eng, body):
    with eng.Fori(0, NB // 2) as j:
        body(((2 * j, 0, j), (2 * j + 1, 1, j)))
    if NB % 2:
        body(((NB - 1, 0, NB // 2),))


def project_nodes(nc, g, io, layer, x_in, normalise):
    H = HEADS[layer]
    F = D // H
    W = D + 2 * H + 1
    with ExitStack() as ctx:
        s = Space(nc, ctx, f"prj{layer}")
        x = s.sb("x", [P, NB, D])
        w = s.sb("w", [P, 2, W])
        wo = s.sb("wo", [P, 2])
        a_row = s.sb("a_row", [P, 2, D])
        prod = s.sb("prod", [P, D])
        bo = s.sb("bo", [P, 1])
        xs = [s.sb(f"xs{i}", [P, D]) for i in range(2)]
        xt = [s.sb(f"xt{i}", [P, 2, P]) for i in range(2)]
        full = [s.sb(f"row{i}", [P, ROW]) for i in range(2)]
        row = [r[:, 0:H * (F + 1)].rearrange("p (h f) -> p h f", h=H) for r in full]
        sums = s.sb("sums", [P, NB, 2 * H + 1])
        norm = Norm(s) if normalise else None
        turned = [s.ps(f"turned{i}") for i in range(2)]
        prod_ps = [s.ps(f"prod_ps{i}") for i in range(2)]
        loaded, wts, linked, link2, wready = (s.sem(n) for n in ("loaded", "wts", "linked", "link2", "wready"))
        fed, t_done, t_copied, m_done, m_read, stored, kept = (
            [s.sem(f"{n}{i}") for i in range(2)]
            for n in ("fed", "t_done", "t_copied", "m_done", "m_read", "stored", "kept"))
        summed, expd, tabled, out_done = (s.sem(n) for n in ("summed", "expd", "tabled", "out_done"))
        nm = lambda n: io[f"L0_gnn_{n}{layer}"]
        with s.block() as block:
            @block.sync
            def _(sp):
                sp.dma_start(x[:, :, :], x_in.rearrange("(b p) d -> p b d", p=P)).then_inc(loaded, 16)
                sp.dma_start(w[:, :, 0:D], nm("Wg").rearrange("(p k) n -> p k n", p=P)).then_inc(wts, 16)
                sp.dma_start(wo[:, :], nm("Wo").rearrange("(p k) -> p k", p=P)).then_inc(wts, 16)
                sp.dma_start(a_row[:, 0, :], across(nm("as").rearrange("h f -> (h f)"), D)).then_inc(wts, 16)
                sp.dma_start(a_row[:, 1, :], across(nm("ad").rearrange("h f -> (h f)"), D)).then_inc(wts, 16)
                sp.dma_start(bo[:, :], across(nm("bo"), 1)).then_inc(wts, 16)

                def body(blocks):
                    if normalise:
                        for b, i, j in blocks:
                            sp.wait_ge(fed[i], after(j + 1))
                            sp.dma_start(g.x_norm[bass.ds(b * P, P), :], xs[i][:, :]).then_inc(kept[i], 16)
                    for b, i, j in blocks:
                        sp.wait_ge(m_read[i], after(j + 1))
                        sp.dma_start(g.hx_rows[bass.ds(b * P, P), :], full[i][:, :]).then_inc(stored[i], 16)
                pairs(sp, body)
                sp.wait_ge(tabled, after(1))
                sp.dma_start(g.small.rearrange("(b p) c -> p b c", p=P), g.small_sb[:, :, :]).then_inc(out_done, 16)
                sp.wait_ge(out_done, after(16))
                for i, turns in ((0, -(-NB // 2)), (1, NB // 2)):
                    sp.wait_ge(stored[i], after(16 * turns))
                    if normalise:
                        sp.wait_ge(kept[i], after(16 * turns))

            @block.vector
            def _(dve):
                dve.wait_ge(loaded, after(16))
                if normalise:
                    norm.on_vector(dve, linked, x)
                dve.wait_ge(wts, after(80))
                link = Linked(dve, link2)
                for k in range(2):
                    for c in range(2):
                        link(dve.tensor_tensor(prod[:, :], w[:, k, 0:D], a_row[:, c, :], ALU.mult))
                        link(dve.tensor_reduce(w[:, k, D + c * H:D + (c + 1) * H],
                                               prod[:, :].rearrange("p (h f) -> p h f", h=H), AX, ALU.add))
                link(dve.tensor_copy(w[:, :, W - 1], wo[:, :]))
                link(dve.memset(full[0][:, :], 1.0))
                link(dve.memset(full[1][:, :], 1.0))
                dve.sem_inc(wready, 1)

                def body(blocks):
                    for b, i, j in blocks:
                        dve.wait_ge(t_done[i], after(j))
                        if normalise:
                            dve.wait_ge(kept[i], after(16 * j))
                            norm.block(dve, xs[i][:, :], x, b).then_inc(fed[i], 1)
                        else:
                            dve.tensor_copy(xs[i][:, :], at(x, b)).then_inc(fed[i], 1)
                    for b, i, j in blocks:
                        dve.wait_ge(m_done[i], after(j + 1))
                        dve.wait_ge(stored[i], after(16 * j))
                        dve.tensor_copy(row[i][:, :, 0:F], prod_ps[i][:, 0:D].rearrange("p (h f) -> p h f", h=H))
                        dve.tensor_copy(at(sums, b), prod_ps[i][:, D:W]).then_inc(m_read[i], 1)
                pairs(dve, body)
                dve.wait_ge(m_read[0], after(-(-NB // 2)))
                dve.wait_ge(m_read[1], after(NB // 2))
                link(dve.memset(g.small_sb[:, :, :], 0.0))
                link(dve.tensor_copy(g.small_sb[:, :, 0:H], sums[:, :, 0:H]))
                dve.tensor_copy(g.node_d[:, :, 0:H], sums[:, :, H:2 * H]).then_inc(summed, 1)

            @block.scalar
            def _(act):
                if normalise:
                    norm.on_scalar(act)

                def body(blocks):
                    for b, i, j in blocks:
                        act.wait_ge(t_done[i], after(j + 1))
                        act.wait_ge(m_done[i], after(j))
                        act.activation(xt[i][:, :, :].rearrange("p k n -> p (k n)"), turned[i][:, 0:2 * P],
                                       ACT.Copy).then_inc(t_copied[i], 1)
                pairs(act, body)
                act.wait_ge(summed, after(1))
                act.activation(g.small_sb[:, :, 4], sums[:, :, 2 * H], ACT.Exp, bias=bo[:, 0:1]).then_inc(tabled, 1)

            @block.tensor
            def _(pe):
                pe.wait_ge(loaded, after(16))
                pe.wait_ge(wready, after(1))

                def body(blocks):
                    for b, i, j in blocks:
                        pe.wait_ge(fed[i], after(j + 1))
                        pe.wait_ge(t_copied[i], after(j))
                        for k in range(2):
                            mm = pe.transpose(turned[i][:, k * P:(k + 1) * P], xs[i][:, k:D:2], g.ident[:, :])
                        mm.then_inc(t_done[i], 1)
                    for b, i, j in blocks:
                        pe.wait_ge(t_copied[i], after(j + 1))
                        pe.wait_ge(m_read[i], after(j))
                        for k in range(2):
                            mm = pe.matmul(prod_ps[i][:, 0:W], xt[i][:, k, :], w[:, k, :], start=(k == 0), stop=(k == 1))
                        mm.then_inc(m_done[i], 1)
                pairs(pe, body)


def edge_terms(s, g, io, banks):
    COLS = 8
    WIDE = COLS * P // 2
    HT = sum(HEADS)
    room, used = g.counts[:, :, :].rearrange("p b n -> p (b n)").bitcast(F32), [0]

    def part(width, rows=P):
        used[0] += width
        return room[0:rows, used[0] - width:used[0]]

    ea = part(2 * COLS * P, ED).rearrange("f (i c) -> f i c", i=2)
    we, be = part(2 * PH, ED), part(1)
    wge, ae, v = part(D), part(D), part(HT)
    hid = [part(WIDE) for i in range(2)]
    terms = part(HT * ET).rearrange("p (h j) -> p h j", h=HT)
    up, down = banks[0:2], banks[2]
    wts, linked, ready, out_done = (s.sem(n) for n in ("e_wts", "e_linked", "e_ready", "e_out_done"))
    came = [s.sem(f"e_came{i}") for i in range(2)]
    upped, activated, downed, copied = (s.sem(n) for n in ("upped", "activated", "downed", "copied"))
    turns = ET // COLS

    def on_sync(sp):
        for n in range(2):
            lo, hi = n * PH, (n + 1) * PH
            sp.dma_start(we[:, lo:hi], io[f"L0_gnn_We{n}"]).then_inc(wts, 16)
            sp.dma_start(be[lo:hi, :], io[f"L0_gnn_be{n}"].rearrange("(p a) -> p a", a=1)).then_inc(wts, 16)
            sp.dma_start(wge[lo:hi, :], io[f"L0_gnn_Wge{n}"]).then_inc(wts, 16)
            sp.dma_start(ae[lo:hi, :], io[f"L0_gnn_ae{n}"].rearrange("h f -> (h f)").rearrange(
                "(a n) -> a n", a=1).to_broadcast([PH, D])).then_inc(wts, 16)

        def load(j, i):
            sp.dma_start(ea[:, i, :], io["edge_attr"][:, bass.ds(j * COLS, COLS), :].rearrange(
                "f j p -> f (j p)")).then_inc(came[i], 16)

        load(0, 0)
        load(1, 1)
        with sp.Fori(0, turns // 2 - 1) as j:
            sp.wait_ge(upped, after(4 * j + 2))
            load(2 * j + 2, 0)
            sp.wait_ge(upped, after(4 * j + 4))
            load(2 * j + 3, 1)
        sp.wait_ge(upped, after(2 * (turns - 2)))
        load(turns - 1, 0)
        sp.wait_ge(copied, after(turns))
        sp.dma_start(g.edge_terms, terms[:, :, :]).then_inc(out_done, 16)
        sp.wait_ge(out_done, after(16))

    def on_vector(dve):
        link = Linked(dve, linked)
        dve.wait_ge(wts, after(16 * 8))
        link(dve.memset(v[:, :], 0.0))
        link(dve.tensor_tensor(wge[:, :], wge[:, :], ae[:, :], ALU.mult))
        for n, lo in ((0, 0), (1, HEADS[0])):
            link(dve.tensor_reduce(v[n * PH:(n + 1) * PH, lo:lo + HEADS[n]],
                                   wge[n * PH:(n + 1) * PH, :].rearrange("p (h f) -> p h f", h=HEADS[n]),
                                   AX, ALU.add))
        dve.sem_inc(ready, 1)
        with dve.Fori(0, turns) as j:
            dve.wait_ge(downed, after(2 * j + 2))
            dve.tensor_copy(terms[:, :, bass.ds(j * COLS, COLS)],
                            down[:, 0:COLS * HT].rearrange("p (c h) -> p h c", h=HT)).then_inc(copied, 1)

    def on_scalar(act):
        with act.Fori(0, turns) as j:
            for i in range(2):
                act.wait_ge(upped, after(2 * j + i + 1))
                act.wait_ge(downed, after(2 * j + i))
                act.activation(hid[i], up[i][:, :], ACT.Relu, bias=be[:, 0:1]).then_inc(activated, 1)

    def on_tensor(pe):
        pe.wait_ge(ready, after(1))

        def turn(j, i, nth):
            pe.wait_ge(came[i], after(16 * nth))
            pe.wait_ge(activated, after(2 * j))
            for k in range(2):
                pe.matmul(up[k][:, :], we[:, :], ea[:, i, k * WIDE:(k + 1) * WIDE], start=True,
                          stop=True).then_inc(upped, 1)
            pe.wait_ge(copied, after(j))
            for k in range(2):
                pe.wait_ge(activated, after(2 * j + k + 1))
                for c in range(COLS // 2):
                    col = (k * (COLS // 2) + c) * HT
                    mm = pe.matmul(down[:, col:col + HT], hid[k][:, c * P:(c + 1) * P], v[:, :],
                                   start=True, stop=True)
                mm.then_inc(downed, 1)

        with pe.Fori(0, turns // 2) as j:
            turn(2 * j, 0, j + 1)
            turn(2 * j + 1, 1, j + 1)
        turn(turns - 1, 0, turns // 2 + 1)
        pe.wait_ge(copied, after(turns))

    def over(eng):
        eng.wait_ge(out_done, after(16))

    return on_sync, on_vector, on_scalar, on_tensor, over


def gather_small(s, g, io):
    half = RING // 2
    ring = s.sb("ring", [P, RING, SW])
    ids = g.ids
    now = [s.sb(f"now{i}", [P, half], I32) for i in range(2)]
    came = [s.pool_sem(f"came{k}") for k in range(RING)]
    listed = s.pool_sem("listed")
    picked, taken, gate = (s.sem(n) for n in ("picked", "taken", "gate"))

    def on_pool(pool):
        def issue(j, i):
            pool.tensor_copy(now[i][:, :], ids[:, bass.ds(j * RING + i * half, half)]).then_inc(picked, 1)
            pool.wait_ge(picked, after(2 * j + i + 1))
            pool.sem_inc(gate, 1)
            for k in range(half):
                pool.indirect_dma_start(
                    out=ring[:, i * half + k, :], out_offset=None, in_=g.small,
                    in_offset=bass.IndirectOffsetOnAxis(ap=now[i][:, k:k + 1], axis=0)
                ).then_inc(came[i * half + k], 16)

        def take(j, i):
            for k in range(half):
                pool.wait_ge(came[i * half + k], 16 * (j + 1))
            pool.tensor_copy(g.per_edge[:, bass.ds(j * RING + i * half, half), :],
                             ring[:, i * half:(i + 1) * half, :]).then_inc(taken, 1)
            pool.wait_ge(taken, after(2 * j + i + 1))

        pool.dma_start(ids[:, :], io["src_rows"]).then_inc(listed, 16)
        pool.wait_ge(listed, 16)
        issue(0, 0)
        issue(0, 1)
        with pool.Fori(1, ET // RING) as j:
            for i in range(2):
                take(j - 1, i)
                issue(j, i)
        take(ET // RING - 1, 0)
        take(ET // RING - 1, 1)

    return on_pool


def counts_and_gather(nc, g, io, c_sems, blocks, first_part):
    lo, hi = blocks
    with ExitStack() as ctx:
        s = Space(nc, ctx, f"cnt{lo}")
        BANK = 512
        banks = [(c, min(BANK, NP - c)) for c in range(0, NP, BANK)]
        n_act = (len(banks) + 1) // 2
        n_dve = len(banks) // 2
        DEPTH = 3
        HALF = NP // 2
        src_f = s.sb("src_f", [P, ET])
        number = s.sb("number", [P, NP], F16)
        oh_src = s.sb("oh_src", [P, DEPTH, NP], F16)
        oh_dst = s.sb("oh_dst", [P, DEPTH, P], F16)
        count16 = s.sb("count16", [P, P], F16)
        zero16 = s.sb("zero16", [P, P], F16)
        acc = [s.ps(f"acc{i}") for i in range(len(banks))]
        numbered, linked, ready, diag = (s.sem(n) for n in ("numbered", "linked", "ready", "diag"))
        hot, used, summed, act_read, dve_read = c_sems
        gather_on_pool = gather_small(s, g, io)
        edges = edge_terms(s, g, io, acc) if first_part else None
        with s.block() as block:
            if edges:
                @block.sync
                def _(sp):
                    edges[0](sp)

            @block.gpsimd
            def _(pool):
                pool.iota(number[:, :], pattern=[[1, NP]], base=-HALF, channel_multiplier=0,
                          allow_small_or_imprecise_dtypes=True).then_inc(numbered, 1)
                gather_on_pool(pool)

            def bounds(eng, b):
                return (eng.value_load(g.tiles[0:1, bass.ds(b, 1)], min_val=0, max_val=ET - 1),
                        eng.value_load(g.tiles[0:1, bass.ds(b + 1, 1)], min_val=0, max_val=ET - 1))

            @block.vector
            def _(dve):
                if edges:
                    edges[1](dve)
                link = Linked(dve, linked)
                link(dve.memset(zero16[:, :], 0.0))
                link(dve.tensor_copy(count16[:, :], g.count[:, :]))
                link(dve.tensor_scalar(src_f[:, :], g.src_i[:, :], float(-HALF), None, ALU.add))
                dve.sem_inc(ready, 1)
                dve.wait_ge(numbered, after(1))
                if edges:
                    dve.sem_inc(dve_read, n_dve)
                    edges[4](dve)

                def step(t, b):
                    dve.wait_ge(used, after(t + b))
                    dve.tensor_scalar(at(oh_dst, (t + b) % DEPTH), count16[:, :], at(g.dst_f, t), at(g.minus_base, b),
                                      ALU.subtract, ALU.is_equal)
                    dve.tensor_scalar(at(oh_src, (t + b) % DEPTH), number[:, :], at(src_f, t), None,
                                      ALU.is_equal).then_inc(hot, 1)

                def block_sums(b, more):
                    first, last = bounds(dve, b)
                    with dve.If(last > first):
                        with dve.Fori(first + 1, last + 1) as t:
                            step(t, b)
                    if more:
                        step(last, b + 1)
                    dve.wait_ge(summed, after(b + 1))
                    for n, (c, width) in enumerate(banks):
                        if n % 2:
                            dve.tensor_copy(g.counts[:, bass.ds(b, 1), c:c + width].rearrange("p a f -> p (a f)"),
                                            acc[n][:, 0:width]).then_inc(dve_read, 1)

                step(bounds(dve, lo)[0], lo)
                with dve.Fori(lo, hi - 1) as b:
                    block_sums(b, True)
                block_sums(hi - 1, False)
                dve.wait_ge(act_read, after((hi + 1) * n_act))
                dve.wait_ge(dve_read, after((hi + 1) * n_dve))
                for b in range(lo, hi):
                    own = g.counts[:, b, b * P:(b + 1) * P]
                    dve.tensor_tensor(own, own, g.ident[:, :], ALU.add).then_inc(diag, 1)

            @block.scalar
            def _(act):
                if edges:
                    edges[2](act)
                    act.sem_inc(act_read, n_act)
                    edges[4](act)
                with act.Fori(lo, hi) as b:
                    act.wait_ge(summed, after(b + 1))
                    for n, (c, width) in enumerate(banks):
                        if n % 2 == 0:
                            act.activation(g.counts[:, bass.ds(b, 1), c:c + width].rearrange("p a f -> p (a f)"),
                                           acc[n][:, 0:width], ACT.Copy).then_inc(act_read, 1)

            @block.tensor
            def _(pe):
                if edges:
                    edges[3](pe)
                    pe.sem_inc(used, DEPTH - 1)
                pe.wait_ge(ready, after(1))
                with pe.Fori(lo, hi) as b:
                    first, last = bounds(pe, b)
                    for n, (c, width) in enumerate(banks):
                        if n % 2:
                            pe.wait_ge(dve_read, after(b * n_dve + n // 2 + 1))
                        else:
                            pe.wait_ge(act_read, after(b * n_act + n // 2 + 1))
                        pe.matmul(acc[n][:, 0:1], zero16[:, 0:P], zero16[:, 0:1], start=True, stop=False,
                                  skip_group_check=True)
                    with pe.Fori(first, last + 1) as t:
                        pe.wait_ge(hot, after(t + b + 1))
                        for n, (c, width) in enumerate(banks):
                            mm = pe.matmul(acc[n][:, 0:width], at(oh_dst, (t + b) % DEPTH),
                                           oh_src[:, bass.ds((t + b) % DEPTH, 1), c:c + width].rearrange("p a f -> p (a f)"),
                                           start=False, stop=False, skip_group_check=True)
                        mm.then_inc(used, 1)
                    for n, (c, width) in enumerate(banks):
                        mm = pe.matmul(acc[n][:, 0:1], zero16[:, 0:P], zero16[:, 0:1], start=False, stop=True,
                                       skip_group_check=True)
                    mm.then_inc(summed, 1)


def edge_weights(nc, g, io, layer):
    H = HEADS[layer]
    first_head = sum(HEADS[:layer])
    chunks = [(c, min(P, ET - c)) for c in range(0, ET, P)]
    with ExitStack() as ctx:
        s = Space(nc, ctx, f"wts{layer}")
        u, v = s.sb("u", [P, H * ET]), s.sb("v", [P, H * ET])
        uh, vh = (x[:, :].rearrange("p (h j) -> p h j", h=H) for x in (u, v))
        dsts = s.sb("dsts", [P, 2 * ET], I32)
        before, here, tail = dsts[:, 0:ET], dsts[:, ET:], dsts[:, :].bitcast(F32)
        same, fresh = s.sb("same", [P, ET]), s.sb("fresh", [P, ET])
        rows = s.sb("rows", [P, 4, 2 * H])
        turned = s.sb("turned", [2 * H, 4, P])
        chain = s.sb("chain", [2 * H, 2, P + 1])
        carry = s.sb("carry", [P, 2, 2 * H])
        ends, fill = g.spare[:, 0, :, :], g.spare[:, 1, :, :]
        self_v, top = s.sb("self_v", [P, NB, H]), s.sb("top", [P, NB, H])
        turn_ps, back_ps = s.ps("turn_ps"), s.ps("back_ps")
        cols_ps = [s.ps(f"cols_ps{i}") for i in range(2)]
        loaded, linked = s.sem("loaded"), s.sem("linked")
        summed_up, transposed, chained, returned = (s.sem(n) for n in ("summed_up", "transposed", "chained", "returned"))
        scanned, stored, node_done, spread = (s.sem(n) for n in ("scanned", "stored", "node_done", "spread"))
        gathered, scattered = s.pool_sem("gathered"), s.pool_sem("scattered")
        weighed, exp_done, w_stored, turned_cols, copied_cols = (
            s.sem(n) for n in ("weighed", "exp_done", "w_stored", "turned_cols", "copied_cols"))
        w_loaded = [s.sem(f"w_loaded{i}") for i in range(len(chunks))]
        by_tile = [u[0:n, i * P * H:(i + 1) * P * H] if i < len(chunks) - 1 else tail[0:n, 0:P * H]
                   for i, (_, n) in enumerate(chunks)]
        pe_all = g.per_edge
        per_node = lambda x: x[:, :].unsqueeze(2).to_broadcast([P, NB, H])
        with s.block() as block:
            @block.sync
            def _(sp):
                sp.dma_start(before, io["dst_after"][0:EP].rearrange("(p j) -> p j", p=P)).then_inc(loaded, 16)
                sp.dma_start(here, io["dst_after"][1:EP + 1].rearrange("(p j) -> p j", p=P)).then_inc(loaded, 16)
                sp.dma_start(uh, g.edge_terms[:, first_head:first_head + H, :]).then_inc(loaded, 16)
                sp.wait_ge(scanned, after(1))
                sp.dma_start(g.edge_scan.rearrange("(p j) c -> p j c", p=P), pe_all[:, :, :]).then_inc(stored, 16)
                sp.wait_ge(scattered, 16 * NB)
                sp.dma_start(pe_all[:, :, :], g.edge_fill.rearrange("(p j) c -> p j c", p=P)).then_inc(spread, 16)
                sp.wait_ge(exp_done, after(2))
                w_dram = g.edge_w[0:EP * H]
                sp.dma_start(w_dram.rearrange("(p c) -> p c", p=P), v[:, :]).then_inc(w_stored, 16)
                sp.wait_ge(w_stored, after(16))
                for i, (c, n) in enumerate(chunks):
                    sp.dma_start(by_tile[i], w_dram.rearrange("(t c) -> t c", t=ET)[c:c + n, :]).then_inc(w_loaded[i], 16)

            @block.gpsimd
            def _(pool):
                pool.wait_ge(stored, after(16))
                for b in range(NB):
                    pool.indirect_dma_start(
                        out=ends[:, b, :], out_offset=None, in_=g.edge_scan,
                        in_offset=bass.IndirectOffsetOnAxis(ap=g.seg_end[:, b:b + 1], axis=0)).then_inc(gathered, 16)
                pool.wait_ge(node_done, after(1))
                for b in range(NB):
                    pool.indirect_dma_start(
                        out=g.edge_fill, out_offset=bass.IndirectOffsetOnAxis(ap=g.seg_start[:, b:b + 1], axis=0),
                        in_=fill[:, b, :], in_offset=None, bounds_check=EP - 1, oob_is_err=False).then_inc(scattered, 16)

            @block.vector
            def _(dve):
                link = Linked(dve, linked)
                events = [0]

                def scan_sum(out, data, start):
                    link(dve.tensor_tensor_scan(out, same[:, :], data, start, ALU.mult, ALU.add))

                def scan_max(out, data, start):
                    link(dve.tensor_tensor_scan(out, fresh[:, :], data, start, ALU.add, ALU.max))

                def carries(n_sum, n_max):
                    n = max(n_sum, n_max)
                    events[0] += 1
                    dve.sem_inc(summed_up, 1)
                    dve.wait_ge(transposed, after(events[0]))
                    link(dve.tensor_copy(turned[0:n, :, :].rearrange("h k p -> h (k p)"), turn_ps[0:n, :]))
                    link(dve.memset(chain[0:n, 0, 0:1], 0.0))
                    link(dve.memset(chain[0:n, 1, 0:1], -BIG))
                    link(dve.tensor_tensor_scan(chain[0:n, 0, 1:P + 1], turned[0:n, 2, :], turned[0:n, 0, :], 0.0,
                                                ALU.mult, ALU.add))
                    link(dve.tensor_tensor_scan(chain[0:n, 1, 1:P + 1], turned[0:n, 3, :], turned[0:n, 1, :], -BIG,
                                                ALU.add, ALU.max))
                    dve.sem_inc(chained, 1)
                    dve.wait_ge(returned, after(events[0]))
                    link(dve.tensor_copy(carry[:, :, 0:n], back_ps[:, 0:2 * n].rearrange("p (k h) -> p k h", k=2)))

                dve.wait_ge(loaded, after(48))
                link(dve.tensor_tensor(same[:, :], before, here, ALU.is_equal))
                link(dve.tensor_scalar(fresh[:, :], same[:, :], -1.0, BIG, ALU.add, ALU.mult))
                link(dve.memset(rows[:, :, :], 0.0))
                link(dve.tensor_reduce(rows[:, 2, 0:1], same[:, :], AX, ALU.min))
                link(dve.tensor_copy(rows[:, 2, 1:2 * H], rows[:, 2, 0:1].to_broadcast([P, 2 * H - 1])))
                link(dve.tensor_scalar(rows[:, 3, :], rows[:, 2, :], -1.0, BIG, ALU.add, ALU.mult))
                link(dve.tensor_tensor(uh, uh, pe_all[:, :, 4:5].rearrange("p j a -> p a j").to_broadcast([P, H, ET]),
                                       ALU.mult))
                link(dve.tensor_tensor(vh, uh, pe_all[:, :, 0:H].rearrange("p j h -> p h j"), ALU.add))
                for h in range(H):
                    scan_sum(pe_all[:, :, h], uh[:, h, :], 0.0)
                    scan_max(pe_all[:, :, H + h], vh[:, h, :], -BIG)
                link(dve.tensor_copy(rows[:, 0, 0:H], pe_all[:, ET - 1, 0:H]))
                link(dve.tensor_copy(rows[:, 1, 0:H], pe_all[:, ET - 1, H:2 * H]))
                carries(2 * H, 2 * H)
                for h in range(H):
                    scan_sum(pe_all[:, :, h], uh[:, h, :], carry[:, 0, h:h + 1])
                    scan_max(pe_all[:, :, H + h], vh[:, h, :], carry[:, 1, h:h + 1])
                dve.sem_inc(scanned, 1)

                dve.wait_ge(gathered, 16 * NB)
                link(dve.memset(fill[:, :, :], 0.0))
                total, peak = ends[:, :, 0:H], ends[:, :, H:2 * H]
                link(dve.tensor_tensor(self_v[:, :, :], total, per_node(g.inv_deg), ALU.mult))
                link(dve.tensor_tensor(self_v[:, :, :], self_v[:, :, :], per_node(g.has), ALU.mult))
                link(dve.tensor_tensor(self_v[:, :, :], self_v[:, :, :], g.small_sb[:, :, 0:H], ALU.add))
                link(dve.tensor_tensor(top[:, :, :], peak, per_node(g.has), ALU.mult))
                link(dve.tensor_scalar(ends[:, :, 0], g.has[:, :], -1.0, BIG, ALU.add, ALU.mult))
                link(dve.tensor_tensor(top[:, :, :], top[:, :, :], ends[:, :, 0:1].to_broadcast([P, NB, H]), ALU.add))
                link(dve.tensor_tensor(top[:, :, :], top[:, :, :], self_v[:, :, :], ALU.max))
                link(dve.tensor_tensor(top[:, :, :], top[:, :, :], g.node_d[:, :, 0:H], ALU.add))
                link(dve.scalar_tensor_tensor(fill[:, :, H:2 * H], top[:, :, :], SLOPE, top[:, :, :], ALU.mult, ALU.max))
                link(dve.tensor_copy(fill[:, :, 0:H], g.node_d[:, :, 0:H]))
                dve.sem_inc(node_done, 1)
                link(dve.tensor_tensor(self_v[:, :, :], self_v[:, :, :], g.node_d[:, :, 0:H], ALU.add))
                link(dve.scalar_tensor_tensor(self_v[:, :, :], self_v[:, :, :], SLOPE, self_v[:, :, :], ALU.mult, ALU.max))
                link(dve.tensor_tensor(self_v[:, :, :], self_v[:, :, :], fill[:, :, H:2 * H], ALU.subtract))
                dve.sem_inc(weighed, 1)

                dve.wait_ge(spread, after(16))
                for c in range(2 * H):
                    scan_sum(uh[:, 0, :], pe_all[:, :, c], 0.0)
                    link(dve.tensor_copy(rows[:, 0, c:c + 1], uh[:, 0, ET - 1:ET]))
                carries(2 * H, 2 * H)
                for c in range(2 * H):
                    scan_sum(pe_all[:, :, c], pe_all[:, :, c], carry[:, 0, c:c + 1])
                link(dve.tensor_tensor(uh, vh, pe_all[:, :, 0:H].rearrange("p j h -> p h j"), ALU.add))
                link(dve.scalar_tensor_tensor(u[:, :], u[:, :], SLOPE, u[:, :], ALU.mult, ALU.max))
                link(dve.tensor_tensor(uh, uh, pe_all[:, :, H:2 * H].rearrange("p j h -> p h j"), ALU.subtract))
                dve.sem_inc(weighed, 1)
                for i, (c, n) in enumerate(chunks):
                    for h in range(H):
                        k = i * H + h
                        dve.wait_ge(turned_cols, after(k + 1))
                        dve.tensor_copy(g.w_cols[:, c:c + n, h], cols_ps[k % 2][:, 0:n]).then_inc(copied_cols, 1)

            @block.scalar
            def _(act):
                act.wait_ge(weighed, after(1))
                act.activation(g.w_self[:, :, 0:H], self_v[:, :, :], ACT.Exp).then_inc(exp_done, 1)
                act.wait_ge(weighed, after(2))
                act.activation(v[:, :].rearrange("p (j h) -> p h j", h=H), uh, ACT.Exp).then_inc(exp_done, 1)

            @block.tensor
            def _(pe):
                for n in range(2):
                    pe.wait_ge(summed_up, after(n + 1))
                    for k in range(4):
                        mm = pe.transpose(turn_ps[0:2 * H, k * P:(k + 1) * P], rows[:, k, :], g.ident[:, :])
                    mm.then_inc(transposed, 1)
                    pe.wait_ge(chained, after(n + 1))
                    for k in range(2):
                        mm = pe.transpose(back_ps[:, k * 2 * H:(k + 1) * 2 * H], chain[:, k, 0:P],
                                          g.ident[0:2 * H, 0:2 * H])
                    mm.then_inc(returned, 1)
                for i, (c, n) in enumerate(chunks):
                    pe.wait_ge(w_loaded[i], after(16))
                    for h in range(H):
                        k = i * H + h
                        if k >= 2:
                            pe.wait_ge(copied_cols, after(k - 1))
                        pe.transpose(cols_ps[k % 2][:, 0:n], by_tile[i][:, h:P * H:H],
                                     g.ident[0:n, 0:n]).then_inc(turned_cols, 1)


def aggregate(nc, g, io, layer, out_dram):
    H = HEADS[layer]
    F = D // H
    R = H * (F + 1)
    half = RING // 2
    with ExitStack() as ctx:
        s = Space(nc, ctx, f"agg{layer}")
        ring = g.ring
        now = [s.sb(f"now{i}", [P, half], I32) for i in range(2)]
        oh = [s.sb(f"oh{k}", [P, P]) for k in range(2)]
        msg = s.sb("msg", [P, 4, R])
        own, res = s.sb("own", [P, ROW]), s.sb("res", [P, 3, D])
        y, inv = s.sb("y", [P, R]), s.sb("inv", [P, H])
        bias = s.sb("bias", [P, D])
        zero = s.sb("zero", [P, P])
        acc = s.ps("acc", (P, 2, 512))
        yh = y[:, :].rearrange("p (h f) -> p h f", h=H)
        came = [s.pool_sem(f"came{k}") for k in range(RING)]
        picked, gate, in_order, freed, summed, read, loaded, finished, stored, consts, linked = (
            s.sem(n) for n in ("picked", "gate", "in_order", "freed", "summed", "read", "loaded", "finished", "stored",
                               "consts", "linked"))
        hot, used = ([s.sem(f"{n}{k}") for k in range(2)] for n in ("hot", "used"))
        residuals = [g.x_norm] if layer == 0 else [g.x_mid, g.x_norm, io["x"]]
        n_loads = 1 + len(residuals)
        n_links = 4 + len(residuals) + (layer == 0)

        def bounds(eng, b):
            return (eng.value_load(g.tile_pairs[0:1, bass.ds(b, 1)], min_val=0, max_val=ET // 2 - 1),
                    eng.value_load(g.tile_pairs[0:1, bass.ds(b + 1, 1)], min_val=0, max_val=ET // 2 - 1))

        with s.block() as block:
            @block.gpsimd
            def _(pool):
                with pool.Fori(0, ET // RING) as j:
                    for i in range(2):
                        pool.wait_ge(freed, after(j * half + -(-(i + 1) * half // 2)))
                        pool.tensor_copy(now[i][:, :], g.src_i[:, bass.ds(j * RING + i * half, half)]).then_inc(picked, 1)
                        pool.wait_ge(picked, after(2 * j + i + 1))
                        pool.sem_inc(gate, 1)
                        for k in range(half):
                            pool.indirect_dma_start(
                                out=ring[:, i * half + k, :], out_offset=None, in_=g.hx_rows,
                                in_offset=bass.IndirectOffsetOnAxis(ap=now[i][:, k:k + 1], axis=0)
                            ).then_inc(came[i * half + k], 16)

            @block.scalar
            def _(act):
                with act.Fori(0, ET // RING) as j:
                    for k in range(RING):
                        act.wait_ge(came[k], 16 * (j + 1))
                        act.sem_inc(in_order, 1)

            @block.sync
            def _(sp):
                sp.dma_start(bias[:, :], across(io[f"L0_gnn_bg{layer}"], D)).then_inc(consts, 16)
                with sp.Fori(0, NB) as b:
                    sp.wait_ge(finished, after(b))
                    sp.dma_start(own[:, :], g.hx_rows[bass.ds(b * P, P), :]).then_inc(loaded, 16)
                    for n, src in enumerate(residuals):
                        sp.dma_start(res[:, n, :], src[bass.ds(b * P, P), :]).then_inc(loaded, 16)
                    sp.wait_ge(finished, after(b + 1))
                    sp.dma_start(out_dram[bass.ds(b * P, P), :], y[:, 0:D]).then_inc(stored, 16)
                sp.wait_ge(stored, after(16 * NB))

            @block.vector
            def _(dve):
                dve.memset(zero[:, :], 0.0).then_inc(linked, 1)
                dve.sem_inc(freed, half)
                dve.sem_inc(read, 1)
                dve.wait_ge(consts, after(16))

                def step(p, b, frees=False):
                    for k in range(2):
                        tile = 2 * p + k
                        dve.wait_ge(in_order, after(tile + 1))
                        dve.wait_ge(used[k], after(p + b))
                        row = ring[:, bass.ds(tile % RING, 1), 0:R].rearrange("p a (h f) -> p (a h) f", h=H)
                        weighted = dve.tensor_tensor(
                            msg[:, bass.ds((p + b) % 2 * 2 + k, 1), :].rearrange("p a (h f) -> p (a h) f", h=H), row,
                            g.w_cols[:, bass.ds(tile, 1), 0:H].rearrange("p a h -> p (a h)").unsqueeze(2)
                            .to_broadcast([P, H, F + 1]), ALU.mult)
                        if frees and k:
                            weighted.then_inc(freed, 1)
                        dve.wait_ge(used[k], after(p + b + 1))
                        dve.tensor_scalar(oh[k][:, :], g.count[:, :], at(g.dst_f, tile), at(g.minus_base, b),
                                          ALU.subtract, ALU.is_equal).then_inc(hot[k], 1)

                def sum_block(b, more):
                    first, last = bounds(dve, b)
                    with dve.If(last > first):
                        dve.sem_inc(freed, 1)
                        with dve.If(last > first + 1):
                            with dve.Fori(first + 1, last) as p:
                                step(p, b, frees=True)
                        step(last, b)
                    if more:
                        step(last, b + 1)
                    link = Linked(dve, linked, 1 + n_links * b)
                    dve.wait_ge(loaded, after(16 * n_loads * (b + 1)))
                    base = res[:, 0, :]
                    link(dve.tensor_tensor(base, base, bias[:, :], ALU.add))
                    for n in range(1, len(residuals)):
                        link(dve.tensor_tensor(base, base, res[:, n, :], ALU.add))
                    dve.wait_ge(summed, after(b + 1))
                    dve.wait_ge(stored, after(16 * b))
                    for h in range(H):
                        cols = slice(h * (F + 1), (h + 1) * (F + 1))
                        looped = dve.scalar_tensor_tensor(
                            yh[:, h, :], own[:, cols], g.w_self[:, bass.ds(b, 1), h:h + 1].rearrange("p a f -> p (a f)"),
                            acc[:, bass.ds(b % 2, 1), cols].rearrange("p a f -> p (a f)"), ALU.mult, ALU.add)
                    link(looped)
                    dve.sem_inc(read, 1)
                    link(dve.reciprocal(inv[:, :], yh[:, :, F]))
                    link(dve.tensor_tensor(own[:, 0:D].rearrange("p (h f) -> p h f", h=H), yh[:, :, 0:F],
                                           inv[:, :].unsqueeze(2).to_broadcast([P, H, F]), ALU.mult))
                    link(dve.tensor_tensor(y[:, 0:D], own[:, 0:D], base, ALU.add))
                    if layer == 0:
                        link(dve.tensor_scalar(y[:, 0:D], y[:, 0:D], 0.0, None, ALU.max))
                    dve.sem_inc(finished, 1)

                step(0, 0)
                with dve.Fori(0, NB - 1) as b:
                    sum_block(b, True)
                sum_block(NB - 1, False)

            @block.tensor
            def _(pe):
                for k in range(2):
                    pe.sem_inc(used[k], 1)
                pe.wait_ge(linked, after(1))
                with pe.Fori(0, NB) as b:
                    first, last = bounds(pe, b)
                    pe.wait_ge(read, after(b))
                    sums = at(acc, b % 2)
                    pe.matmul(sums[:, 0:1], zero[:, :], zero[:, 0:1], start=True, stop=False, skip_group_check=True)
                    with pe.Fori(first, last + 1) as p:
                        for k in range(2):
                            pe.wait_ge(hot[k], after(p + b + 1))
                            pe.matmul(sums[:, 0:R], oh[k][:, :], at(msg, (p + b) % 2 * 2 + k), start=False, stop=False,
                                      skip_group_check=True).then_inc(used[k], 1)
                    pe.matmul(sums[:, 0:1], zero[:, :], zero[:, 0:1], start=False, stop=True,
                              skip_group_check=True).then_inc(summed, 1)


def route(nc, g, io):
    with ExitStack() as ctx:
        s = Space(nc, ctx, "rte")
        x = s.sb("x", [P, NB, D])
        gw, gb = s.sb("gw", [P, 2, NE]), s.sb("gb", [P, NE])
        xs = [s.sb(f"xs{i}", [P, D]) for i in range(2)]
        xt = [s.sb(f"xt{i}", [P, 2, P]) for i in range(2)]
        cube = lambda n: s.sb(n, [P, NB, NE])
        logits, hot, number, work, before = (cube(n) for n in ("logits", "hot", "number", "work", "before"))
        top, choice, place, kept_f = (s.sb(n, [P, NB]) for n in ("top", "choice", "place", "kept_f"))
        zero = s.sb("zero", [P, NB])
        norm = Norm(s)
        turned = [s.ps(f"turned{i}") for i in range(2)]
        lg = [s.ps(f"lg{i}") for i in range(2)]
        sums = s.ps("sums")
        loaded, linked, link2, numbered, shifted, expd, hotted, cumulated, placed = (
            s.sem(n) for n in ("loaded", "linked", "link2", "numbered", "shifted", "expd", "hotted", "cumulated",
                               "placed"))
        sent = s.pool_sem("sent")
        fed, t_done, t_copied, m_done, m_read, kept = ([s.sem(f"{n}{i}") for i in range(2)] for n in (
            "fed", "t_done", "t_copied", "m_done", "m_read", "kept"))
        flat = lambda c: c[:, :, :].rearrange("p b e -> p (b e)")
        with s.block() as block:
            @block.sync
            def _(sp):
                sp.dma_start(x[:, :, :], g.x_gnn.rearrange("(b p) d -> p b d", p=P)).then_inc(loaded, 16)
                sp.dma_start(gw[:, :, :], io["L0_ffn_gate_w"].rearrange("(p k) e -> p k e", p=P)).then_inc(loaded, 16)
                sp.dma_start(gb[:, :], across(io["L0_ffn_gate_b"], NE)).then_inc(loaded, 16)

            @block.gpsimd
            def _(pool):
                pool.iota(number[:, :, :], pattern=[[0, NB], [1, NE]], base=0, channel_multiplier=0,
                          allow_small_or_imprecise_dtypes=True).then_inc(numbered, 1)
                pool.wait_ge(placed, after(1))
                for b in range(NB):
                    pool.indirect_dma_start(
                        out=g.expert_in, out_offset=bass.IndirectOffsetOnAxis(ap=g.slot_in[:, b:b + 1], axis=0),
                        in_=x[:, b, :], in_offset=None, bounds_check=NE * SLOTS - 1, oob_is_err=False).then_inc(sent, 16)
                pool.wait_ge(sent, 16 * NB)

            @block.vector
            def _(dve):
                dve.wait_ge(loaded, after(48))
                norm.on_vector(dve, linked, x)
                link = Linked(dve, link2)

                def body(blocks):
                    for b, i, j in blocks:
                        dve.wait_ge(t_done[i], after(j))
                        dve.wait_ge(kept[i], after(j))
                        norm.block(dve, xs[i][:, :], x, b).then_inc(fed[i], 1)
                    for b, i, j in blocks:
                        dve.wait_ge(m_done[i], after(j + 1))
                        dve.tensor_tensor(at(logits, b), lg[i][:, 0:NE], gb[:, :], ALU.add).then_inc(m_read[i], 1)
                pairs(dve, body)
                wide = lambda t: t[:, :].unsqueeze(2).to_broadcast([P, NB, NE])
                dve.wait_ge(m_read[0], after(-(-NB // 2)))
                dve.wait_ge(m_read[1], after(NB // 2))
                dve.wait_ge(numbered, after(1))
                link(dve.tensor_reduce(top[:, :], logits[:, :, :], AX, ALU.max))
                link(dve.tensor_tensor(work[:, :, :], logits[:, :, :], wide(top), ALU.subtract))
                dve.sem_inc(shifted, 1)
                link(dve.tensor_tensor(hot[:, :, :], logits[:, :, :], wide(top), ALU.is_lt))
                link(dve.scalar_tensor_tensor(hot[:, :, :], hot[:, :, :], float(NE), number[:, :, :], ALU.mult, ALU.add))
                link(dve.tensor_reduce(choice[:, :], hot[:, :, :], AX, ALU.min))
                link(dve.tensor_tensor(hot[:, :, :], number[:, :, :], wide(choice), ALU.is_equal))
                dve.sem_inc(hotted, 1)
                dve.wait_ge(expd, after(1))
                link(dve.tensor_reduce(top[:, :], work[:, :, :], AX, ALU.add))
                link(dve.reciprocal(top[:, :], top[:, :]))
                dve.wait_ge(cumulated, after(1))
                W = NB * NE
                link(dve.tensor_copy(flat(work), sums[:, 256:256 + W]))
                link(dve.memset(zero[:, :], 0.0))
                for e in range(NE):
                    link(dve.tensor_tensor_scan(before[:, :, e], work[:, :, e], zero[:, :], 0.0, ALU.add, ALU.add))
                link(dve.tensor_tensor(before[:, :, :], before[:, :, :], work[:, :, :], ALU.subtract))
                link(dve.tensor_tensor(flat(before), flat(before), sums[:, 0:W], ALU.add))
                link(dve.tensor_tensor(before[:, :, :], before[:, :, :], hot[:, :, :], ALU.mult))
                link(dve.tensor_reduce(place[:, :], before[:, :, :], AX, ALU.add))
                link(dve.tensor_scalar(place[:, :], place[:, :], -1.0, None, ALU.add))
                link(dve.tensor_scalar(kept_f[:, :], place[:, :], float(CAP), None, ALU.is_lt))
                link(dve.tensor_tensor(g.share[:, :], top[:, :], kept_f[:, :], ALU.mult))
                link(dve.tensor_scalar(place[:, :], place[:, :], float(CAP - 1), None, ALU.min))
                link(dve.scalar_tensor_tensor(place[:, :], choice[:, :], float(SLOTS), place[:, :], ALU.mult, ALU.add))
                link(dve.tensor_copy(g.slot_out[:, :], place[:, :]))
                link(dve.tensor_scalar(kept_f[:, :], kept_f[:, :], -1.0, float(-NE * SLOTS), ALU.add, ALU.mult))
                link(dve.tensor_tensor(place[:, :], place[:, :], kept_f[:, :], ALU.add))
                link(dve.tensor_copy(g.slot_in[:, :], place[:, :]))
                dve.wait_ge(kept[0], after(-(-NB // 2)))
                dve.wait_ge(kept[1], after(NB // 2))
                dve.sem_inc(placed, 1)

            @block.scalar
            def _(act):
                norm.on_scalar(act)

                def body(blocks):
                    for b, i, j in blocks:
                        act.wait_ge(t_done[i], after(j + 1))
                        act.wait_ge(m_done[i], after(j))
                        act.activation(xt[i][:, :, :].rearrange("p k n -> p (k n)"), turned[i][:, 0:2 * P],
                                       ACT.Copy).then_inc(t_copied[i], 1)
                    for b, i, j in blocks:
                        act.activation(at(x, b), xs[i][:, :], ACT.Copy).then_inc(kept[i], 1)
                pairs(act, body)
                act.wait_ge(shifted, after(1))
                act.activation(flat(work), flat(work), ACT.Exp).then_inc(expd, 1)

            @block.tensor
            def _(pe):
                pe.wait_ge(loaded, after(48))

                def body(blocks):
                    for b, i, j in blocks:
                        pe.wait_ge(fed[i], after(j + 1))
                        pe.wait_ge(t_copied[i], after(j))
                        for k in range(2):
                            mm = pe.transpose(turned[i][:, k * P:(k + 1) * P], xs[i][:, k:D:2], g.ident[:, :])
                        mm.then_inc(t_done[i], 1)
                    for b, i, j in blocks:
                        pe.wait_ge(t_copied[i], after(j + 1))
                        pe.wait_ge(m_read[i], after(j))
                        for k in range(2):
                            mm = pe.matmul(lg[i][:, 0:NE], xt[i][:, k, :], gw[:, k, :], start=(k == 0), stop=(k == 1))
                        mm.then_inc(m_done[i], 1)
                pairs(pe, body)
                pe.wait_ge(hotted, after(1))
                W = NB * NE
                pe.matmul(sums[:, 0:W], g.tri_upto[:, :], flat(hot), start=True, stop=True)
                pe.matmul(sums[:, 256:256 + W], g.ones[:, :], flat(hot), start=True, stop=True).then_inc(cumulated, 1)


def experts(nc, g, io):
    KF = FF // P
    Q = SLOTS // P
    with ExitStack() as ctx:
        s = Space(nc, ctx, "exp")
        w1 = [s.sb(f"w1_{i}", [P, 2, FF]) for i in range(2)]
        w2 = s.sb("w2", [P, KF, D])
        b1, b2 = s.sb("b1", [P, NE, KF]), s.sb("b2", [P, D])
        rows = s.sb("rows", [P, Q, D])
        xt = s.sb("xt", [P, 2, SLOTS])
        hid = [s.sb(f"hid{i}", [P, SLOTS]) for i in range(2)]
        y = s.sb("y", [P, Q, D])
        up = [s.ps(f"up{i}") for i in range(2)]
        turned = [s.ps(f"turned{i}") for i in range(2)]
        down = [s.ps(f"down{q}") for q in range(Q)]
        w1_in = [s.sem(f"w1_in{i}") for i in range(2)]
        w2_in, rows_in, b_in, t_done, t_copied, u_done, act_done, d_chunk, d_read, y_left = (
            s.sem(n) for n in ("w2_in", "rows_in", "b_in", "t_done", "t_copied", "u_done", "act_done", "d_chunk",
                               "d_read", "y_left"))
        y_out = s.pool_sem("y_out")
        w1_d = io["L0_ffn_w1"].rearrange("e (p k) f -> e p k f", p=P)
        w2_d = io["L0_ffn_w2"].rearrange("e (p c) d -> e p c d", p=P)
        in_d = g.expert_in.rearrange("(e q p) d -> e p q d", e=NE, p=P)
        out_d = g.expert_out.rearrange("(e q p) d -> e p q d", e=NE, p=P)
        b2_d = io["L0_ffn_b2"]
        one = lambda ap, e: ap[bass.ds(e, 1)].rearrange("a p k f -> (a p) k f")

        def by_parity(eng, body):
            with eng.Fori(0, NE // 2) as j:
                body(2 * j, 0, j)
                body(2 * j + 1, 1, j)

        with s.block() as block:
            @block.sync
            def _(sp):
                sp.dma_start(b1[:, :, :], io["L0_ffn_b1"].rearrange("e (p c) -> p e c", p=P)).then_inc(b_in, 16)
                sp.wait_ge(b_in, after(16))

                def body(e, i, j):
                    sp.wait_ge(t_done, after(2 * Q * e))
                    sp.dma_start(rows[:, :, :], one(in_d, e)).then_inc(rows_in, 16)
                    sp.wait_ge(u_done, after(KF * e))
                    sp.dma_start(w1[i][:, :, :], one(w1_d, e)).then_inc(w1_in[i], 16)
                    sp.wait_ge(d_chunk, after(KF * e))
                    sp.dma_start(w2[:, :, :], one(w2_d, e)).then_inc(w2_in, 16)
                    sp.wait_ge(d_read, after(Q * e))
                    sp.dma_start(b2[:, :], b2_d[bass.ds(e, 1), :].to_broadcast([P, D])).then_inc(b_in, 16)
                by_parity(sp, body)

            @block.gpsimd
            def _(pool):
                with pool.Fori(0, NE) as e:
                    pool.wait_ge(d_read, after(Q * (e + 1)))
                    pool.dma_start(one(out_d, e), y[:, :, :]).then_inc(y_out, 16)
                    pool.wait_ge(y_out, 16 * (e + 1))
                    pool.sem_inc(y_left, 1)

            @block.vector
            def _(dve):
                with dve.Fori(0, NE) as e:
                    dve.wait_ge(b_in, after(16 * (e + 2)))
                    dve.wait_ge(y_left, after(e))
                    for q in range(Q):
                        dve.wait_ge(d_chunk, after(KF * (e + 1)))
                        dve.tensor_tensor(y[:, q, :], down[q][:, 0:D], b2[:, :], ALU.add).then_inc(d_read, 1)

            @block.scalar
            def _(act):
                act.wait_ge(b_in, after(16))
                with act.Fori(0, NE) as e:
                    act.wait_ge(u_done, after(KF * e + KF))
                    for n in range(2 * Q // 4):
                        act.wait_ge(t_done, after(2 * Q * e + 4 * (n + 1)))
                        act.activation(xt[:, n, :], turned[n][:, :], ACT.Copy).then_inc(t_copied, 1)
                    for c in range(KF):
                        act.wait_ge(u_done, after(KF * e + KF + c + 1))
                        if c >= 2:
                            act.wait_ge(d_chunk, after(KF * e + c - 1))
                        else:
                            act.wait_ge(d_chunk, after(KF * e))
                        act.activation(hid[c % 2][:, :], up[c % 2][:, :], ACT.Relu,
                                       bias=b1[:, bass.ds(e, 1), c:c + 1].rearrange("p a f -> p (a f)")).then_inc(act_done, 1)

            @block.tensor
            def _(pe):
                pe.sem_inc(u_done, KF)

                def body(e, i, j):
                    pe.wait_ge(rows_in, after(16 * (e + 1)))
                    pe.wait_ge(t_copied, after(2 * e))
                    for k in range(2):
                        for q in range(Q):
                            pe.transpose(turned[k][:, q * P:(q + 1) * P], rows[:, q, k:D:2], g.ident[:, :]).then_inc(t_done, 1)

                    def first(c):
                        pe.wait_ge(act_done, after(KF * e + c - 1 if c >= 2 else KF * e))
                        for k in range(2):
                            mm = pe.matmul(up[c % 2][:, :], w1[i][:, k, c:FF:KF], xt[:, k, :], start=(k == 0), stop=(k == 1))
                        mm.then_inc(u_done, 1)

                    pe.wait_ge(t_copied, after(2 * (e + 1)))
                    pe.wait_ge(w1_in[i], after(16 * (j + 1)))
                    first(0)
                    for c in range(KF):
                        if c + 1 < KF:
                            first(c + 1)
                        if c == 0:
                            pe.wait_ge(w2_in, after(16 * (e + 1)))
                            pe.wait_ge(d_read, after(Q * e))
                        pe.wait_ge(act_done, after(KF * e + c + 1))
                        for q in range(Q):
                            mm = pe.matmul(down[q][:, 0:D], hid[c % 2][:, q * P:(q + 1) * P], w2[:, c, :],
                                           start=(c == 0), stop=(c == KF - 1), skip_group_check=True)
                        mm.then_inc(d_chunk, 1)
                by_parity(pe, body)


def combine(nc, g, io):
    PART = 5
    parts = NB // PART
    MAX32 = 3.4028234663852886e38
    with ExitStack() as ctx:
        s = Space(nc, ctx, "cmb")
        y, x, z = ([s.sb(f"{n}{i}", [P, PART, D]) for i in range(2)] for n in ("y", "x", "z"))
        mask = s.sb("mask", [P, PART, D])
        edge = s.sb("edge", [P, 2, D])
        loaded, stored, linked, done = (s.sem(n) for n in ("loaded", "stored", "linked", "done"))
        came_by = [s.pool_sem(f"came{c}") for c in range(parts)]
        view = lambda d, c: d.rearrange("(b p) d -> p b d", p=P)[:, c * PART:(c + 1) * PART, :]
        with s.block() as block:
            @block.sync
            def _(sp):
                for c in range(parts):
                    if c >= 2:
                        sp.wait_ge(stored, after(16 * (c - 1)))
                    if c >= 1:
                        sp.wait_ge(loaded, after(16 * c))
                    sp.dma_start(x[c % 2][:, :, :], view(g.x_gnn, c)).then_inc(loaded, 16)
                    if c >= 1:
                        sp.wait_ge(done, after(c))
                        sp.dma_start(view(g.x_moe, c - 1), x[(c - 1) % 2][:, :, :]).then_inc(stored, 16)
                sp.wait_ge(done, after(parts))
                sp.dma_start(view(g.x_moe, parts - 1), x[(parts - 1) % 2][:, :, :]).then_inc(stored, 16)
                sp.wait_ge(stored, after(16 * parts))

            @block.gpsimd
            def _(pool):
                for c in range(parts):
                    if c >= 2:
                        pool.wait_ge(done, after(c - 1))
                    for b in range(PART):
                        col = c * PART + b
                        pool.indirect_dma_start(
                            out=y[c % 2][:, b, :], out_offset=None, in_=g.expert_out,
                            in_offset=bass.IndirectOffsetOnAxis(ap=g.slot_out[:, col:col + 1], axis=0)
                        ).then_inc(came_by[c], 16)

            @block.vector
            def _(dve):
                link = Linked(dve, linked)
                link(dve.memset(edge[:, 0, :], 1.0e4))
                link(dve.memset(edge[:, 1, :], -1.0e4))
                flat = lambda t: t[:, :, :].rearrange("p b d -> p (b d)")
                for c in range(parts):
                    yc, xc, zc = y[c % 2], x[c % 2], z[c % 2]
                    dve.wait_ge(came_by[c], 16 * PART)
                    link(dve.tensor_tensor(yc[:, :, :], yc[:, :, :],
                                           g.share[:, c * PART:(c + 1) * PART].unsqueeze(2).to_broadcast([P, PART, D]),
                                           ALU.mult))
                    link(dve.memset(zc[:, :, :], 0.0))
                    link(dve.tensor_tensor(mask[:, :, :], yc[:, :, :], yc[:, :, :], ALU.is_equal))
                    link(dve.copy_predicated(flat(zc), flat(mask).bitcast(I32), flat(yc)))
                    for n, (limit, op) in enumerate(((MAX32, ALU.is_gt), (-MAX32, ALU.is_lt))):
                        link(dve.tensor_scalar(mask[:, :, :], yc[:, :, :], limit, None, op))
                        for b in range(PART):
                            link(dve.copy_predicated(zc[:, b, :], mask[:, b, :].bitcast(I32), edge[:, n, :]))
                    dve.wait_ge(loaded, after(16 * (c + 1)))
                    link(dve.tensor_tensor(xc[:, :, :], xc[:, :, :], zc[:, :, :], ALU.add))
                    dve.sem_inc(done, 1)


class Gate:

    def __init__(self, s):
        self.w, self.bias, self.junk = s.sb("w", [P, D]), s.sb("bias", [P, 1]), s.sb("junk", [P, D])
        self.h, self.rest = s.sb("h", [P, D]), s.sb("rest", [P, D])
        self.parts = [s.sb(f"parts{i}", [P, 3, D], BF16) for i in range(2)]
        self.dot, self.gate = s.sb("dot", [P, 2]), s.sb("gate", [P, 2])
        self.given, self.linked = s.sem("given"), s.sem("linked")
        self.dotted, self.gated, self.split, self.added = (
            [s.sem(f"{n}{i}") for i in range(2)] for n in ("dotted", "gated", "split", "added"))

    def load(self, sp, io):
        sp.dma_start(self.w[:, :], across(io["L1_gnn_lin_w"].rearrange("a n -> (a n)"), D)).then_inc(self.given, 16)
        sp.dma_start(self.bias[:, :], across(io["L1_gnn_lin_b"], 1)).then_inc(self.given, 16)

    LINKS = 7

    def on_vector(self, dve, link, i, turn, dis, acc_out, acc_in):
        link(dve.tensor_tensor_reduce(self.junk[:, :], self.h[:, :], self.w[:, :], 1.0, 0.0, ALU.mult, ALU.add,
                                      self.dot[:, i:i + 1]))
        dve.sem_inc(self.dotted[i], 1)
        hi, mid, low = (self.parts[i][:, n, :] for n in range(3))
        link(dve.tensor_scalar(self.rest[:, :], self.h[:, :], dis, None, ALU.mult))
        link(dve.tensor_copy(hi, self.rest[:, :]))
        link(dve.tensor_tensor(self.rest[:, :], self.rest[:, :], hi, ALU.subtract))
        link(dve.tensor_copy(mid, self.rest[:, :]))
        link(dve.tensor_tensor(self.rest[:, :], self.rest[:, :], mid, ALU.subtract))
        dve.tensor_copy(low, self.rest[:, :]).then_inc(self.split[i], 1)
        dve.wait_ge(self.gated[i], after(turn + 1))
        link(dve.scalar_tensor_tensor(acc_out, self.h[:, :], self.gate[:, i:i + 1], acc_in, ALU.mult, ALU.add))
        dve.sem_inc(self.added[i], 1)

    def on_scalar(self, act, i, turn):
        act.wait_ge(self.dotted[i], after(turn + 1))
        act.activation(self.gate[:, i:i + 1], self.dot[:, i:i + 1], ACT.Sigmoid,
                       bias=self.bias[:, 0:1]).then_inc(self.gated[i], 1)


TURNS = (-(-NB // 2), NB // 2)


def hop_parts(g, parity, b):
    return g.hop_parts[bass.ds(parity * NP + b * P, P), :]


def hops_start(nc, g, io):
    with ExitStack() as ctx:
        s = Space(nc, ctx, "hp0")
        x = s.sb("x", [P, NB, D])
        acc = [s.sb(f"acc{i}", [P, D]) for i in range(2)]
        norm, gate = Norm(s), Gate(s)
        loaded, bn = s.sem("loaded"), s.sem("bn")
        kept, saved = ([s.sem(f"{n}{i}") for i in range(2)] for n in ("kept", "saved"))
        with s.block() as block:
            @block.sync
            def _(sp):
                sp.dma_start(x[:, :, :], g.x_moe.rearrange("(b p) d -> p b d", p=P)).then_inc(loaded, 16)
                gate.load(sp, io)

                def body(blocks):
                    for b, i, j in blocks:
                        sp.wait_ge(gate.split[i], after(j + 1))
                        sp.dma_start(hop_parts(g, 0, b), gate.parts[i][:, :, :].rearrange("p n d -> p (n d)")
                                     ).then_inc(kept[i], 16)
                        sp.wait_ge(gate.added[i], after(j + 1))
                        sp.dma_start(g.x_gcn[bass.ds(b * P, P), :], acc[i][:, :]).then_inc(saved[i], 16)
                pairs(sp, body)
                for i in range(2):
                    sp.wait_ge(kept[i], after(16 * TURNS[i]))
                    sp.wait_ge(saved[i], after(16 * TURNS[i]))

            @block.vector
            def _(dve):
                dve.wait_ge(loaded, after(16))
                norm.on_vector(dve, bn, x)
                dve.wait_ge(gate.given, after(32))

                def body(blocks):
                    for b, i, j in blocks:
                        link = Linked(dve, gate.linked, (Gate.LINKS + 1) * b)
                        dve.wait_ge(kept[i], after(16 * j))
                        dve.wait_ge(saved[i], after(16 * j))
                        link(norm.block(dve, gate.h[:, :], x, b))
                        gate.on_vector(dve, link, i, j, at(g.dis, b), acc[i][:, :], at(x, b))
                pairs(dve, body)

            @block.scalar
            def _(act):
                norm.on_scalar(act)
                act.wait_ge(gate.given, after(32))
                pairs(act, lambda blocks: [gate.on_scalar(act, i, j) for b, i, j in blocks])


def hops(nc, g, io):
    CHUNK = 5
    with ExitStack() as ctx:
        s = Space(nc, ctx, "hop")
        hs = s.sb("hs", [P, NB, 3 * D], BF16)
        acc = [s.sb(f"acc{i}", [P, D]) for i in range(2)]
        gate = Gate(s)
        wide, narrow = ([s.ps(f"{n}{i}") for i in range(2)] for n in ("wide", "narrow"))
        here, passed = [s.sem(f"here{c}") for c in range(NB // CHUNK)], s.sem("passed")
        kept, saved, came, summed, read = ([s.sem(f"{n}{i}") for i in range(2)] for n in (
            "kept", "saved", "came", "summed", "read"))
        with s.block() as block:
            @block.sync
            def _(sp):
                gate.load(sp, io)
                with sp.Fori(0, HOPS) as k:
                    for i in range(2):
                        for done, count in ((kept[i], 16 * TURNS[i] * k), (saved[i], 16 * TURNS[i] * k),
                                            (summed[i], TURNS[i] * k)):
                            sp.wait_ge(done, after(count))
                            sp.sem_inc(passed, 1)
                    for c in range(NB // CHUNK):
                        sp.dma_start(hs[:, c * CHUNK:(c + 1) * CHUNK, :],
                                     g.hop_parts[bass.ds((k % 2) * NP + c * CHUNK * P, CHUNK * P), :].rearrange(
                                         "(b p) d -> p b d", p=P)).then_inc(here[c], 16)

                    def body(blocks):
                        for b, i, j in blocks:
                            turn = k * TURNS[i] + j
                            sp.wait_ge(saved[i], after(16 * turn))
                            sp.dma_start(acc[i][:, :], g.x_gcn[bass.ds(b * P, P), :]).then_inc(came[i], 16)
                        for b, i, j in blocks:
                            turn = k * TURNS[i] + j
                            sp.wait_ge(gate.split[i], after(turn + 1))
                            sp.dma_start(hop_parts(g, (k + 1) % 2, b),
                                         gate.parts[i][:, :, :].rearrange("p n d -> p (n d)")).then_inc(kept[i], 16)
                            sp.wait_ge(gate.added[i], after(turn + 1))
                            sp.dma_start(g.x_gcn[bass.ds(b * P, P), :], acc[i][:, :]).then_inc(saved[i], 16)
                    pairs(sp, body)
                for i in range(2):
                    sp.wait_ge(kept[i], after(16 * TURNS[i] * HOPS))
                    sp.wait_ge(saved[i], after(16 * TURNS[i] * HOPS))

            @block.vector
            def _(dve):
                dve.wait_ge(gate.given, after(32))
                with dve.Fori(0, HOPS) as k:
                    def body(blocks):
                        for b, i, j in blocks:
                            turn = k * TURNS[i] + j
                            link = Linked(dve, gate.linked, (Gate.LINKS + 3) * (k * NB + b))
                            dis = at(g.dis, b)
                            dve.wait_ge(summed[i], after(turn + 1))
                            link(dve.tensor_scalar(gate.h[:, :], narrow[i][:, 0:D], dis, None, ALU.mult))
                            for n in (1, 0):
                                link(dve.scalar_tensor_tensor(gate.h[:, :], wide[i][:, n * D:(n + 1) * D], dis,
                                                              gate.h[:, :], ALU.mult, ALU.add))
                            dve.sem_inc(read[i], 1)
                            dve.wait_ge(kept[i], after(16 * turn))
                            dve.wait_ge(came[i], after(16 * (turn + 1)))
                            gate.on_vector(dve, link, i, turn, dis, acc[i][:, :], acc[i][:, :])
                    pairs(dve, body)

            @block.scalar
            def _(act):
                act.wait_ge(gate.given, after(32))
                with act.Fori(0, HOPS) as k:
                    pairs(act, lambda blocks: [gate.on_scalar(act, i, k * TURNS[i] + j) for b, i, j in blocks])

            @block.tensor
            def _(pe):
                with pe.Fori(0, HOPS) as k:
                    def body(blocks):
                        for b, i, j in blocks:
                            pe.wait_ge(read[i], after(k * TURNS[i] + j))
                            for t in range(NB):
                                if t % CHUNK == 0:
                                    pe.wait_ge(here[t // CHUNK], after(16 * (k + 1)))
                                count = g.counts[:, t, bass.ds(b * P, P)]
                                pe.matmul(wide[i][:, :], count, hs[:, t, 0:2 * D], start=(t == 0), stop=(t == NB - 1))
                                mm = pe.matmul(narrow[i][:, 0:D], count, hs[:, t, 2 * D:3 * D], start=(t == 0),
                                               stop=(t == NB - 1))
                            mm.then_inc(summed[i], 1)
                    pairs(pe, body)


def slice_weights(nc, g, a, io):
    HW = SH * SD
    with ExitStack() as ctx:
        s = Space(nc, ctx, "swt")
        wx, wxt = s.sb("wx", [P, 2, HW]), s.sb("wxt", [P, 2, 4, P])
        wsl = s.sb("wsl", [P, SG])
        bx, bxw = s.sb("bx", [SD, SH]), s.sb("bxw", [SD, SH, P])
        bsl, inv_t = s.sb("bsl", [P, SG]), s.sb("inv_t", [P, SH])
        turn = [s.ps(f"turn{k}") for k in range(2)]
        both = [s.ps(f"both{o}") for o in range(2)]
        bias_ps = s.ps("bias_ps")
        loaded, linked, turned, copied, ready, folded = (
            s.sem(n) for n in ("loaded", "linked", "turned", "copied", "ready", "folded"))
        nm = lambda n: io[f"L1_ffn_{n}"]
        with s.block() as block:
            @block.sync
            def _(sp):
                sp.dma_start(a.x[:, :, :], g.x_gcn.rearrange("(b p) d -> p b d", p=P)).then_inc(loaded, 16)
                sp.dma_start(wx[:, :, :], nm("W_x").rearrange("(p k) n -> p k n", p=P)).then_inc(loaded, 16)
                for o in range(2):
                    sp.dma_start(wsl[o * SD:(o + 1) * SD, :], nm("W_slice")).then_inc(loaded, 16)
                with nc.allow_non_contiguous_dma(reason="512 numbers"):
                    sp.dma_start(bx[:, :], nm("b_x").rearrange("(h d) -> d h", h=SH)).then_inc(loaded, 16)
                sp.dma_start(bsl[:, :], across(nm("b_slice"), SG)).then_inc(loaded, 16)
                sp.dma_start(inv_t[:, :], across(nm("temperature").rearrange("a h b c -> (a h b c)"), SH)).then_inc(loaded, 16)

            @block.gpsimd
            def _(pool):
                pool.iota(a.valid[:, :], pattern=[[P, NB]], base=0, channel_multiplier=1,
                          allow_small_or_imprecise_dtypes=True).then_inc(ready, 1)

            @block.vector
            def _(dve):
                link = Linked(dve, linked)
                dve.wait_ge(loaded, after(16 * 7))
                dve.wait_ge(ready, after(1))
                link(dve.tensor_scalar(a.valid[:, :], a.valid[:, :], float(N), None, ALU.is_lt))
                link(dve.tensor_scalar(inv_t[:, :], inv_t[:, :], 0.1, 5.0, ALU.max, ALU.min))
                link(dve.reciprocal(inv_t[:, :], inv_t[:, :]))
                link(dve.tensor_copy(bxw[:, :, :], bx[:, :].unsqueeze(2).to_broadcast([SD, SH, P])))
                dve.sem_inc(ready, 1)
                dve.wait_ge(turned, after(2))
                for k in range(2):
                    link(dve.tensor_copy(wxt[:, k, :, :].rearrange("p m n -> p (m n)"), turn[k][:, :]))
                dve.sem_inc(copied, 1)
                dve.wait_ge(folded, after(1))
                for o in range(2):
                    for k in range(2):
                        link(dve.tensor_tensor(
                            a.wxs[:, k, :].rearrange("p (m o s) -> p m o s", o=2, s=SG)[:, :, o, :],
                            both[o][:, k * 256:(k + 1) * 256].rearrange("p (m s) -> p m s", s=SG),
                            inv_t[:, o:SH:2].unsqueeze(2).to_broadcast([P, 4, SG]), ALU.mult))
                heads = lambda t: t.rearrange("p (h s) -> p h s", h=SH)
                link(dve.tensor_tensor(heads(a.bias[:, :]), heads(bias_ps[:, :]),
                                       bsl[:, :].unsqueeze(1).to_broadcast([P, SH, SG]), ALU.add))
                link(dve.tensor_tensor(heads(a.bias[:, :]), heads(a.bias[:, :]),
                                       inv_t[:, :].unsqueeze(2).to_broadcast([P, SH, SG]), ALU.mult))

            @block.tensor
            def _(pe):
                pe.wait_ge(loaded, after(16 * 7))
                for k in range(2):
                    for m in range(4):
                        mm = pe.transpose(turn[k][:, m * P:(m + 1) * P], wx[:, k, m * P:(m + 1) * P], g.ident[:, :])
                    mm.then_inc(turned, 1)
                pe.wait_ge(ready, after(2))
                for h in range(SH):
                    pe.matmul(bias_ps[:, h * SG:(h + 1) * SG], bxw[:, h, :], wsl[0:SD, :], start=True, stop=True)
                pe.wait_ge(copied, after(1))
                for o in range(2):
                    half = slice(o * SD, (o + 1) * SD)
                    for k in range(2):
                        for m in range(4):
                            c = (k * 4 + m) * SG
                            mm = pe.matmul(both[o][:, c:c + SG], wxt[half, k, m, :], wsl[half, :], start=True, stop=True)
                mm.then_inc(folded, 1)


def slice_tokens(nc, g, a, io):
    HW = SH * SG
    with ExitStack() as ctx:
        s = Space(nc, ctx, "tok")
        xs = [s.sb(f"xs{i}", [P, D + 1]) for i in range(2)]
        xt = [s.sb(f"xt{i}", [P, 2, P]) for i in range(2)]
        sw = [s.sb(f"sw{i}", [P, HW]) for i in range(2)]
        peak, total = s.sb("peak", [P, SH]), s.sb("total", [P, SH])
        zero = s.sb("zero", [P, P])
        norm = Norm(s)
        turned, flipped = s.ps("turned"), s.ps("flipped")
        lg = [s.ps(f"lg{i}") for i in range(2)]
        tok = [s.ps(f"tok{m}") for m in range(4)]
        bn, linked, summed, zeroed = s.sem("bn"), s.sem("linked"), s.sem("summed"), s.sem("zeroed")
        fed, t_done, t_copied, m_done, m_read, shifted, expd, soft, tok_done = (
            [s.sem(f"{n}{i}") for i in range(2)] for n in (
                "fed", "t_done", "t_copied", "m_done", "m_read", "shifted", "expd", "soft", "tok_done"))
        f_done, f_copied = s.sem("f_done"), s.sem("f_copied")
        heads = lambda t: t.rearrange("p (h s) -> p h s", h=SH)
        wide = lambda t: t[:, :].unsqueeze(2).to_broadcast([P, SH, SG])
        with s.block() as block:
            @block.vector
            def _(dve):
                norm.on_vector(dve, bn, a.x)
                dve.tensor_tensor(norm.rstd[:, :], norm.rstd[:, :], a.valid[:, :], ALU.mult).then_inc(zeroed, 1)
                dve.memset(zero[:, :], 0.0).then_inc(zeroed, 1)
                dve.wait_ge(zeroed, after(2))

                def body(blocks):
                    for b, i, j in blocks:
                        dve.wait_ge(tok_done[i], after(j))
                        dve.tensor_copy(xs[i][:, D:D + 1], at(a.valid, b))
                        norm.block(dve, xs[i][:, 0:D], a.x, b).then_inc(fed[i], 1)
                    for b, i, j in blocks:
                        link = Linked(dve, linked, 6 * b)
                        w = heads(sw[i][:, :])
                        dve.wait_ge(m_done[i], after(j + 1))
                        link(dve.tensor_tensor(sw[i][:, :], lg[i][:, :], a.bias[:, :], ALU.add))
                        dve.sem_inc(m_read[i], 1)
                        link(dve.tensor_reduce(peak[:, :], w, AX, ALU.max))
                        link(dve.tensor_tensor(w, w, wide(peak), ALU.subtract))
                        dve.sem_inc(shifted[i], 1)
                        dve.wait_ge(expd[i], after(j + 1))
                        link(dve.tensor_reduce(total[:, :], w, AX, ALU.add))
                        link(dve.reciprocal(total[:, :], total[:, :]))
                        link(dve.tensor_tensor(w, w, wide(total), ALU.mult))
                        dve.sem_inc(soft[i], 1)
                pairs(dve, body)
                dve.wait_ge(summed, after(1))
                for m in range(4):
                    dve.tensor_copy(a.tok[:, m, 0:D + 1], tok[m][:, 0:D + 1])

            @block.scalar
            def _(act):
                norm.on_scalar(act)

                def body(blocks):
                    for b, i, j in blocks:
                        act.wait_ge(t_done[i], after(j + 1))
                        act.wait_ge(m_done[i], after(j))
                        act.activation(xt[i][:, :, :].rearrange("p k n -> p (k n)"),
                                       turned[:, i * D:(i + 1) * D], ACT.Copy).then_inc(t_copied[i], 1)
                    for b, i, j in blocks:
                        act.wait_ge(shifted[i], after(j + 1))
                        act.activation(sw[i][:, :], sw[i][:, :], ACT.Exp).then_inc(expd[i], 1)
                    for b, i, j in blocks:
                        act.wait_ge(f_done, after(b + 1))
                        act.activation(at(a.swt, b), flipped[:, :], ACT.Copy).then_inc(f_copied, 1)
                pairs(act, body)

            @block.tensor
            def _(pe):
                pe.wait_ge(zeroed, after(2))
                for m in range(4):
                    pe.matmul(tok[m][:, 0:D + 1], zero[:, :], a.x[:, 0:2, :].rearrange("p b d -> p (b d)")[:, 0:D + 1],
                              start=True, stop=False, skip_group_check=True)

                def body(blocks):
                    for b, i, j in blocks:
                        pe.wait_ge(fed[i], after(j + 1))
                        pe.wait_ge(t_copied[1 - i], after(j + i))
                        for k in range(2):
                            mm = pe.transpose(turned[:, i * D + k * P:i * D + (k + 1) * P], xs[i][:, k:D:2], g.ident[:, :])
                        mm.then_inc(t_done[i], 1)
                    for b, i, j in blocks:
                        pe.wait_ge(t_copied[i], after(j + 1))
                        pe.wait_ge(m_read[i], after(j))
                        for k in range(2):
                            mm = pe.matmul(lg[i][:, :], xt[i][:, k, :], a.wxs[:, k, :], start=(k == 0), stop=(k == 1))
                        mm.then_inc(m_done[i], 1)
                    for b, i, j in blocks:
                        pe.wait_ge(soft[i], after(j + 1))
                        pe.wait_ge(f_copied, after(b))
                        for m in range(4):
                            mm = pe.transpose(flipped[:, m * P:(m + 1) * P], sw[i][:, m * P:(m + 1) * P], g.ident[:, :])
                        mm.then_inc(f_done, 1)
                        for m in range(4):
                            mm = pe.matmul(tok[m][:, 0:D + 1], sw[i][:, m * P:(m + 1) * P], xs[i][:, :], start=False,
                                           stop=False, skip_group_check=True)
                        mm.then_inc(tok_done[i], 1)
                pairs(pe, body)
                for m in range(4):
                    mm = pe.matmul(tok[m][:, 0:P], zero[:, :], zero[:, :], start=False, stop=True, skip_group_check=True)
                mm.then_inc(summed, 1)


def slice_attention(nc, g, a, io):
    with ExitStack() as ctx:
        s = Space(nc, ctx, "att")
        HW = SH * SD
        wfx, bfx = s.sb("wfx", [P, 2, HW]), s.sb("bfx", [1, HW])
        wq, wk, wv = (s.sb(n, [SD, SD]) for n in ("wq", "wk", "wv"))
        wo = s.sb("wo", [SD, SH, D])
        inv = s.sb("inv", [P, 4])
        tokt, normt = s.sb("tokt", [P, 2, 4 * P]), s.sb("normt", [1, 4 * P])
        st, qt, kt, v, at_, att, ot = (s.sb(n, [SD, SH, SG]) for n in ("st", "qt", "kt", "v", "at", "att", "ot"))
        peak = s.sb("peak", [SG, SH])
        A, B, C, Dd = (s.ps(n) for n in "ABCD")
        O = [s.ps(f"O{m}") for m in range(4)]
        loaded, linked, vec, ten, expd = (s.sem(n) for n in ("loaded", "linked", "vec", "ten", "expd"))
        nm = lambda n: io[f"L1_ffn_{n}"]
        fl = lambda t: t[:, :, :].rearrange("p h g -> p (h g)")
        wide = lambda t: t[:, :].unsqueeze(2).to_broadcast([SG, SH, SG])
        with s.block() as block:
            @block.sync
            def _(sp):
                sp.dma_start(wfx[:, :, :], nm("W_fx").rearrange("(k p) n -> p k n", p=P)).then_inc(loaded, 16)
                sp.dma_start(bfx[:, :], nm("b_fx").rearrange("(a n) -> a n", a=1)).then_inc(loaded, 16)
                for w, n in ((wq, "W_q"), (wk, "W_k"), (wv, "W_v")):
                    sp.dma_start(w[:, :], nm(n)).then_inc(loaded, 16)
                sp.dma_start(wo[:, :, :], nm("W_out").rearrange("(h c) d -> c h d", h=SH)).then_inc(loaded, 16)

            @block.vector
            def _(dve):
                link = Linked(dve, linked)
                link(dve.tensor_scalar(inv[:, :], a.tok[:, :, D], 1e-5, None, ALU.add))
                link(dve.reciprocal(inv[:, :], inv[:, :]))
                link(dve.tensor_tensor(a.tok[:, :, 0:D + 1], a.tok[:, :, 0:D + 1],
                                       inv[:, :].unsqueeze(2).to_broadcast([P, 4, D + 1]), ALU.mult))
                dve.sem_inc(vec, 1)
                dve.wait_ge(ten, after(1))
                for k, src in enumerate((A, B)):
                    link(dve.tensor_copy(tokt[:, k, :], src[:, :]))
                link(dve.tensor_copy(normt[:, :], C[0:1, :]))
                dve.sem_inc(vec, 1)
                dve.wait_ge(ten, after(2))
                for h in range(SH):
                    m, o = h // 2, h % 2
                    link(dve.tensor_copy(st[:, h, :], Dd[o * SD:(o + 1) * SD, m * P + o * SG:m * P + (o + 1) * SG]))
                dve.sem_inc(vec, 1)
                dve.wait_ge(ten, after(3))
                for dst, src in ((qt, A), (kt, B), (v, C)):
                    link(dve.tensor_copy(fl(dst), src[0:SD, :]))
                dve.sem_inc(vec, 1)
                dve.wait_ge(ten, after(4))
                link(dve.tensor_copy(fl(at_), Dd[0:SD, :]))
                link(dve.tensor_reduce(peak[:, :], at_[:, :, :], AX, ALU.max))
                link(dve.tensor_tensor(at_[:, :, :], at_[:, :, :], wide(peak), ALU.subtract))
                dve.sem_inc(vec, 1)
                dve.wait_ge(expd, after(1))
                link(dve.tensor_reduce(peak[:, :], at_[:, :, :], AX, ALU.add))
                link(dve.reciprocal(peak[:, :], peak[:, :]))
                link(dve.tensor_tensor(at_[:, :, :], at_[:, :, :], wide(peak), ALU.mult))
                dve.sem_inc(vec, 1)
                dve.wait_ge(ten, after(5))
                link(dve.tensor_copy(fl(att), A[0:SD, :]))
                dve.sem_inc(vec, 1)
                dve.wait_ge(ten, after(6))
                link(dve.tensor_copy(fl(ot), B[0:SD, :]))
                dve.sem_inc(vec, 1)
                dve.wait_ge(ten, after(7))
                for h in range(SH):
                    m, o = h // 2, h % 2
                    link(dve.tensor_copy(a.v2[o * SG:(o + 1) * SG, m, :], O[m][0:SG, o * D:(o + 1) * D]))

            @block.scalar
            def _(act):
                act.wait_ge(vec, after(5))
                act.activation(fl(at_), fl(at_), ACT.Exp, scale=float(SD) ** -0.5).then_inc(expd, 1)

            @block.tensor
            def _(pe):
                pe.wait_ge(loaded, after(16 * 6))
                pe.wait_ge(vec, after(1))
                for m in range(4):
                    for k, dst in enumerate((A, B)):
                        pe.transpose(dst[:, m * P:(m + 1) * P], a.tok[:, m, k * P:(k + 1) * P], g.ident[:, :])
                    mm = pe.transpose(C[0:1, m * P:(m + 1) * P], a.tok[:, m, D:D + 1], g.ident[:, :])
                mm.then_inc(ten, 1)
                pe.wait_ge(vec, after(2))
                for m in range(4):
                    cols = slice(m * P, (m + 1) * P)
                    for k in range(2):
                        pe.matmul(Dd[:, cols], wfx[:, k, cols], tokt[:, k, cols], start=(k == 0), stop=False)
                    mm = pe.matmul(Dd[:, cols], bfx[0:1, cols], normt[0:1, cols], start=False, stop=True)
                mm.then_inc(ten, 1)
                pe.wait_ge(vec, after(3))
                pe.matmul(A[0:SD, :], wq[:, :], fl(st), start=True, stop=True)
                pe.matmul(B[0:SD, :], wk[:, :], fl(st), start=True, stop=True)
                each = lambda dst, lhs, rhs: [pe.matmul(dst[0:SD, h * SG:(h + 1) * SG], lhs(h), rhs(h), start=True,
                                                        stop=True) for h in range(SH)][-1]
                each(C, lambda h: st[:, h, :], lambda h: wv[:, :]).then_inc(ten, 1)
                pe.wait_ge(vec, after(4))
                each(Dd, lambda h: qt[:, h, :], lambda h: kt[:, h, :]).then_inc(ten, 1)
                pe.wait_ge(vec, after(6))
                for h in range(SH):
                    mm = pe.transpose(A[0:SD, h * SG:(h + 1) * SG], at_[:, h, :], g.ident[0:SG, 0:SG])
                mm.then_inc(ten, 1)
                pe.wait_ge(vec, after(7))
                each(B, lambda h: v[:, h, :], lambda h: att[:, h, :]).then_inc(ten, 1)
                pe.wait_ge(vec, after(8))
                for h in range(SH):
                    m, o = h // 2, h % 2
                    mm = pe.matmul(O[m][0:SG, o * D:(o + 1) * D], ot[:, h, :], wo[:, h, :], start=True, stop=True)
                mm.then_inc(ten, 1)


def slice_output(nc, g, a, io, out):
    with ExitStack() as ctx:
        s = Space(nc, ctx, "out")
        now = [s.sb(f"now{i}", [P, SH * SG]) for i in range(2)]
        y = [s.sb(f"y{i}", [P, D]) for i in range(2)]
        bias = s.sb("bias", [P, D])
        acc = [s.ps(f"acc{i}") for i in range(2)]
        loaded, linked = s.sem("loaded"), s.sem("linked")
        copied, done, made, stored = ([s.sem(f"{n}{i}") for i in range(2)] for n in ("copied", "done", "made", "stored"))
        with s.block() as block:
            @block.sync
            def _(sp):
                sp.dma_start(bias[:, :], across(io["L1_ffn_b_out"], D)).then_inc(loaded, 16)

                def body(blocks):
                    for b, i, j in blocks:
                        sp.wait_ge(made[i], after(j + 1))
                        sp.dma_start(out[bass.ds(b * P, P), :], y[i][:, :]).then_inc(stored[i], 16)
                pairs(sp, body)
                for i in range(2):
                    sp.wait_ge(stored[i], after(16 * TURNS[i]))

            @block.scalar
            def _(act):
                def body(blocks):
                    for b, i, j in blocks:
                        act.wait_ge(done[i], after(j))
                        act.activation(now[i][:, :], at(a.swt, b), ACT.Copy).then_inc(copied[i], 1)
                pairs(act, body)

            @block.tensor
            def _(pe):
                def body(blocks):
                    for b, i, j in blocks:
                        pe.wait_ge(copied[i], after(j + 1))
                        pe.wait_ge(made[i], after(j))
                        for m in range(4):
                            mm = pe.matmul(acc[i][:, 0:D], now[i][:, m * P:(m + 1) * P], a.v2[:, m, :], start=(m == 0),
                                           stop=(m == 3))
                        mm.then_inc(done[i], 1)
                pairs(pe, body)

            @block.vector
            def _(dve):
                dve.wait_ge(loaded, after(16))

                def body(blocks):
                    for b, i, j in blocks:
                        link = Linked(dve, linked, b)
                        dve.wait_ge(done[i], after(j + 1))
                        dve.wait_ge(stored[i], after(16 * j))
                        link(dve.tensor_tensor(y[i][:, :], acc[i][:, 0:D], bias[:, :], ALU.add))
                        dve.tensor_tensor(y[i][:, :], y[i][:, :], at(a.x, b), ALU.add).then_inc(made[i], 1)
                pairs(dve, body)


def main_program(nc, io, out):
    with ExitStack() as whole:
        g = Space(nc, whole, "all")
        dram = lambda name, shape, dt=F32: nc.dram_tensor(name, shape, dt, kind="Internal").ap()
        g.edge_fill, g.edge_scan, g.edge_w = dram("edge_fill", [EP, SW]), dram("edge_scan", [EP, SW]), dram("edge_w", [EP * 4])
        g.edge_terms = dram("edge_terms", [P, sum(HEADS), ET])
        g.hx_rows, g.small = dram("hx_rows", [NP, ROW]), dram("small", [NP, SW])
        g.expert_in, g.expert_out = dram("expert_in", [NE * SLOTS, D]), dram("expert_out", [NE * SLOTS, D])
        g.x_norm, g.x_mid, g.x_gnn, g.x_moe, g.x_gcn = (
            dram(n, [NP, D]) for n in ("x_norm", "x_mid", "x_gnn", "x_moe", "x_gcn"))
        g.hop_parts = dram("hop_parts", [2 * NP, 3 * D], BF16)
        g.ident, g.count, g.ones = g.sb("ident", [P, P]), g.sb("count", [P, P]), g.sb("ones", [P, P])
        g.tri_upto, g.tri_below = g.sb("tri_upto", [P, P]), g.sb("tri_below", [P, P])
        g.dis, g.share = g.sb("dis", [P, NB]), g.sb("share", [P, NB])
        g.slot_in, g.slot_out = g.sb("slot_in", [P, NB], I32), g.sb("slot_out", [P, NB], I32)
        constants(nc, g)
        with ExitStack() as counted:
            g.counts = counted.enter_context(nc.sbuf_tensor("counts", [P, NB, NP], F16))
            with ExitStack() as graph:
                sb = lambda n, shape, dt=F32: graph.enter_context(nc.sbuf_tensor(n, shape, dt))
                g.src_i, g.dst_f = sb("src_i", [P, ET], I32), sb("dst_f", [P, ET])
                g.indeg, g.inv_deg, g.has, g.minus_base = (sb(n, [P, NB]) for n in ("indeg", "inv_deg", "has", "minus_base"))
                g.seg_start, g.seg_end = sb("seg_start", [P, NB], I32), sb("seg_end", [P, NB], I32)
                g.tiles, g.tile_pairs = sb("tiles", [P, NB + 1], I32), sb("tile_pairs", [P, NB + 1], I32)
                g.small_sb, g.node_d, g.w_self = sb("small_sb", [P, NB, SW]), sb("node_d", [P, NB, 4]), sb("w_self", [P, NB, 4])
                graph_tables(nc, g, io)
                project_nodes(nc, g, io, 0, io["x"], True)
                c_space = Space(nc, graph, "count")
                c_sems = [c_space.sem(n) for n in ("hot", "used", "summed", "act_read", "dve_read")]
                c_space.arm()
                for layer, target in enumerate((g.x_mid, g.x_gnn)):
                    if layer:
                        project_nodes(nc, g, io, layer, g.x_mid, False)
                    with ExitStack() as held:
                        room = held.enter_context(nc.sbuf_tensor(f"room{layer}", [P, max(ET * (SW + 1), ET * SW + 2 * NB * SW, RING * ROW)], F32))
                        g.per_edge = room[:, 0:ET * SW].rearrange("p (j c) -> p j c", c=SW)
                        g.ids = room[:, ET * SW:ET * (SW + 1)].bitcast(I32)
                        g.spare = room[:, ET * SW:ET * SW + 2 * NB * SW].rearrange("p (n b c) -> p n b c", n=2, c=SW)
                        g.ring = room[:, 0:RING * ROW].rearrange("p (k c) -> p k c", c=ROW)
                        counts_and_gather(nc, g, io, c_sems, ((0, SPLIT), (SPLIT, NB))[layer], layer == 0)
                        g.w_cols = held.enter_context(nc.sbuf_tensor(f"w_cols{layer}", [P, ET, 4], F32))
                        edge_weights(nc, g, io, layer)
                        aggregate(nc, g, io, layer, target)
            route(nc, g, io)
            experts(nc, g, io)
            combine(nc, g, io)
            hops_start(nc, g, io)
            hops(nc, g, io)
        with ExitStack() as slices:
            a = Space(nc, slices, "slc")
            a.x, a.swt = a.sb("x", [P, NB, D]), a.sb("swt", [P, NB, SH * SG])
            a.wxs, a.bias, a.valid = a.sb("wxs", [P, 2, SH * SG]), a.sb("bias", [P, SH * SG]), a.sb("valid", [P, NB])
            a.tok, a.v2 = a.sb("tok", [P, 4, D + 1]), a.sb("v2", [P, 4, D])
            slice_weights(nc, g, a, io)
            slice_tokens(nc, g, a, io)
            slice_attention(nc, g, a, io)
            slice_output(nc, g, a, io, out)


def kernel(**inputs):
    import numpy as np
    import concourse.bacc as bacc
    from concourse.bass_utils import run_bass_kernel_spmd

    a = {k: np.ascontiguousarray(v) for k, v in inputs.items()}
    pad = lambda v, n, fill=0: np.concatenate([v, np.full((n - len(v), *v.shape[1:]), fill, v.dtype)])
    x, src, dst, ea = a.pop("x"), a.pop("src"), a.pop("dst"), a.pop("edge_attr_32")
    src, dst, ea = pad(src, EP, NP - 1), pad(dst, EP, NP - 1), pad(ea, EP)
    arrays = {
        "x": pad(x, NP),
        "src_cols": src.reshape(ET, P).T, "dst_cols": dst.reshape(ET, P).T,
        "src_rows": src.reshape(P, ET),
        "dst_after": np.concatenate([np.full(1, -1, dst.dtype), dst]),
        "edge_attr": ea.reshape(P, ET, ED).transpose(2, 1, 0),
        **a,
    }
    arrays = {"in_" + k: np.ascontiguousarray(v).reshape(v.shape or (1,)) for k, v in arrays.items()}
    nc = bacc.Bacc("TRN2", target_bir_lowering=False, num_devices=1)
    io = {k[3:]: nc.dram_tensor(k, v.shape, mybir.dt.from_np(v.dtype), kind="ExternalInput").ap()
          for k, v in arrays.items()}
    out = nc.dram_tensor("out_0_dram", (NP, D), F32, kind="ExternalOutput").ap()
    main_program(nc, io, out)
    r = run_bass_kernel_spmd(nc, [arrays], core_ids=[0])
    return r.results[0]["out_0_dram"][:N]
```

```python
from contextlib import ExitStack

import concourse.bass as bass
from concourse import mybir

P = 128
N, E, D = 3125, 50000, 256
NB = -(-N // P)
NP = NB * P
RING = 14
ET = -(-(-(-E // P)) // RING) * RING
EP = ET * P
SPLIT = 9
ED, PH = 32, 64
HEADS = (4, 1)
SW = 8
ROW = 260
BIG = 1.0e30
LN_EPS = 1e-5
SLOPE = 0.2
NE, CAP, SLOTS, FF = 8, -(-5 * N // (4 * 8)), 512, 1024
HOPS = 5
SH, SD, SG = 8, 64, 64

ALU = mybir.AluOpType
ACT = mybir.ActivationFunctionType
AX = mybir.AxisListType.X
F32, I32, F16, BF16 = mybir.dt.float32, mybir.dt.int32, mybir.dt.float16, mybir.dt.bfloat16


def after(count):
    return count + 1


class Linked:

    def __init__(self, eng, sem, base=0):
        self.eng, self.sem, self.base, self.n = eng, sem, base, 0

    def __call__(self, instruction):
        self.n += 1
        instruction.then_inc(self.sem, 1)
        self.eng.wait_ge(self.sem, after(self.base + self.n))


class Space:

    def __init__(self, nc, ctx, tag):
        self.nc, self.ctx, self.tag, self.sems, self.from_zero = nc, ctx, tag, [], []
        ctx.callback(self.close)

    def close(self):
        self.nc.clear_and_free_semaphores(self.sems + self.from_zero)

    def block(self):
        self.arm()
        self.nc.all_engine_barrier()
        return self.nc.Block()

    def arm(self):
        for sem in self.sems:
            self.nc.gpsimd.sem_inc(sem, 1)

    def sb(self, name, shape, dt=F32):
        return self.ctx.enter_context(self.nc.sbuf_tensor(f"{self.tag}_{name}", shape, dt))

    def ps(self, name, shape=(P, 512), dt=F32):
        return self.ctx.enter_context(self.nc.psum_tensor(f"{self.tag}_{name}", list(shape), dt))

    def sem(self, name):
        self.sems.append(self.nc.alloc_semaphore(f"{self.tag}_{name}"))
        return self.sems[-1]

    def pool_sem(self, name):
        self.from_zero.append(self.nc.alloc_semaphore(f"{self.tag}_{name}"))
        return self.from_zero[-1]


def at(ap, i):
    s = ap[:, bass.ds(i, 1)] if len(ap.shape) == 2 else ap[:, bass.ds(i, 1), :]
    return s if len(ap.shape) == 2 else s.rearrange("p a f -> p (a f)")


def across(row, width):
    return row.rearrange("(a n) -> a n", a=1).to_broadcast([P, width])


def constants(nc, g):
    with ExitStack() as ctx:
        s = Space(nc, ctx, "cst")
        zero = s.sb("zero", [P, 2048])
        made, filled = s.sem("made"), s.sem("filled")
        with s.block() as block:
            @block.gpsimd
            def _(pool):
                link = Linked(pool, made)
                link(pool.memset(g.ident[:, :], 0.0))
                link(pool.affine_select(out=g.ident[:, :], in_=g.ident[:, :], compare_op=ALU.not_equal,
                                        fill=1.0, base=0, pattern=[[-1, P]], channel_multiplier=1))
                for tri, base in ((g.tri_upto, 0), (g.tri_below, -1)):
                    link(pool.memset(tri[:, :], 1.0))
                    link(pool.affine_select(out=tri[:, :], in_=tri[:, :], compare_op=ALU.is_ge, fill=0.0,
                                            base=base, pattern=[[1, P]], channel_multiplier=-1))
                link(pool.iota(g.count[:, :], pattern=[[1, P]], base=0, channel_multiplier=0,
                               allow_small_or_imprecise_dtypes=True))

            @block.vector
            def _(dve):
                nc.vector.memset(g.ones[:, :], 1.0)
                nc.vector.memset(zero[:, :], 0.0).then_inc(filled, 1)

            @block.sync
            def _(sp):
                sp.wait_ge(filled, after(1))
                sp.dma_start(g.edge_fill.rearrange("(p j) c -> p (j c)", p=P)[:, 0:2048], zero[:, :]).then_inc(filled, 16)
                sp.dma_start(g.edge_fill.rearrange("(p j) c -> p (j c)", p=P)[:, 2048:ET * SW],
                             zero[:, 0:ET * SW - 2048]).then_inc(filled, 16)
                per = NE * SLOTS * D // P // 2048
                for k in range(per):
                    sp.dma_start(g.expert_in.rearrange("(p j) c -> p (j c)", p=P)[:, k * 2048:(k + 1) * 2048],
                                 zero[:, :]).then_inc(filled, 16)
                sp.wait_ge(filled, after(1 + 16 * (2 + per)))


def graph_tables(nc, g, io):
    with ExitStack() as ctx:
        s = Space(nc, ctx, "grf")
        GRP = 8
        dst_i = s.sb("dst_i", [P, ET], I32)
        digit = s.sb("digit", [P, ET], I32)
        low, high = s.sb("low", [P, ET], F16), s.sb("high", [P, ET], F16)
        count16 = s.sb("count16", [P, P], F16)
        oh_low = s.sb("oh_low", [P, 2 * GRP, P], F16)
        oh_high = s.sb("oh_high", [P, 2 * GRP, NB], F16)
        zero16 = s.sb("zero16", [P, P], F16)
        total, upto = s.sb("total", [P, NB]), s.sb("upto", [P, NB])
        t0, t1 = s.sb("t0", [P, NB]), s.sb("t1", [P, NB])
        hist, prefix = s.ps("hist"), s.ps("prefix")
        loaded, linked, hot, used = s.sem("loaded"), s.sem("linked"), s.sem("hot"), s.sem("used")
        counted, summed, table, rooted = s.sem("counted"), s.sem("summed"), s.sem("table"), s.sem("rooted")
        have = s.sem("have")

        def by_halves(eng, group):
            with eng.Fori(0, ET // GRP // 2) as m:
                group(2 * m, 0)
                group(2 * m + 1, 1)
            assert ET // GRP % 2
            group(ET // GRP - 1, 0)

        with s.block() as block:
            @block.sync
            def _(sp):
                sp.dma_start(dst_i[:, :], io["dst_cols"]).then_inc(loaded, 16)
                sp.dma_start(g.src_i[:, :], io["src_cols"]).then_inc(loaded, 16)

            @block.vector
            def _(dve):
                link = Linked(dve, linked)
                dve.wait_ge(loaded, after(32))
                link(nc.vector.memset(zero16[:, :], 0.0))
                link(nc.vector.tensor_copy(count16[:, :], g.count[:, :]))
                link(nc.vector.tensor_copy(g.dst_f[:, :], dst_i[:, :]))
                link(nc.vector.tensor_scalar(digit[:, :], dst_i[:, :], P - 1, None, ALU.bitwise_and))
                link(nc.vector.tensor_copy(low[:, :], digit[:, :]))
                link(nc.vector.tensor_scalar(digit[:, :], dst_i[:, :], 7, None, ALU.logical_shift_right))
                link(nc.vector.tensor_copy(high[:, :], digit[:, :]))
                nc.vector.memset(zero16[:, 0:1], 0.0).then_inc(used, 1)

                def group(n, half):
                    dve.wait_ge(used, after(n))
                    nc.vector.tensor_tensor(
                        oh_low[:, half * GRP:(half + 1) * GRP, :], count16[:, :].unsqueeze(1).to_broadcast([P, GRP, P]),
                        low[:, bass.ds(n * GRP, GRP)].unsqueeze(2).to_broadcast([P, GRP, P]), ALU.is_equal)
                    nc.vector.tensor_tensor(
                        oh_high[:, half * GRP:(half + 1) * GRP, :],
                        count16[:, 0:NB].unsqueeze(1).to_broadcast([P, GRP, NB]),
                        high[:, bass.ds(n * GRP, GRP)].unsqueeze(2).to_broadcast([P, GRP, NB]),
                        ALU.is_equal).then_inc(hot, 1)
                by_halves(dve, group)
                dve.wait_ge(counted, after(1))
                nc.vector.tensor_copy(g.indeg[:, :], hist[:, 0:NB]).then_inc(have, 1)
                dve.wait_ge(summed, after(1))
                link(nc.vector.tensor_copy(total[:, :], prefix[:, 64:64 + NB]))
                link(nc.vector.memset(t0[:, :], 0.0))
                link(nc.vector.tensor_tensor_scan(upto[:, :], total[:, :], t0[:, :], 0.0, ALU.add, ALU.add))
                link(nc.vector.tensor_tensor(t0[:, :], upto[:, :], total[:, :], ALU.subtract))
                link(nc.vector.tensor_tensor(t0[:, :], t0[:, :], prefix[:, 0:NB], ALU.add))
                link(nc.vector.tensor_scalar(t1[:, :], g.indeg[:, :], 0.0, float(2 * EP), ALU.is_equal, ALU.mult))
                link(nc.vector.tensor_tensor(t1[:, :], t1[:, :], t0[:, :], ALU.add))
                link(nc.vector.tensor_copy(g.seg_start[:, :], t1[:, :]))
                link(nc.vector.tensor_tensor(t0[:, :], t0[:, :], g.indeg[:, :], ALU.add))
                link(nc.vector.tensor_scalar(t0[:, :], t0[:, :], -1.0, 0.0, ALU.add, ALU.max))
                link(nc.vector.tensor_copy(g.seg_end[:, :], t0[:, :]))
                link(nc.vector.tensor_copy(g.tiles[:, 1:NB + 1], upto[:, :]))
                link(nc.vector.tensor_scalar(g.tiles[:, 1:NB + 1], g.tiles[:, 1:NB + 1], 7, None,
                                             ALU.logical_shift_right))
                link(nc.vector.tensor_scalar(g.tiles[:, 1:NB + 1], g.tiles[:, 1:NB + 1], float(ET - 1), None, ALU.min))
                link(nc.vector.memset(g.tiles[:, 0:1], 0))
                link(nc.vector.tensor_scalar(g.tile_pairs[:, :], g.tiles[:, :], 1, None, ALU.logical_shift_right))
                link(nc.vector.tensor_scalar(g.minus_base[:, :], g.count[:, 0:NB], float(-P), None, ALU.mult))
                link(nc.vector.tensor_scalar(g.has[:, :], g.indeg[:, :], 1.0, None, ALU.min))
                link(nc.vector.tensor_scalar(t0[:, :], g.indeg[:, :], 1.0, None, ALU.max))
                link(nc.vector.reciprocal(g.inv_deg[:, :], t0[:, :]))
                nc.vector.tensor_scalar(t1[:, :], g.indeg[:, :], 1.0, None, ALU.add).then_inc(table, 1)
                dve.wait_ge(rooted, after(1))
                nc.vector.reciprocal(g.dis[:, :], t1[:, :]).then_inc(table, 1)

            @block.scalar
            def _(act):
                act.wait_ge(table, after(1))
                nc.scalar.activation(t1[:, :], t1[:, :], ACT.Sqrt).then_inc(rooted, 1)

            @block.tensor
            def _(pe):
                pe.wait_ge(hot, after(1))
                nc.tensor.matmul(hist[:, 0:NB], zero16[:, :], oh_high[:, 0, :], start=True, stop=False,
                                 skip_group_check=True)

                def group(n, half):
                    pe.wait_ge(hot, after(n + 1))
                    for k in range(half * GRP, (half + 1) * GRP):
                        mm = nc.tensor.matmul(hist[:, 0:NB], oh_low[:, k, :], oh_high[:, k, :],
                                              start=False, stop=False, skip_group_check=True)
                    mm.then_inc(used, 1)
                by_halves(pe, group)
                nc.tensor.matmul(hist[:, 0:NB], zero16[:, :], oh_high[:, 0, :], start=False, stop=True,
                                 skip_group_check=True).then_inc(counted, 1)
                pe.wait_ge(have, after(1))
                nc.tensor.matmul(prefix[:, 0:NB], g.tri_below[:, :], g.indeg[:, :], start=True, stop=True)
                nc.tensor.matmul(prefix[:, 64:64 + NB], g.ones[:, :], g.indeg[:, :], start=True,
                                 stop=True).then_inc(summed, 1)


def inverse_root(dve, link, out, var, root, half):
    link(dve.reciprocal(out, root))
    link(dve.tensor_tensor(half, out, out, ALU.mult))
    link(dve.tensor_tensor(half, half, var, ALU.mult))
    link(dve.tensor_scalar(half, half, -0.5, 1.5, ALU.mult, ALU.add))
    link(dve.tensor_tensor(out, out, half, ALU.mult))


ROWS_PART = 5


def load_rows(eng, x, rows, came):
    for c, sem in enumerate(came):
        part = slice(c * ROWS_PART, (c + 1) * ROWS_PART)
        eng.dma_start(x[:, part, :], rows.rearrange("(b p) d -> p b d", p=P)[:, part, :]).then_inc(sem, 16)


def rows_sems(s):
    return [s.sem(f"rows{c}") for c in range(NB // ROWS_PART)]


class Norm:

    def __init__(self, s):
        self.stats, self.pair = s.sb("stats", [P, NB, 6]), s.sb("pair", [P, NB, 2])
        self.mean, self.var = s.sb("mean", [P, NB]), s.sb("var", [P, NB])
        self.root, self.half, self.rstd = (s.sb(n, [P, NB]) for n in ("root", "half", "rstd"))
        self.varied, self.rooted = s.sem("varied"), s.sem("rooted")

    def on_vector(self, dve, sem, x, came=()):
        for b in range(NB):
            if came and b % ROWS_PART == 0:
                dve.wait_ge(came[b // ROWS_PART], after(16))
            dve.bn_stats(self.stats[:, b, :], x[:, b, :]).then_inc(sem, 1)
        dve.wait_ge(sem, after(NB))
        link = Linked(dve, sem, NB)
        for b in range(NB):
            last = dve.bn_aggr(self.pair[:, b, :], self.stats[:, b, :])
        link(last)
        link(dve.tensor_scalar(self.var[:, :], self.pair[:, :, 1], LN_EPS, None, ALU.add))
        link(dve.tensor_copy(self.mean[:, :], self.pair[:, :, 0]))
        dve.sem_inc(self.varied, 1)
        dve.wait_ge(self.rooted, after(1))
        inverse_root(dve, link, self.rstd[:, :], self.var[:, :], self.root[:, :], self.half[:, :])

    def block(self, dve, out, x, b):
        return dve.tensor_scalar(out, at(x, b), at(self.mean, b), at(self.rstd, b), ALU.subtract, ALU.mult)

    def on_scalar(self, act):
        act.wait_ge(self.varied, after(1))
        act.activation(self.root[:, :], self.var[:, :], ACT.Sqrt).then_inc(self.rooted, 1)


def pairs(eng, body):
    with eng.Fori(0, NB // 2) as j:
        body(((2 * j, 0, j), (2 * j + 1, 1, j)))
    if NB % 2:
        body(((NB - 1, 0, NB // 2),))


def lagged(eng, step, ahead=1):
    def both(b, i, j):
        following = (b + 2, i, j + 1) if ahead == 2 else (b + 1, 1 - i, j + i)
        step((b, i, j), following if not isinstance(b, int) or b + ahead < NB else None)

    whole = (NB - ahead) // 2
    with eng.Fori(0, whole) as j:
        for i in range(2):
            both(2 * j + i, i, j)
    for b in range(2 * whole, NB):
        both(b, b % 2, b // 2)


def project_nodes(nc, g, io, layer, x_in, normalise):
    H = HEADS[layer]
    F = D // H
    W = D + 2 * H + 1
    with ExitStack() as ctx:
        s = Space(nc, ctx, f"prj{layer}")
        x = s.sb("x", [P, NB, D])
        w = s.sb("w", [P, 2, W])
        wo = s.sb("wo", [P, 2])
        a_row = s.sb("a_row", [P, 2, D])
        prod = s.sb("prod", [P, D])
        bo = s.sb("bo", [P, 1])
        xs = [s.sb(f"xs{i}", [P, D]) for i in range(2)]
        xt = [s.sb(f"xt{i}", [P, 2, P]) for i in range(2)]
        full = [s.sb(f"row{i}", [P, ROW]) for i in range(2)]
        row = [r[:, 0:H * (F + 1)].rearrange("p (h f) -> p h f", h=H) for r in full]
        sums = s.sb("sums", [P, NB, 2 * H + 1])
        norm = Norm(s) if normalise else None
        turned = [s.ps(f"turned{i}") for i in range(2)]
        prod_ps = [s.ps(f"prod_ps{i}") for i in range(2)]
        rows_came = rows_sems(s)
        wts, linked, link2, wready = (s.sem(n) for n in ("wts", "linked", "link2", "wready"))
        fed, t_done, t_copied, m_done, m_read, stored, kept = (
            [s.sem(f"{n}{i}") for i in range(2)]
            for n in ("fed", "t_done", "t_copied", "m_done", "m_read", "stored", "kept"))
        summed, expd, tabled, out_done = (s.sem(n) for n in ("summed", "expd", "tabled", "out_done"))
        nm = lambda n: io[f"L0_gnn_{n}{layer}"]
        with s.block() as block:
            @block.sync
            def _(sp):
                load_rows(sp, x, x_in, rows_came)
                sp.dma_start(w[:, :, 0:D], nm("Wg").rearrange("(p k) n -> p k n", p=P)).then_inc(wts, 16)
                sp.dma_start(wo[:, :], nm("Wo").rearrange("(p k) -> p k", p=P)).then_inc(wts, 16)
                sp.dma_start(a_row[:, 0, :], across(nm("as").rearrange("h f -> (h f)"), D)).then_inc(wts, 16)
                sp.dma_start(a_row[:, 1, :], across(nm("ad").rearrange("h f -> (h f)"), D)).then_inc(wts, 16)
                sp.dma_start(bo[:, :], across(nm("bo"), 1)).then_inc(wts, 16)

                def body(blocks):
                    for b, i, j in blocks:
                        sp.wait_ge(m_read[i], after(j + 1))
                        sp.dma_start(g.hx_rows[bass.ds(b * P, P), :], full[i][:, :]).then_inc(stored[i], 16)
                pairs(sp, body)
                sp.wait_ge(tabled, after(1))
                sp.dma_start(g.small.rearrange("(b p) c -> p b c", p=P), g.small_sb[:, :, :]).then_inc(out_done, 16)
                sp.wait_ge(out_done, after(16))
                for i, turns in ((0, -(-NB // 2)), (1, NB // 2)):
                    sp.wait_ge(stored[i], after(16 * turns))
                    if normalise:
                        sp.wait_ge(kept[i], after(16 * turns))

            @block.vector
            def _(dve):
                if normalise:
                    norm.on_vector(dve, linked, x, rows_came)
                dve.wait_ge(wts, after(80))
                link = Linked(dve, link2)
                for k in range(2):
                    for c in range(2):
                        link(dve.tensor_tensor(prod[:, :], w[:, k, 0:D], a_row[:, c, :], ALU.mult))
                        link(dve.tensor_reduce(w[:, k, D + c * H:D + (c + 1) * H],
                                               prod[:, :].rearrange("p (h f) -> p h f", h=H), AX, ALU.add))
                link(dve.tensor_copy(w[:, :, W - 1], wo[:, :]))
                link(dve.memset(full[0][:, :], 1.0))
                link(dve.memset(full[1][:, :], 1.0))
                dve.sem_inc(wready, 1)

                def feed(b, i, j):
                    dve.wait_ge(t_done[i], after(j))
                    if normalise:
                        dve.wait_ge(kept[i], after(16 * j))
                        norm.block(dve, xs[i][:, :], x, b).then_inc(fed[i], 1)
                    else:
                        dve.tensor_copy(xs[i][:, :], at(x, b)).then_inc(fed[i], 1)

                def step(block, following):
                    if following:
                        feed(*following)
                    b, i, j = block
                    dve.wait_ge(m_done[i], after(j + 1))
                    dve.wait_ge(stored[i], after(16 * j))
                    dve.tensor_copy(row[i][:, :, 0:F], prod_ps[i][:, 0:D].rearrange("p (h f) -> p h f", h=H))
                    dve.tensor_copy(at(sums, b), prod_ps[i][:, D:W]).then_inc(m_read[i], 1)

                if not normalise:
                    for sem in rows_came:
                        dve.wait_ge(sem, after(16))
                feed(0, 0, 0)
                feed(1, 1, 0)
                lagged(dve, step, ahead=2)
                dve.wait_ge(m_read[0], after(-(-NB // 2)))
                dve.wait_ge(m_read[1], after(NB // 2))
                link(dve.memset(g.small_sb[:, :, :], 0.0))
                link(dve.tensor_copy(g.small_sb[:, :, 0:H], sums[:, :, 0:H]))
                dve.tensor_copy(g.node_d[:, :, 0:H], sums[:, :, H:2 * H]).then_inc(summed, 1)

            @block.scalar
            def _(act):
                if normalise:
                    norm.on_scalar(act)

                def body(blocks):
                    for b, i, j in blocks:
                        act.wait_ge(t_done[i], after(j + 1))
                        act.wait_ge(m_done[i], after(j))
                        act.activation(xt[i][:, :, :].rearrange("p k n -> p (k n)"), turned[i][:, 0:2 * P],
                                       ACT.Copy).then_inc(t_copied[i], 1)
                        if normalise:
                            act.wait_ge(fed[i], after(j + 1))
                            act.dma_start(g.x_norm[bass.ds(b * P, P), :], xs[i][:, :]).then_inc(kept[i], 16)
                pairs(act, body)
                act.wait_ge(summed, after(1))
                act.activation(g.small_sb[:, :, 4], sums[:, :, 2 * H], ACT.Exp, bias=bo[:, 0:1]).then_inc(tabled, 1)

            @block.tensor
            def _(pe):
                pe.wait_ge(wready, after(1))

                def turn(b, i, j):
                    pe.wait_ge(fed[i], after(j + 1))
                    pe.wait_ge(t_copied[i], after(j))
                    for k in range(2):
                        mm = pe.transpose(turned[i][:, k * P:(k + 1) * P], xs[i][:, k:D:2], g.ident[:, :])
                    mm.then_inc(t_done[i], 1)

                def step(block, following):
                    if following:
                        turn(*following)
                    b, i, j = block
                    pe.wait_ge(t_copied[i], after(j + 1))
                    pe.wait_ge(m_read[i], after(j))
                    for k in range(2):
                        mm = pe.matmul(prod_ps[i][:, 0:W], xt[i][:, k, :], w[:, k, :], start=(k == 0), stop=(k == 1))
                    mm.then_inc(m_done[i], 1)

                turn(0, 0, 0)
                lagged(pe, step)


def edge_terms(s, g, io, banks):
    WIDE = 512
    TURN = 2 * WIDE
    HT = sum(HEADS)
    room, used = g.counts[:, :, :].rearrange("p b n -> p (b n)").bitcast(F32), [0]

    def part(width, rows=P):
        used[0] += width
        return room[0:rows, used[0] - width:used[0]]

    ea = [part(TURN, ED) for i in range(2)]
    we, be = part(2 * PH, ED), part(1)
    wge, ae, v = part(D), part(D), part(HT)
    hid = [part(WIDE) for k in range(2)]
    terms = [part(TURN, HT) for i in range(2)]
    up, down = banks[0:2], banks[2:4]
    wts, linked, ready = (s.sem(n) for n in ("e_wts", "e_linked", "e_ready"))
    came, stored = ([s.sem(f"e_{n}{i}") for i in range(2)] for n in ("came", "stored"))
    upped, activated, downed, copied = (s.sem(n) for n in ("upped", "activated", "downed", "copied"))
    turns = EP // TURN
    assert turns % 2 == 1

    def on_sync(sp):
        for n in range(2):
            lo, hi = n * PH, (n + 1) * PH
            sp.dma_start(we[:, lo:hi], io[f"L0_gnn_We{n}"]).then_inc(wts, 16)
            sp.dma_start(be[lo:hi, :], io[f"L0_gnn_be{n}"].rearrange("(p a) -> p a", a=1)).then_inc(wts, 16)
            sp.dma_start(wge[lo:hi, :], io[f"L0_gnn_Wge{n}"]).then_inc(wts, 16)
            sp.dma_start(ae[lo:hi, :], io[f"L0_gnn_ae{n}"].rearrange("h f -> (h f)").rearrange(
                "(a n) -> a n", a=1).to_broadcast([PH, D])).then_inc(wts, 16)

        def load(t, i):
            sp.dma_start(ea[i], io["edge_attr"][:, bass.ds(t * TURN, TURN)]).then_inc(came[i], 16)

        def turn(t, i, load_more):
            if load_more:
                sp.wait_ge(upped, after(2 * t + 2))
                load(t + 2, i)
            sp.wait_ge(copied, after(2 * t + 2))
            sp.dma_start(g.edge_terms[:, bass.ds(t * TURN, TURN)], terms[i]).then_inc(stored[i], 16)

        load(0, 0)
        load(1, 1)
        with sp.Fori(0, turns // 2 - 1) as m:
            turn(2 * m, 0, True)
            turn(2 * m + 1, 1, True)
        turn(turns - 3, 0, True)
        turn(turns - 2, 1, False)
        turn(turns - 1, 0, False)
        over(sp)

    def on_vector(dve):
        link = Linked(dve, linked)
        dve.wait_ge(wts, after(16 * 8))
        link(dve.memset(v[:, :], 0.0))
        link(dve.tensor_tensor(wge[:, :], wge[:, :], ae[:, :], ALU.mult))
        for n, lo in ((0, 0), (1, HEADS[0])):
            link(dve.tensor_reduce(v[n * PH:(n + 1) * PH, lo:lo + HEADS[n]],
                                   wge[n * PH:(n + 1) * PH, :].rearrange("p (h f) -> p h f", h=HEADS[n]),
                                   AX, ALU.add))
        dve.sem_inc(ready, 1)

        def turn(t, i, m):
            dve.wait_ge(stored[i], after(16 * m))
            for k in range(2):
                dve.wait_ge(downed, after(2 * t + k + 1))
                dve.tensor_copy(terms[i][:, k * WIDE:(k + 1) * WIDE], down[k][0:HT, :]).then_inc(copied, 1)

        with dve.Fori(0, turns // 2) as m:
            turn(2 * m, 0, m)
            turn(2 * m + 1, 1, m)
        turn(turns - 1, 0, turns // 2)

    def on_scalar(act):
        with act.Fori(0, turns) as t:
            for k in range(2):
                act.wait_ge(upped, after(2 * t + k + 1))
                act.wait_ge(downed, after(2 * t))
                act.activation(hid[k], up[k][:, :], ACT.Relu, bias=be[:, 0:1]).then_inc(activated, 1)

    def on_tensor(pe):
        pe.wait_ge(ready, after(1))

        def hidden(t, i, nth, k, first=False):
            if k == 0:
                pe.wait_ge(came[i], after(16 * nth))
            if not first:
                pe.wait_ge(activated, after(2 * t - 1 + k))
            pe.matmul(up[k][:, :], we[:, :], ea[i][:, k * WIDE:(k + 1) * WIDE], start=True,
                      stop=True).then_inc(upped, 1)

        def outcome(t, k):
            pe.wait_ge(copied, after(2 * t))
            pe.wait_ge(activated, after(2 * t + k + 1))
            pe.matmul(down[k][0:HT, :], v[:, :], hid[k], start=True, stop=True).then_inc(downed, 1)

        def turn(t, i, nth):
            for k in range(2):
                outcome(t - 1, k)
                hidden(t, i, nth, k)

        for k in range(2):
            hidden(0, 0, 1, k, first=True)
        with pe.Fori(0, turns // 2) as m:
            turn(2 * m + 1, 1, m + 1)
            turn(2 * m + 2, 0, m + 2)
        for k in range(2):
            outcome(turns - 1, k)
        pe.wait_ge(copied, after(2 * turns))

    def over(eng):
        for i in range(2):
            eng.wait_ge(stored[i], after(16 * (turns // 2 + 1 - i)))

    return {"sync": on_sync, "vector": on_vector, "scalar": on_scalar, "tensor": on_tensor, "over": over}


def gather_small(s, g, io):
    half = RING // 2
    ring = s.sb("ring", [P, RING, SW])
    ids = g.ids
    now = [s.sb(f"now{i}", [P, half], I32) for i in range(2)]
    came = [s.pool_sem(f"came{k}") for k in range(RING)]
    listed = s.pool_sem("listed")
    picked, taken, gate = (s.sem(n) for n in ("picked", "taken", "gate"))

    def on_pool(pool):
        def issue(j, i):
            pool.tensor_copy(now[i][:, :], ids[:, bass.ds(j * RING + i * half, half)]).then_inc(picked, 1)
            pool.wait_ge(picked, after(2 * j + i + 1))
            pool.sem_inc(gate, 1)
            for k in range(half):
                pool.indirect_dma_start(
                    out=ring[:, i * half + k, :], out_offset=None, in_=g.small,
                    in_offset=bass.IndirectOffsetOnAxis(ap=now[i][:, k:k + 1], axis=0)
                ).then_inc(came[i * half + k], 16)

        def take(j, i):
            for k in range(half):
                pool.wait_ge(came[i * half + k], 16 * (j + 1))
            pool.tensor_copy(g.per_edge[:, bass.ds(j * RING + i * half, half), :],
                             ring[:, i * half:(i + 1) * half, :]).then_inc(taken, 1)
            pool.wait_ge(taken, after(2 * j + i + 1))

        pool.dma_start(ids[:, :], io["src_rows"]).then_inc(listed, 16)
        pool.wait_ge(listed, 16)
        issue(0, 0)
        issue(0, 1)
        with pool.Fori(1, ET // RING) as j:
            for i in range(2):
                take(j - 1, i)
                issue(j, i)
        take(ET // RING - 1, 0)
        take(ET // RING - 1, 1)

    return on_pool


def counts_and_gather(nc, g, io, c_sems, blocks, first_part):
    lo, hi = blocks
    with ExitStack() as ctx:
        s = Space(nc, ctx, f"cnt{lo}")
        BANK = 512
        banks = [(c, min(BANK, NP - c)) for c in range(0, NP, BANK)]
        n_act = (len(banks) + 1) // 2
        n_dve = len(banks) // 2
        DEPTH = 3
        HALF = NP // 2
        src_f = s.sb("src_f", [P, ET])
        number = s.sb("number", [P, NP], F16)
        oh_src = s.sb("oh_src", [P, DEPTH, NP], F16)
        oh_dst = s.sb("oh_dst", [P, DEPTH, P], F16)
        count16 = s.sb("count16", [P, P], F16)
        zero16 = s.sb("zero16", [P, P], F16)
        acc = [s.ps(f"acc{i}") for i in range(len(banks))]
        numbered, linked, ready, diag = (s.sem(n) for n in ("numbered", "linked", "ready", "diag"))
        hot, used, summed, act_read, dve_read = c_sems
        gather_on_pool = gather_small(s, g, io)
        edges = edge_terms(s, g, io, acc) if first_part else None
        with s.block() as block:
            if edges:
                @block.sync
                def _(sp):
                    edges["sync"](sp)

            @block.gpsimd
            def _(pool):
                pool.iota(number[:, :], pattern=[[1, NP]], base=-HALF, channel_multiplier=0,
                          allow_small_or_imprecise_dtypes=True).then_inc(numbered, 1)
                gather_on_pool(pool)

            def bounds(eng, b):
                return (eng.value_load(g.tiles[0:1, bass.ds(b, 1)], min_val=0, max_val=ET - 1),
                        eng.value_load(g.tiles[0:1, bass.ds(b + 1, 1)], min_val=0, max_val=ET - 1))

            @block.vector
            def _(dve):
                if edges:
                    edges["vector"](dve)
                link = Linked(dve, linked)
                link(dve.memset(zero16[:, :], 0.0))
                link(dve.tensor_copy(count16[:, :], g.count[:, :]))
                link(dve.tensor_scalar(src_f[:, :], g.src_i[:, :], float(-HALF), None, ALU.add))
                dve.sem_inc(ready, 1)
                dve.wait_ge(numbered, after(1))
                if edges:
                    dve.sem_inc(dve_read, n_dve)
                    edges["over"](dve)

                def step(t, b):
                    dve.wait_ge(used, after(t + b))
                    dve.tensor_scalar(at(oh_dst, (t + b) % DEPTH), count16[:, :], at(g.dst_f, t), at(g.minus_base, b),
                                      ALU.subtract, ALU.is_equal)
                    dve.tensor_scalar(at(oh_src, (t + b) % DEPTH), number[:, :], at(src_f, t), None,
                                      ALU.is_equal).then_inc(hot, 1)

                def block_sums(b, more):
                    first, last = bounds(dve, b)
                    with dve.If(last > first):
                        with dve.Fori(first + 1, last + 1) as t:
                            step(t, b)
                    if more:
                        step(last, b + 1)
                    dve.wait_ge(summed, after(b + 1))
                    for n, (c, width) in enumerate(banks):
                        if n % 2:
                            dve.tensor_copy(g.counts[:, bass.ds(b, 1), c:c + width].rearrange("p a f -> p (a f)"),
                                            acc[n][:, 0:width]).then_inc(dve_read, 1)

                step(bounds(dve, lo)[0], lo)
                with dve.Fori(lo, hi - 1) as b:
                    block_sums(b, True)
                block_sums(hi - 1, False)
                dve.wait_ge(act_read, after((hi + 1) * n_act))
                dve.wait_ge(dve_read, after((hi + 1) * n_dve))
                for b in range(lo, hi):
                    own = g.counts[:, b, b * P:(b + 1) * P]
                    dve.tensor_tensor(own, own, g.ident[:, :], ALU.add).then_inc(diag, 1)

            @block.scalar
            def _(act):
                if edges:
                    edges["scalar"](act)
                    act.sem_inc(act_read, n_act)
                    edges["over"](act)
                with act.Fori(lo, hi) as b:
                    act.wait_ge(summed, after(b + 1))
                    for n, (c, width) in enumerate(banks):
                        if n % 2 == 0:
                            act.activation(g.counts[:, bass.ds(b, 1), c:c + width].rearrange("p a f -> p (a f)"),
                                           acc[n][:, 0:width], ACT.Copy).then_inc(act_read, 1)

            @block.tensor
            def _(pe):
                if edges:
                    edges["tensor"](pe)
                    pe.sem_inc(used, DEPTH - 1)
                pe.wait_ge(ready, after(1))
                with pe.Fori(lo, hi) as b:
                    first, last = bounds(pe, b)
                    for n, (c, width) in enumerate(banks):
                        if n % 2:
                            pe.wait_ge(dve_read, after(b * n_dve + n // 2 + 1))
                        else:
                            pe.wait_ge(act_read, after(b * n_act + n // 2 + 1))
                        pe.matmul(acc[n][:, 0:1], zero16[:, 0:P], zero16[:, 0:1], start=True, stop=False,
                                  skip_group_check=True)
                    with pe.Fori(first, last + 1) as t:
                        pe.wait_ge(hot, after(t + b + 1))
                        for n, (c, width) in enumerate(banks):
                            mm = pe.matmul(acc[n][:, 0:width], at(oh_dst, (t + b) % DEPTH),
                                           oh_src[:, bass.ds((t + b) % DEPTH, 1), c:c + width].rearrange("p a f -> p (a f)"),
                                           start=False, stop=False, skip_group_check=True)
                        mm.then_inc(used, 1)
                    for n, (c, width) in enumerate(banks):
                        mm = pe.matmul(acc[n][:, 0:1], zero16[:, 0:P], zero16[:, 0:1], start=False, stop=True,
                                       skip_group_check=True)
                    mm.then_inc(summed, 1)


def edge_weights(nc, g, io, layer):
    H = HEADS[layer]
    first_head = sum(HEADS[:layer])
    chunks = [(c, min(P, ET - c)) for c in range(0, ET, P)]
    with ExitStack() as ctx:
        s = Space(nc, ctx, f"wts{layer}")
        u, v = s.sb("u", [P, H * ET]), s.sb("v", [P, H * ET])
        uh, vh = (x[:, :].rearrange("p (h j) -> p h j", h=H) for x in (u, v))
        dsts = s.sb("dsts", [P, 2 * ET], I32)
        before, here, tail = dsts[:, 0:ET], dsts[:, ET:], dsts[:, :].bitcast(F32)
        same, fresh = s.sb("same", [P, ET]), s.sb("fresh", [P, ET])
        rows = s.sb("rows", [P, 4, 2 * H])
        turned = s.sb("turned", [2 * H, 4, P])
        chain = s.sb("chain", [2 * H, 2, P + 1])
        carry = s.sb("carry", [P, 2, 2 * H])
        ends, fill = g.spare[:, 0, :, :], g.spare[:, 1, :, :]
        self_v, top = s.sb("self_v", [P, NB, H]), s.sb("top", [P, NB, H])
        turn_ps, back_ps = s.ps("turn_ps"), s.ps("back_ps")
        cols_ps = [s.ps(f"cols_ps{i}") for i in range(2)]
        loaded, linked = s.sem("loaded"), s.sem("linked")
        summed_up, transposed, chained, returned = (s.sem(n) for n in ("summed_up", "transposed", "chained", "returned"))
        scanned, stored, node_done, spread = (s.sem(n) for n in ("scanned", "stored", "node_done", "spread"))
        gathered, scattered = s.pool_sem("gathered"), s.pool_sem("scattered")
        weighed, exp_done, w_stored, turned_cols, copied_cols = (
            s.sem(n) for n in ("weighed", "exp_done", "w_stored", "turned_cols", "copied_cols"))
        w_loaded = [s.sem(f"w_loaded{i}") for i in range(len(chunks))]
        by_tile = [u[0:n, i * P * H:(i + 1) * P * H] if i < len(chunks) - 1 else tail[0:n, 0:P * H]
                   for i, (_, n) in enumerate(chunks)]
        pe_all = g.per_edge
        per_node = lambda x: x[:, :].unsqueeze(2).to_broadcast([P, NB, H])
        with s.block() as block:
            @block.sync
            def _(sp):
                sp.dma_start(before, io["dst_after"][0:EP].rearrange("(p j) -> p j", p=P)).then_inc(loaded, 16)
                sp.dma_start(here, io["dst_after"][1:EP + 1].rearrange("(p j) -> p j", p=P)).then_inc(loaded, 16)
                sp.dma_start(uh, g.edge_terms[first_head:first_head + H, :].rearrange(
                    "h (p j) -> p h j", p=P)).then_inc(loaded, 16)
                sp.wait_ge(scanned, after(1))
                sp.dma_start(g.edge_scan.rearrange("(p j) c -> p j c", p=P), pe_all[:, :, :]).then_inc(stored, 16)
                sp.wait_ge(scattered, 16 * NB)
                sp.dma_start(pe_all[:, :, :], g.edge_fill.rearrange("(p j) c -> p j c", p=P)).then_inc(spread, 16)
                sp.wait_ge(exp_done, after(2))
                w_dram = g.edge_w[0:EP * H]
                sp.dma_start(w_dram.rearrange("(p c) -> p c", p=P), v[:, :]).then_inc(w_stored, 16)
                sp.wait_ge(w_stored, after(16))
                for i, (c, n) in enumerate(chunks):
                    sp.dma_start(by_tile[i], w_dram.rearrange("(t c) -> t c", t=ET)[c:c + n, :]).then_inc(w_loaded[i], 16)

            @block.gpsimd
            def _(pool):
                pool.wait_ge(stored, after(16))
                for b in range(NB):
                    pool.indirect_dma_start(
                        out=ends[:, b, :], out_offset=None, in_=g.edge_scan,
                        in_offset=bass.IndirectOffsetOnAxis(ap=g.seg_end[:, b:b + 1], axis=0)).then_inc(gathered, 16)
                pool.wait_ge(node_done, after(1))
                for b in range(NB):
                    pool.indirect_dma_start(
                        out=g.edge_fill, out_offset=bass.IndirectOffsetOnAxis(ap=g.seg_start[:, b:b + 1], axis=0),
                        in_=fill[:, b, :], in_offset=None, bounds_check=EP - 1, oob_is_err=False).then_inc(scattered, 16)

            @block.vector
            def _(dve):
                link = Linked(dve, linked)
                events = [0]

                def scan_sum(out, data, start):
                    link(dve.tensor_tensor_scan(out, same[:, :], data, start, ALU.mult, ALU.add))

                def scan_max(out, data, start):
                    link(dve.tensor_tensor_scan(out, fresh[:, :], data, start, ALU.add, ALU.max))

                def carries(n_sum, n_max):
                    n = max(n_sum, n_max)
                    events[0] += 1
                    dve.sem_inc(summed_up, 1)
                    dve.wait_ge(transposed, after(events[0]))
                    link(dve.tensor_copy(turned[0:n, :, :].rearrange("h k p -> h (k p)"), turn_ps[0:n, :]))
                    link(dve.memset(chain[0:n, 0, 0:1], 0.0))
                    link(dve.memset(chain[0:n, 1, 0:1], -BIG))
                    link(dve.tensor_tensor_scan(chain[0:n, 0, 1:P + 1], turned[0:n, 2, :], turned[0:n, 0, :], 0.0,
                                                ALU.mult, ALU.add))
                    link(dve.tensor_tensor_scan(chain[0:n, 1, 1:P + 1], turned[0:n, 3, :], turned[0:n, 1, :], -BIG,
                                                ALU.add, ALU.max))
                    dve.sem_inc(chained, 1)
                    dve.wait_ge(returned, after(events[0]))
                    link(dve.tensor_copy(carry[:, :, 0:n], back_ps[:, 0:2 * n].rearrange("p (k h) -> p k h", k=2)))

                dve.wait_ge(loaded, after(48))
                link(dve.tensor_tensor(same[:, :], before, here, ALU.is_equal))
                link(dve.tensor_scalar(fresh[:, :], same[:, :], -1.0, BIG, ALU.add, ALU.mult))
                link(dve.memset(rows[:, :, :], 0.0))
                link(dve.tensor_reduce(rows[:, 2, 0:1], same[:, :], AX, ALU.min))
                link(dve.tensor_copy(rows[:, 2, 1:2 * H], rows[:, 2, 0:1].to_broadcast([P, 2 * H - 1])))
                link(dve.tensor_scalar(rows[:, 3, :], rows[:, 2, :], -1.0, BIG, ALU.add, ALU.mult))
                link(dve.tensor_tensor(uh, uh, pe_all[:, :, 4:5].rearrange("p j a -> p a j").to_broadcast([P, H, ET]),
                                       ALU.mult))
                link(dve.tensor_tensor(vh, uh, pe_all[:, :, 0:H].rearrange("p j h -> p h j"), ALU.add))
                for h in range(H):
                    scan_sum(pe_all[:, :, h], uh[:, h, :], 0.0)
                    scan_max(pe_all[:, :, H + h], vh[:, h, :], -BIG)
                link(dve.tensor_copy(rows[:, 0, 0:H], pe_all[:, ET - 1, 0:H]))
                link(dve.tensor_copy(rows[:, 1, 0:H], pe_all[:, ET - 1, H:2 * H]))
                carries(2 * H, 2 * H)
                for h in range(H):
                    scan_sum(pe_all[:, :, h], uh[:, h, :], carry[:, 0, h:h + 1])
                    scan_max(pe_all[:, :, H + h], vh[:, h, :], carry[:, 1, h:h + 1])
                dve.sem_inc(scanned, 1)

                dve.wait_ge(gathered, 16 * NB)
                link(dve.memset(fill[:, :, :], 0.0))
                total, peak = ends[:, :, 0:H], ends[:, :, H:2 * H]
                link(dve.tensor_tensor(self_v[:, :, :], total, per_node(g.inv_deg), ALU.mult))
                link(dve.tensor_tensor(self_v[:, :, :], self_v[:, :, :], per_node(g.has), ALU.mult))
                link(dve.tensor_tensor(self_v[:, :, :], self_v[:, :, :], g.small_sb[:, :, 0:H], ALU.add))
                link(dve.tensor_tensor(top[:, :, :], peak, per_node(g.has), ALU.mult))
                link(dve.tensor_scalar(ends[:, :, 0], g.has[:, :], -1.0, BIG, ALU.add, ALU.mult))
                link(dve.tensor_tensor(top[:, :, :], top[:, :, :], ends[:, :, 0:1].to_broadcast([P, NB, H]), ALU.add))
                link(dve.tensor_tensor(top[:, :, :], top[:, :, :], self_v[:, :, :], ALU.max))
                link(dve.tensor_tensor(top[:, :, :], top[:, :, :], g.node_d[:, :, 0:H], ALU.add))
                link(dve.scalar_tensor_tensor(fill[:, :, H:2 * H], top[:, :, :], SLOPE, top[:, :, :], ALU.mult, ALU.max))
                link(dve.tensor_copy(fill[:, :, 0:H], g.node_d[:, :, 0:H]))
                dve.sem_inc(node_done, 1)
                link(dve.tensor_tensor(self_v[:, :, :], self_v[:, :, :], g.node_d[:, :, 0:H], ALU.add))
                link(dve.scalar_tensor_tensor(self_v[:, :, :], self_v[:, :, :], SLOPE, self_v[:, :, :], ALU.mult, ALU.max))
                link(dve.tensor_tensor(self_v[:, :, :], self_v[:, :, :], fill[:, :, H:2 * H], ALU.subtract))
                dve.sem_inc(weighed, 1)

                dve.wait_ge(spread, after(16))
                for c in range(2 * H):
                    scan_sum(uh[:, 0, :], pe_all[:, :, c], 0.0)
                    link(dve.tensor_copy(rows[:, 0, c:c + 1], uh[:, 0, ET - 1:ET]))
                carries(2 * H, 2 * H)
                for c in range(2 * H):
                    scan_sum(pe_all[:, :, c], pe_all[:, :, c], carry[:, 0, c:c + 1])
                link(dve.tensor_tensor(uh, vh, pe_all[:, :, 0:H].rearrange("p j h -> p h j"), ALU.add))
                link(dve.scalar_tensor_tensor(u[:, :], u[:, :], SLOPE, u[:, :], ALU.mult, ALU.max))
                link(dve.tensor_tensor(uh, uh, pe_all[:, :, H:2 * H].rearrange("p j h -> p h j"), ALU.subtract))
                dve.sem_inc(weighed, 1)
                for i, (c, n) in enumerate(chunks):
                    for h in range(H):
                        k = i * H + h
                        dve.wait_ge(turned_cols, after(k + 1))
                        dve.tensor_copy(g.w_cols[:, c:c + n, h], cols_ps[k % 2][:, 0:n]).then_inc(copied_cols, 1)

            @block.scalar
            def _(act):
                act.wait_ge(weighed, after(1))
                act.activation(g.w_self[:, :, 0:H], self_v[:, :, :], ACT.Exp).then_inc(exp_done, 1)
                act.wait_ge(weighed, after(2))
                act.activation(v[:, :].rearrange("p (j h) -> p h j", h=H), uh, ACT.Exp).then_inc(exp_done, 1)

            @block.tensor
            def _(pe):
                for n in range(2):
                    pe.wait_ge(summed_up, after(n + 1))
                    for k in range(4):
                        mm = pe.transpose(turn_ps[0:2 * H, k * P:(k + 1) * P], rows[:, k, :], g.ident[:, :])
                    mm.then_inc(transposed, 1)
                    pe.wait_ge(chained, after(n + 1))
                    for k in range(2):
                        mm = pe.transpose(back_ps[:, k * 2 * H:(k + 1) * 2 * H], chain[:, k, 0:P],
                                          g.ident[0:2 * H, 0:2 * H])
                    mm.then_inc(returned, 1)
                for i, (c, n) in enumerate(chunks):
                    pe.wait_ge(w_loaded[i], after(16))
                    for h in range(H):
                        k = i * H + h
                        if k >= 2:
                            pe.wait_ge(copied_cols, after(k - 1))
                        pe.transpose(cols_ps[k % 2][:, 0:n], by_tile[i][:, h:P * H:H],
                                     g.ident[0:n, 0:n]).then_inc(turned_cols, 1)


def aggregate(nc, g, io, layer, out_dram):
    H = HEADS[layer]
    F = D // H
    R = H * (F + 1)
    with ExitStack() as ctx:
        s = Space(nc, ctx, f"agg{layer}")
        ring = g.ring
        now = [s.sb(f"now{i}", [P, RING], I32) for i in range(2)]
        oh, far = ([s.sb(f"{n}{k}", [P, P]) for k in range(2)] for n in ("oh", "far"))
        nodes = s.sb("nodes", [P, P])
        msg = s.sb("msg", [P, 4, R])
        own, res = s.sb("own", [P, ROW]), s.sb("res", [P, 3, D])
        y, inv = s.sb("y", [P, R]), s.sb("inv", [P, H])
        bias = s.sb("bias", [P, D])
        zero = s.sb("zero", [P, P])
        acc, idle = s.ps("acc", (P, 2, 512)), s.ps("idle")
        yh = y[:, :].rearrange("p (h f) -> p h f", h=H)
        came = [s.pool_sem(f"came{k}") for k in range(RING)]
        picked, gate, in_order, freed, summed, read, loaded, finished, stored, consts, linked = (
            s.sem(n) for n in ("picked", "gate", "in_order", "freed", "summed", "read", "loaded", "finished", "stored",
                               "consts", "linked"))
        weighed, apart, numbered = s.sem("weighed"), s.sem("apart"), s.sem("numbered")
        hot, used = ([s.sem(f"{n}{k}") for k in range(2)] for n in ("hot", "used"))
        residuals = [g.x_norm] if layer == 0 else [g.x_mid, g.x_norm, io["x"]]
        n_loads = 1 + len(residuals)
        n_links = len(residuals) + (3 if layer else 5)

        def bounds(eng, b):
            return (eng.value_load(g.tile_pairs[0:1, bass.ds(b, 1)], min_val=0, max_val=ET // 2 - 1),
                    eng.value_load(g.tile_pairs[0:1, bass.ds(b + 1, 1)], min_val=0, max_val=ET // 2 - 1))

        with s.block() as block:
            @block.gpsimd
            def _(pool):
                with pool.Fori(0, ET // (2 * RING)) as j:
                    for i in range(2):
                        pool.tensor_copy(now[i][:, :], g.src_i[:, bass.ds((2 * j + i) * RING, RING)]).then_inc(picked, 1)
                        pool.wait_ge(picked, after(2 * j + i + 1))
                        pool.sem_inc(gate, 1)
                        for q in range(RING // 2):
                            pool.wait_ge(freed, after((2 * j + i) * (RING // 2) + q + 1))
                            pool.sem_inc(gate, 1)
                            for k in (2 * q, 2 * q + 1):
                                pool.indirect_dma_start(
                                    out=ring[:, k, :], out_offset=None, in_=g.hx_rows,
                                    in_offset=bass.IndirectOffsetOnAxis(ap=now[i][:, k:k + 1], axis=0)
                                ).then_inc(came[k], 16)

            @block.sync
            def _(sp):
                with sp.Fori(0, ET // RING) as j:
                    for k in range(RING):
                        sp.wait_ge(came[k], 16 * (j + 1))
                        sp.sem_inc(in_order, 1)

            @block.scalar
            def _(act):
                act.dma_start(bias[:, :], across(io[f"L0_gnn_bg{layer}"], D)).then_inc(consts, 16)

                def load(b):
                    act.dma_start(own[:, :], g.hx_rows[bass.ds(b * P, P), :]).then_inc(loaded, 16)
                    for n, src in enumerate(residuals):
                        act.dma_start(res[:, n, :], src[bass.ds(b * P, P), :]).then_inc(loaded, 16)

                def store(b):
                    act.wait_ge(finished, after(b + 1))
                    act.dma_start(out_dram[bass.ds(b * P, P), :], y[:, 0:D]).then_inc(stored, 16)

                def step(p, b):
                    for k in range(2):
                        act.wait_ge(hot[k], after(p + b))
                        act.activation(far[k][:, :], nodes[:, :], ACT.Abs, bias=at(g.dst_f, 2 * p + k)).then_inc(apart, 1)
                    for k in range(2):
                        act.wait_ge(apart, after(2 * (p + b) + k + 1))
                        act.wait_ge(used[k], after(p + b + 1))
                        act.activation(oh[k][:, :], far[k][:, :], ACT.Relu, scale=-1.0,
                                       bias=g.ones[:, 0:1]).then_inc(hot[k], 1)

                def number(b):
                    act.activation(nodes[:, :], g.count[:, :], ACT.Identity, scale=-1.0,
                                   bias=at(g.minus_base, b)).then_inc(numbered, 1)
                    act.wait_ge(numbered, after(b + 1))

                def rest_of_block(b, more):
                    first, last = bounds(act, b)
                    with act.If(last > first):
                        with act.Fori(first + 1, last + 1) as p:
                            step(p, b)
                    if more:
                        number(b + 1)
                        step(last, b + 1)
                    store(b)
                    if more:
                        load(b + 1)

                load(0)
                number(0)
                step(0, 0)
                with act.Fori(0, NB - 1) as b:
                    rest_of_block(b, True)
                rest_of_block(NB - 1, False)
                act.wait_ge(stored, after(16 * NB))

            @block.vector
            def _(dve):
                dve.memset(zero[:, :], 0.0).then_inc(linked, 1)
                dve.sem_inc(freed, RING // 2)
                dve.sem_inc(read, 1)
                dve.wait_ge(consts, after(16))

                def step(p, b):
                    dve.wait_ge(in_order, after(2 * p + 2))
                    dve.wait_ge(used[1], after(p + b))
                    split = lambda t: t.rearrange("p k (h f) -> p (k h) f", h=H)
                    weighted = dve.tensor_tensor(
                        split(msg[:, bass.ds((p + b) % 2 * 2, 2), :]),
                        split(ring[:, bass.ds(p % (RING // 2) * 2, 2), 0:R]),
                        g.w_cols[:, bass.ds(2 * p, 2), 0:H].rearrange("p k h -> p (k h)").unsqueeze(2)
                        .to_broadcast([P, 2 * H, F + 1]) if H == 4 else
                        g.w_cols[:, bass.ds(2 * p, 2), 0:1].to_broadcast([P, 2, F + 1]), ALU.mult)
                    weighted.then_inc(weighed, 1)

                def sum_block(b, more):
                    first, last = bounds(dve, b)
                    with dve.If(last > first):
                        with dve.Fori(first + 1, last + 1) as p:
                            dve.wait_ge(weighed, after(p + b))
                            dve.sem_inc(freed, 1)
                            step(p, b)
                    if more:
                        step(last, b + 1)
                    link = Linked(dve, linked, 1 + n_links * b)
                    dve.wait_ge(loaded, after(16 * n_loads * (b + 1)))
                    base = res[:, 0, :]
                    link(dve.tensor_tensor(base, base, bias[:, :], ALU.add))
                    for n in range(1, len(residuals)):
                        link(dve.tensor_tensor(base, base, res[:, n, :], ALU.add))
                    dve.wait_ge(summed, after(b + 1))
                    dve.wait_ge(stored, after(16 * b))
                    for h in range(H):
                        cols = slice(h * (F + 1), (h + 1) * (F + 1))
                        looped = dve.scalar_tensor_tensor(
                            yh[:, h, :], own[:, cols], g.w_self[:, bass.ds(b, 1), h:h + 1].rearrange("p a f -> p (a f)"),
                            acc[:, bass.ds(b % 2, 1), cols].rearrange("p a f -> p (a f)"), ALU.mult, ALU.add)
                    link(looped)
                    dve.sem_inc(read, 1)
                    link(dve.reciprocal(inv[:, :], yh[:, :, F]))
                    if layer:
                        link(dve.scalar_tensor_tensor(y[:, 0:D], y[:, 0:D], inv[:, 0:1], base, ALU.mult, ALU.add))
                    else:
                        link(dve.tensor_tensor(own[:, 0:D].rearrange("p (h f) -> p h f", h=H), yh[:, :, 0:F],
                                               inv[:, :].unsqueeze(2).to_broadcast([P, H, F]), ALU.mult))
                        link(dve.tensor_tensor(y[:, 0:D], own[:, 0:D], base, ALU.add))
                        link(dve.tensor_scalar(y[:, 0:D], y[:, 0:D], 0.0, None, ALU.max))
                    dve.sem_inc(finished, 1)

                step(0, 0)
                with dve.Fori(0, NB - 1) as b:
                    sum_block(b, True)
                sum_block(NB - 1, False)

            @block.tensor
            def _(pe):
                for k in range(2):
                    pe.sem_inc(used[k], 1)
                pe.wait_ge(linked, after(1))
                with pe.Fori(0, NB) as b:
                    first, last = bounds(pe, b)
                    pe.wait_ge(read, after(b))
                    sums = at(acc, b % 2)
                    pe.matmul(sums[:, 0:1], zero[:, :], zero[:, 0:1], start=True, stop=False, skip_group_check=True)

                    def step(p):
                        pe.wait_ge(weighed, after(p + b + 1))
                        for k in range(2):
                            pe.wait_ge(hot[k], after(p + b + 1))
                            pe.matmul(sums[:, 0:R], oh[k][:, :], at(msg, (p + b) % 2 * 2 + k), start=False, stop=False,
                                      skip_group_check=True).then_inc(used[k], 1)

                    step(first)
                    with pe.If(last > first):
                        for _ in range(12):
                            pe.matmul(idle[:, 0:P], zero[:, :], zero[:, :], start=True, stop=True)
                        with pe.Fori(first + 1, last + 1) as p:
                            step(p)
                    pe.matmul(sums[:, 0:1], zero[:, :], zero[:, 0:1], start=False, stop=True,
                              skip_group_check=True).then_inc(summed, 1)


def route(nc, g, io):
    with ExitStack() as ctx:
        s = Space(nc, ctx, "rte")
        x = s.sb("x", [P, NB, D])
        gw, gb = s.sb("gw", [P, 2, NE]), s.sb("gb", [P, NE])
        xs = [s.sb(f"xs{i}", [P, D]) for i in range(2)]
        xt = [s.sb(f"xt{i}", [P, 2, P]) for i in range(2)]
        cube = lambda n: s.sb(n, [P, NB, NE])
        logits, hot, number, work, before = (cube(n) for n in ("logits", "hot", "number", "work", "before"))
        top, choice, place, kept_f = (s.sb(n, [P, NB]) for n in ("top", "choice", "place", "kept_f"))
        zero = s.sb("zero", [P, NB])
        norm = Norm(s)
        turned = [s.ps(f"turned{i}") for i in range(2)]
        lg = [s.ps(f"lg{i}") for i in range(2)]
        sums = s.ps("sums")
        loaded, linked, link2, numbered, shifted, expd, hotted, cumulated, placed = (
            s.sem(n) for n in ("loaded", "linked", "link2", "numbered", "shifted", "expd", "hotted", "cumulated",
                               "placed"))
        sent, rows_came = s.pool_sem("sent"), rows_sems(s)
        fed, t_done, t_copied, m_done, m_read, kept = ([s.sem(f"{n}{i}") for i in range(2)] for n in (
            "fed", "t_done", "t_copied", "m_done", "m_read", "kept"))
        flat = lambda c: c[:, :, :].rearrange("p b e -> p (b e)")
        with s.block() as block:
            @block.sync
            def _(sp):
                load_rows(sp, x, g.x_gnn, rows_came)
                sp.dma_start(gw[:, :, :], io["L0_ffn_gate_w"].rearrange("(p k) e -> p k e", p=P)).then_inc(loaded, 16)
                sp.dma_start(gb[:, :], across(io["L0_ffn_gate_b"], NE)).then_inc(loaded, 16)

            @block.gpsimd
            def _(pool):
                pool.iota(number[:, :, :], pattern=[[0, NB], [1, NE]], base=0, channel_multiplier=0,
                          allow_small_or_imprecise_dtypes=True).then_inc(numbered, 1)
                pool.wait_ge(placed, after(1))
                for b in range(NB):
                    pool.indirect_dma_start(
                        out=g.expert_in, out_offset=bass.IndirectOffsetOnAxis(ap=g.slot_in[:, b:b + 1], axis=0),
                        in_=x[:, b, :], in_offset=None, bounds_check=NE * SLOTS - 1, oob_is_err=False).then_inc(sent, 16)
                pool.wait_ge(sent, 16 * NB)

            @block.vector
            def _(dve):
                norm.on_vector(dve, linked, x, rows_came)
                dve.wait_ge(loaded, after(32))
                link = Linked(dve, link2)

                def feed(b, i, j):
                    dve.wait_ge(t_done[i], after(j))
                    dve.wait_ge(kept[i], after(j))
                    norm.block(dve, xs[i][:, :], x, b).then_inc(fed[i], 1)

                def step(block, following):
                    if following:
                        feed(*following)
                    b, i, j = block
                    dve.wait_ge(m_done[i], after(j + 1))
                    dve.tensor_tensor(at(logits, b), lg[i][:, 0:NE], gb[:, :], ALU.add).then_inc(m_read[i], 1)

                feed(0, 0, 0)
                feed(1, 1, 0)
                lagged(dve, step, ahead=2)
                wide = lambda t: t[:, :].unsqueeze(2).to_broadcast([P, NB, NE])
                dve.wait_ge(m_read[0], after(-(-NB // 2)))
                dve.wait_ge(m_read[1], after(NB // 2))
                dve.wait_ge(numbered, after(1))
                link(dve.tensor_reduce(top[:, :], logits[:, :, :], AX, ALU.max))
                link(dve.tensor_tensor(work[:, :, :], logits[:, :, :], wide(top), ALU.subtract))
                dve.sem_inc(shifted, 1)
                link(dve.tensor_tensor(hot[:, :, :], logits[:, :, :], wide(top), ALU.is_lt))
                link(dve.scalar_tensor_tensor(hot[:, :, :], hot[:, :, :], float(NE), number[:, :, :], ALU.mult, ALU.add))
                link(dve.tensor_reduce(choice[:, :], hot[:, :, :], AX, ALU.min))
                link(dve.tensor_tensor(hot[:, :, :], number[:, :, :], wide(choice), ALU.is_equal))
                dve.sem_inc(hotted, 1)
                dve.wait_ge(expd, after(1))
                link(dve.tensor_reduce(top[:, :], work[:, :, :], AX, ALU.add))
                link(dve.reciprocal(top[:, :], top[:, :]))
                dve.wait_ge(cumulated, after(1))
                W = NB * NE
                link(dve.tensor_copy(flat(work), sums[:, 256:256 + W]))
                link(dve.memset(zero[:, :], 0.0))
                for e in range(NE):
                    link(dve.tensor_tensor_scan(before[:, :, e], work[:, :, e], zero[:, :], 0.0, ALU.add, ALU.add))
                link(dve.tensor_tensor(before[:, :, :], before[:, :, :], work[:, :, :], ALU.subtract))
                link(dve.tensor_tensor(flat(before), flat(before), sums[:, 0:W], ALU.add))
                link(dve.tensor_tensor(before[:, :, :], before[:, :, :], hot[:, :, :], ALU.mult))
                link(dve.tensor_reduce(place[:, :], before[:, :, :], AX, ALU.add))
                link(dve.tensor_scalar(place[:, :], place[:, :], -1.0, None, ALU.add))
                link(dve.tensor_scalar(kept_f[:, :], place[:, :], float(CAP), None, ALU.is_lt))
                link(dve.tensor_tensor(g.share[:, :], top[:, :], kept_f[:, :], ALU.mult))
                link(dve.tensor_scalar(place[:, :], place[:, :], float(CAP - 1), None, ALU.min))
                link(dve.scalar_tensor_tensor(place[:, :], choice[:, :], float(SLOTS), place[:, :], ALU.mult, ALU.add))
                link(dve.tensor_copy(g.slot_out[:, :], place[:, :]))
                link(dve.tensor_scalar(kept_f[:, :], kept_f[:, :], -1.0, float(-NE * SLOTS), ALU.add, ALU.mult))
                link(dve.tensor_tensor(place[:, :], place[:, :], kept_f[:, :], ALU.add))
                link(dve.tensor_copy(g.slot_in[:, :], place[:, :]))
                dve.wait_ge(kept[0], after(-(-NB // 2)))
                dve.wait_ge(kept[1], after(NB // 2))
                dve.sem_inc(placed, 1)

            @block.scalar
            def _(act):
                norm.on_scalar(act)

                def body(blocks):
                    for b, i, j in blocks:
                        act.wait_ge(t_done[i], after(j + 1))
                        act.wait_ge(m_done[i], after(j))
                        act.activation(xt[i][:, :, :].rearrange("p k n -> p (k n)"), turned[i][:, 0:2 * P],
                                       ACT.Copy).then_inc(t_copied[i], 1)
                    for b, i, j in blocks:
                        act.activation(at(x, b), xs[i][:, :], ACT.Copy).then_inc(kept[i], 1)
                pairs(act, body)
                act.wait_ge(shifted, after(1))
                act.activation(flat(work), flat(work), ACT.Exp).then_inc(expd, 1)

            @block.tensor
            def _(pe):
                pe.wait_ge(loaded, after(32))

                def turn(b, i, j):
                    pe.wait_ge(fed[i], after(j + 1))
                    pe.wait_ge(t_copied[i], after(j))
                    for k in range(2):
                        mm = pe.transpose(turned[i][:, k * P:(k + 1) * P], xs[i][:, k:D:2], g.ident[:, :])
                    mm.then_inc(t_done[i], 1)

                def step(block, following):
                    if following:
                        turn(*following)
                    b, i, j = block
                    pe.wait_ge(t_copied[i], after(j + 1))
                    pe.wait_ge(m_read[i], after(j))
                    for k in range(2):
                        mm = pe.matmul(lg[i][:, 0:NE], xt[i][:, k, :], gw[:, k, :], start=(k == 0), stop=(k == 1))
                    mm.then_inc(m_done[i], 1)

                turn(0, 0, 0)
                lagged(pe, step)
                pe.wait_ge(hotted, after(1))
                W = NB * NE
                pe.matmul(sums[:, 0:W], g.tri_upto[:, :], flat(hot), start=True, stop=True)
                pe.matmul(sums[:, 256:256 + W], g.ones[:, :], flat(hot), start=True, stop=True).then_inc(cumulated, 1)


def experts(nc, g, io):
    KF = FF // P
    Q = SLOTS // P
    with ExitStack() as ctx:
        s = Space(nc, ctx, "exp")
        w1 = [s.sb(f"w1_{i}", [P, 2, FF]) for i in range(2)]
        w2 = s.sb("w2", [P, KF, D])
        b1, b2 = s.sb("b1", [P, NE, KF]), s.sb("b2", [P, D])
        rows = s.sb("rows", [P, Q, D])
        xt = s.sb("xt", [P, 2, SLOTS])
        hid = [s.sb(f"hid{i}", [P, SLOTS]) for i in range(2)]
        y = s.sb("y", [P, Q, D])
        up = [s.ps(f"up{i}") for i in range(2)]
        turned = [s.ps(f"turned{i}") for i in range(2)]
        down = [s.ps(f"down{q}") for q in range(Q)]
        w1_in = [s.sem(f"w1_in{i}") for i in range(2)]
        w2_in, rows_in, b_in, t_done, t_copied, u_done, act_done, d_chunk, d_read, y_left = (
            s.sem(n) for n in ("w2_in", "rows_in", "b_in", "t_done", "t_copied", "u_done", "act_done", "d_chunk",
                               "d_read", "y_left"))
        y_out = s.pool_sem("y_out")
        w1_d = io["L0_ffn_w1"].rearrange("e (p k) f -> e p k f", p=P)
        w2_d = io["L0_ffn_w2"].rearrange("e (p c) d -> e p c d", p=P)
        in_d = g.expert_in.rearrange("(e q p) d -> e p q d", e=NE, p=P)
        out_d = g.expert_out.rearrange("(e q p) d -> e p q d", e=NE, p=P)
        b2_d = io["L0_ffn_b2"]
        one = lambda ap, e: ap[bass.ds(e, 1)].rearrange("a p k f -> (a p) k f")

        def by_parity(eng, body):
            with eng.Fori(0, NE // 2) as j:
                body(2 * j, 0, j)
                body(2 * j + 1, 1, j)

        with s.block() as block:
            @block.sync
            def _(sp):
                sp.dma_start(b1[:, :, :], io["L0_ffn_b1"].rearrange("e (p c) -> p e c", p=P)).then_inc(b_in, 16)
                sp.wait_ge(b_in, after(16))

                def body(e, i, j):
                    sp.wait_ge(t_done, after(2 * Q * e))
                    sp.dma_start(rows[:, :, :], one(in_d, e)).then_inc(rows_in, 16)
                    sp.wait_ge(u_done, after(KF * e))
                    sp.dma_start(w1[i][:, :, :], one(w1_d, e)).then_inc(w1_in[i], 16)
                    sp.wait_ge(d_chunk, after(KF * e))
                    sp.dma_start(w2[:, :, :], one(w2_d, e)).then_inc(w2_in, 16)
                    sp.wait_ge(d_read, after(Q * e))
                    sp.dma_start(b2[:, :], b2_d[bass.ds(e, 1), :].to_broadcast([P, D])).then_inc(b_in, 16)
                by_parity(sp, body)

            @block.gpsimd
            def _(pool):
                with pool.Fori(0, NE) as e:
                    pool.wait_ge(d_read, after(Q * (e + 1)))
                    pool.dma_start(one(out_d, e), y[:, :, :]).then_inc(y_out, 16)
                    pool.wait_ge(y_out, 16 * (e + 1))
                    pool.sem_inc(y_left, 1)

            @block.vector
            def _(dve):
                with dve.Fori(0, NE) as e:
                    dve.wait_ge(b_in, after(16 * (e + 2)))
                    dve.wait_ge(y_left, after(e))
                    for q in range(Q):
                        dve.wait_ge(d_chunk, after(KF * (e + 1)))
                        dve.tensor_tensor(y[:, q, :], down[q][:, 0:D], b2[:, :], ALU.add).then_inc(d_read, 1)

            @block.scalar
            def _(act):
                act.wait_ge(b_in, after(16))
                with act.Fori(0, NE) as e:
                    act.wait_ge(u_done, after(KF * e + KF))
                    for n in range(2 * Q // 4):
                        act.wait_ge(t_done, after(2 * Q * e + 4 * (n + 1)))
                        act.activation(xt[:, n, :], turned[n][:, :], ACT.Copy).then_inc(t_copied, 1)
                    for c in range(KF):
                        act.wait_ge(u_done, after(KF * e + KF + c + 1))
                        if c >= 2:
                            act.wait_ge(d_chunk, after(KF * e + c - 1))
                        else:
                            act.wait_ge(d_chunk, after(KF * e))
                        act.activation(hid[c % 2][:, :], up[c % 2][:, :], ACT.Relu,
                                       bias=b1[:, bass.ds(e, 1), c:c + 1].rearrange("p a f -> p (a f)")).then_inc(act_done, 1)

            @block.tensor
            def _(pe):
                pe.sem_inc(u_done, KF)

                def body(e, i, j):
                    pe.wait_ge(rows_in, after(16 * (e + 1)))
                    pe.wait_ge(t_copied, after(2 * e))
                    for k in range(2):
                        for q in range(Q):
                            pe.transpose(turned[k][:, q * P:(q + 1) * P], rows[:, q, k:D:2], g.ident[:, :]).then_inc(t_done, 1)

                    def first(c):
                        pe.wait_ge(act_done, after(KF * e + c - 1 if c >= 2 else KF * e))
                        for k in range(2):
                            mm = pe.matmul(up[c % 2][:, :], w1[i][:, k, c:FF:KF], xt[:, k, :], start=(k == 0), stop=(k == 1))
                        mm.then_inc(u_done, 1)

                    pe.wait_ge(t_copied, after(2 * (e + 1)))
                    pe.wait_ge(w1_in[i], after(16 * (j + 1)))
                    first(0)
                    for c in range(KF):
                        if c + 1 < KF:
                            first(c + 1)
                        if c == 0:
                            pe.wait_ge(w2_in, after(16 * (e + 1)))
                            pe.wait_ge(d_read, after(Q * e))
                        pe.wait_ge(act_done, after(KF * e + c + 1))
                        for q in range(Q):
                            mm = pe.matmul(down[q][:, 0:D], hid[c % 2][:, q * P:(q + 1) * P], w2[:, c, :],
                                           start=(c == 0), stop=(c == KF - 1), skip_group_check=True)
                        mm.then_inc(d_chunk, 1)
                by_parity(pe, body)


def combine(nc, g, io):
    PART = 5
    parts = NB // PART
    MAX32 = 3.4028234663852886e38
    with ExitStack() as ctx:
        s = Space(nc, ctx, "cmb")
        y, x, z = ([s.sb(f"{n}{i}", [P, PART, D]) for i in range(2)] for n in ("y", "x", "z"))
        mask = s.sb("mask", [P, PART, D])
        edge = s.sb("edge", [P, 2, PART * D])
        loaded, stored, linked, done, shared, zeroed = (
            s.sem(n) for n in ("loaded", "stored", "linked", "done", "shared", "zeroed"))
        came_by = [s.pool_sem(f"came{c}") for c in range(parts)]
        view = lambda d, c: d.rearrange("(b p) d -> p b d", p=P)[:, c * PART:(c + 1) * PART, :]
        with s.block() as block:
            @block.sync
            def _(sp):
                for c in range(parts):
                    if c >= 2:
                        sp.wait_ge(stored, after(16 * (c - 1)))
                    if c >= 1:
                        sp.wait_ge(loaded, after(16 * c))
                    sp.dma_start(x[c % 2][:, :, :], view(g.x_gnn, c)).then_inc(loaded, 16)
                    if c >= 1:
                        sp.wait_ge(done, after(c))
                        sp.dma_start(view(g.x_moe, c - 1), x[(c - 1) % 2][:, :, :]).then_inc(stored, 16)
                sp.wait_ge(done, after(parts))
                sp.dma_start(view(g.x_moe, parts - 1), x[(parts - 1) % 2][:, :, :]).then_inc(stored, 16)
                sp.wait_ge(stored, after(16 * parts))

            @block.gpsimd
            def _(pool):
                for c in range(parts):
                    if c >= 2:
                        pool.wait_ge(done, after(c - 1))
                    pool.memset(z[c % 2][:, :, :], 0.0).then_inc(zeroed, 1)
                    for b in range(PART):
                        col = c * PART + b
                        pool.indirect_dma_start(
                            out=y[c % 2][:, b, :], out_offset=None, in_=g.expert_out,
                            in_offset=bass.IndirectOffsetOnAxis(ap=g.slot_out[:, col:col + 1], axis=0)
                        ).then_inc(came_by[c], 16)

            @block.scalar
            def _(act):
                for c in range(parts):
                    act.wait_ge(came_by[c], 16 * PART)
                    for b in range(PART):
                        col = c * PART + b
                        act.activation(y[c % 2][:, b, :], y[c % 2][:, b, :], ACT.Copy,
                                       scale=g.share[:, col:col + 1]).then_inc(shared, 1)

            @block.vector
            def _(dve):
                link = Linked(dve, linked)
                link(dve.memset(edge[:, 0, :], 1.0e4))
                link(dve.memset(edge[:, 1, :], -1.0e4))
                flat = lambda t: t[:, :, :].rearrange("p b d -> p (b d)")
                for c in range(parts):
                    yc, xc, zc = y[c % 2], x[c % 2], z[c % 2]
                    dve.wait_ge(shared, after(c * PART + PART))
                    dve.wait_ge(zeroed, after(c + 1))
                    link(dve.tensor_tensor(mask[:, :, :], yc[:, :, :], yc[:, :, :], ALU.is_equal))
                    link(dve.copy_predicated(flat(zc), flat(mask).bitcast(I32), flat(yc)))
                    for n, (limit, op) in enumerate(((MAX32, ALU.is_gt), (-MAX32, ALU.is_lt))):
                        link(dve.tensor_scalar(mask[:, :, :], yc[:, :, :], limit, None, op))
                        link(dve.copy_predicated(flat(zc), flat(mask).bitcast(I32), edge[:, n, :]))
                    dve.wait_ge(loaded, after(16 * (c + 1)))
                    link(dve.tensor_tensor(xc[:, :, :], xc[:, :, :], zc[:, :, :], ALU.add))
                    dve.sem_inc(done, 1)


class Gate:

    def __init__(self, s):
        self.w, self.bias, self.junk = s.sb("w", [P, D]), s.sb("bias", [P, 1]), s.sb("junk", [P, D])
        self.h, self.rest = s.sb("h", [P, D]), s.sb("rest", [P, D])
        self.parts = [s.sb(f"parts{i}", [P, 3, D], BF16) for i in range(2)]
        self.dot, self.gate = s.sb("dot", [P, 2]), s.sb("gate", [P, 2])
        self.given, self.linked = s.sem("given"), s.sem("linked")
        self.dotted, self.gated, self.split, self.added = (
            [s.sem(f"{n}{i}") for i in range(2)] for n in ("dotted", "gated", "split", "added"))

    def load(self, sp, io):
        sp.dma_start(self.w[:, :], across(io["L1_gnn_lin_w"].rearrange("a n -> (a n)"), D)).then_inc(self.given, 16)
        sp.dma_start(self.bias[:, :], across(io["L1_gnn_lin_b"], 1)).then_inc(self.given, 16)

    LINKS = 5

    def on_vector(self, dve, link, i, turn, dis, acc_out, acc_in, came=None):
        link(dve.tensor_tensor_reduce(self.junk[:, :], self.h[:, :], self.w[:, :], 1.0, 0.0, ALU.mult, ALU.add,
                                      self.dot[:, i:i + 1]))
        dve.sem_inc(self.dotted[i], 1)
        hi, mid, low = (self.parts[i][:, n, :] for n in range(3))
        link(dve.tensor_scalar(hi, self.h[:, :], dis, None, ALU.mult))
        link(dve.scalar_tensor_tensor(self.rest[:, :], self.h[:, :], dis, hi, ALU.mult, ALU.subtract))
        link(dve.tensor_copy(mid, self.rest[:, :]))
        dve.tensor_tensor(low, self.rest[:, :], mid, ALU.subtract).then_inc(self.split[i], 1)
        dve.wait_ge(self.gated[i], after(turn + 1))
        if came:
            dve.wait_ge(*came)
        link(dve.scalar_tensor_tensor(acc_out, self.h[:, :], self.gate[:, i:i + 1], acc_in, ALU.mult, ALU.add))
        dve.sem_inc(self.added[i], 1)

    def on_scalar(self, act, i, turn):
        act.wait_ge(self.dotted[i], after(turn + 1))
        act.activation(self.gate[:, i:i + 1], self.dot[:, i:i + 1], ACT.Sigmoid,
                       bias=self.bias[:, 0:1]).then_inc(self.gated[i], 1)


TURNS = (-(-NB // 2), NB // 2)


def hop_parts(g, parity, b):
    return g.hop_parts[bass.ds(parity * NP + b * P, P), :]


def hops_start(nc, g, io):
    with ExitStack() as ctx:
        s = Space(nc, ctx, "hp0")
        x = s.sb("x", [P, NB, D])
        acc = [s.sb(f"acc{i}", [P, D]) for i in range(2)]
        norm, gate = Norm(s), Gate(s)
        bn, rows_came = s.sem("bn"), rows_sems(s)
        kept, saved = ([s.sem(f"{n}{i}") for i in range(2)] for n in ("kept", "saved"))
        with s.block() as block:
            @block.sync
            def _(sp):
                load_rows(sp, x, g.x_moe, rows_came)
                gate.load(sp, io)

                def body(blocks):
                    for b, i, j in blocks:
                        sp.wait_ge(gate.split[i], after(j + 1))
                        sp.dma_start(hop_parts(g, 0, b), gate.parts[i][:, :, :].rearrange("p n d -> p (n d)")
                                     ).then_inc(kept[i], 16)
                        sp.wait_ge(gate.added[i], after(j + 1))
                        sp.dma_start(g.x_gcn[bass.ds(b * P, P), :], acc[i][:, :]).then_inc(saved[i], 16)
                pairs(sp, body)
                for i in range(2):
                    sp.wait_ge(kept[i], after(16 * TURNS[i]))
                    sp.wait_ge(saved[i], after(16 * TURNS[i]))

            @block.vector
            def _(dve):
                norm.on_vector(dve, bn, x, rows_came)
                dve.wait_ge(gate.given, after(32))

                def body(blocks):
                    for b, i, j in blocks:
                        link = Linked(dve, gate.linked, (Gate.LINKS + 1) * b)
                        dve.wait_ge(kept[i], after(16 * j))
                        dve.wait_ge(saved[i], after(16 * j))
                        link(norm.block(dve, gate.h[:, :], x, b))
                        gate.on_vector(dve, link, i, j, at(g.dis, b), acc[i][:, :], at(x, b))
                pairs(dve, body)

            @block.scalar
            def _(act):
                norm.on_scalar(act)
                act.wait_ge(gate.given, after(32))
                pairs(act, lambda blocks: [gate.on_scalar(act, i, j) for b, i, j in blocks])


def hops(nc, g, io):
    CHUNK = 5
    with ExitStack() as ctx:
        s = Space(nc, ctx, "hop")
        hs = s.sb("hs", [P, NB, 3 * D], BF16)
        acc = [s.sb(f"acc{i}", [P, D]) for i in range(2)]
        gate = Gate(s)
        wide, narrow = ([s.ps(f"{n}{i}") for i in range(2)] for n in ("wide", "narrow"))
        here = [s.pool_sem(f"here{c}") for c in range(NB // CHUNK)]
        read_last = [s.sem(f"read_last{c}") for c in range(NB // CHUNK - 1)]
        passed = s.sem("passed")
        kept, saved, came, summed, read = ([s.sem(f"{n}{i}") for i in range(2)] for n in (
            "kept", "saved", "came", "summed", "read"))
        with s.block() as block:
            @block.gpsimd
            def _(pool):
                def load(k, c):
                    pool.dma_start(hs[:, c * CHUNK:(c + 1) * CHUNK, :],
                                   g.hop_parts[bass.ds((k % 2) * NP + c * CHUNK * P, CHUNK * P), :].rearrange(
                                       "(b p) d -> p b d", p=P)).then_inc(here[c], 16)

                for c in range(NB // CHUNK):
                    load(0, c)
                with pool.Fori(0, HOPS - 1) as k:
                    for c in range(NB // CHUNK):
                        last = (c + 1) * CHUNK
                        products = (read_last[c], k + 1) if last < NB else (summed[0], TURNS[0] * (k + 1))
                        for done, count in (products, (kept[0], 16 * (TURNS[0] * k + (last + 1) // 2)),
                                            (kept[1], 16 * (TURNS[1] * k + last // 2))):
                            pool.wait_ge(done, after(count))
                            pool.sem_inc(passed, 1)
                        load(k + 1, c)

            @block.sync
            def _(sp):
                gate.load(sp, io)
                with sp.Fori(0, HOPS) as k:
                    def body(blocks):
                        for b, i, j in blocks:
                            turn = k * TURNS[i] + j
                            sp.wait_ge(saved[i], after(16 * turn))
                            sp.dma_start(acc[i][:, :], g.x_gcn[bass.ds(b * P, P), :]).then_inc(came[i], 16)
                        for b, i, j in blocks:
                            turn = k * TURNS[i] + j
                            sp.wait_ge(gate.split[i], after(turn + 1))
                            sp.dma_start(hop_parts(g, (k + 1) % 2, b),
                                         gate.parts[i][:, :, :].rearrange("p n d -> p (n d)")).then_inc(kept[i], 16)
                            sp.wait_ge(gate.added[i], after(turn + 1))
                            sp.dma_start(g.x_gcn[bass.ds(b * P, P), :], acc[i][:, :]).then_inc(saved[i], 16)
                    pairs(sp, body)
                for i in range(2):
                    sp.wait_ge(kept[i], after(16 * TURNS[i] * HOPS))
                    sp.wait_ge(saved[i], after(16 * TURNS[i] * HOPS))

            @block.vector
            def _(dve):
                dve.wait_ge(gate.given, after(32))
                with dve.Fori(0, HOPS) as k:
                    def body(blocks):
                        for b, i, j in blocks:
                            turn = k * TURNS[i] + j
                            link = Linked(dve, gate.linked, (Gate.LINKS + 3) * (k * NB + b))
                            dis = at(g.dis, b)
                            dve.wait_ge(summed[i], after(turn + 1))
                            link(dve.tensor_scalar(gate.h[:, :], narrow[i][:, 0:D], dis, None, ALU.mult))
                            for n in (1, 0):
                                link(dve.scalar_tensor_tensor(gate.h[:, :], wide[i][:, n * D:(n + 1) * D], dis,
                                                              gate.h[:, :], ALU.mult, ALU.add))
                            dve.sem_inc(read[i], 1)
                            dve.wait_ge(kept[i], after(16 * turn))
                            gate.on_vector(dve, link, i, turn, dis, acc[i][:, :], acc[i][:, :],
                                           came=(came[i], after(16 * (turn + 1))))
                    pairs(dve, body)

            @block.scalar
            def _(act):
                act.wait_ge(gate.given, after(32))
                with act.Fori(0, HOPS) as k:
                    pairs(act, lambda blocks: [gate.on_scalar(act, i, k * TURNS[i] + j) for b, i, j in blocks])

            @block.tensor
            def _(pe):
                with pe.Fori(0, HOPS) as k:
                    def body(blocks):
                        for b, i, j in blocks:
                            pe.wait_ge(read[i], after(k * TURNS[i] + j))
                            for t in range(NB):
                                if t % CHUNK == 0:
                                    pe.wait_ge(here[t // CHUNK], 16 * (k + 1))
                                count = g.counts[:, t, bass.ds(b * P, P)]
                                pe.matmul(wide[i][:, :], count, hs[:, t, 0:2 * D], start=(t == 0), stop=(t == NB - 1))
                                mm = pe.matmul(narrow[i][:, 0:D], count, hs[:, t, 2 * D:3 * D], start=(t == 0),
                                               stop=(t == NB - 1))
                                if len(blocks) == 1 and t % CHUNK == CHUNK - 1 and t < NB - 1:
                                    mm.then_inc(read_last[t // CHUNK], 1)
                            mm.then_inc(summed[i], 1)
                    pairs(pe, body)


def slice_weights(nc, g, a, io):
    HW = SH * SD
    with ExitStack() as ctx:
        s = Space(nc, ctx, "swt")
        wx, wxt = s.sb("wx", [P, 2, HW]), s.sb("wxt", [P, 2, 4, P])
        wsl = s.sb("wsl", [P, SG])
        bx, bxw = s.sb("bx", [SD, SH]), s.sb("bxw", [SD, SH, P])
        bsl, inv_t = s.sb("bsl", [P, SG]), s.sb("inv_t", [P, SH])
        turn = [s.ps(f"turn{k}") for k in range(2)]
        both = [s.ps(f"both{o}") for o in range(2)]
        bias_ps = s.ps("bias_ps")
        loaded, linked, turned, copied, ready, folded = (
            s.sem(n) for n in ("loaded", "linked", "turned", "copied", "ready", "folded"))
        nm = lambda n: io[f"L1_ffn_{n}"]
        with s.block() as block:
            @block.sync
            def _(sp):
                sp.dma_start(a.x[:, :, :], g.x_gcn.rearrange("(b p) d -> p b d", p=P)).then_inc(loaded, 16)
                sp.dma_start(wx[:, :, :], nm("W_x").rearrange("(p k) n -> p k n", p=P)).then_inc(loaded, 16)
                for o in range(2):
                    sp.dma_start(wsl[o * SD:(o + 1) * SD, :], nm("W_slice")).then_inc(loaded, 16)
                with nc.allow_non_contiguous_dma(reason="512 numbers"):
                    sp.dma_start(bx[:, :], nm("b_x").rearrange("(h d) -> d h", h=SH)).then_inc(loaded, 16)
                sp.dma_start(bsl[:, :], across(nm("b_slice"), SG)).then_inc(loaded, 16)
                sp.dma_start(inv_t[:, :], across(nm("temperature").rearrange("a h b c -> (a h b c)"), SH)).then_inc(loaded, 16)

            @block.gpsimd
            def _(pool):
                pool.iota(a.valid[:, :], pattern=[[P, NB]], base=0, channel_multiplier=1,
                          allow_small_or_imprecise_dtypes=True).then_inc(ready, 1)

            @block.vector
            def _(dve):
                link = Linked(dve, linked)
                dve.wait_ge(loaded, after(16 * 7))
                dve.wait_ge(ready, after(1))
                link(dve.tensor_scalar(a.valid[:, :], a.valid[:, :], float(N), None, ALU.is_lt))
                link(dve.tensor_scalar(inv_t[:, :], inv_t[:, :], 0.1, 5.0, ALU.max, ALU.min))
                link(dve.reciprocal(inv_t[:, :], inv_t[:, :]))
                link(dve.tensor_copy(bxw[:, :, :], bx[:, :].unsqueeze(2).to_broadcast([SD, SH, P])))
                dve.sem_inc(ready, 1)
                dve.wait_ge(turned, after(2))
                for k in range(2):
                    link(dve.tensor_copy(wxt[:, k, :, :].rearrange("p m n -> p (m n)"), turn[k][:, :]))
                dve.sem_inc(copied, 1)
                dve.wait_ge(folded, after(1))
                for o in range(2):
                    for k in range(2):
                        link(dve.tensor_tensor(
                            a.wxs[:, k, :].rearrange("p (m o s) -> p m o s", o=2, s=SG)[:, :, o, :],
                            both[o][:, k * 256:(k + 1) * 256].rearrange("p (m s) -> p m s", s=SG),
                            inv_t[:, o:SH:2].unsqueeze(2).to_broadcast([P, 4, SG]), ALU.mult))
                heads = lambda t: t.rearrange("p (h s) -> p h s", h=SH)
                link(dve.tensor_tensor(heads(a.bias[:, :]), heads(bias_ps[:, :]),
                                       bsl[:, :].unsqueeze(1).to_broadcast([P, SH, SG]), ALU.add))
                link(dve.tensor_tensor(heads(a.bias[:, :]), heads(a.bias[:, :]),
                                       inv_t[:, :].unsqueeze(2).to_broadcast([P, SH, SG]), ALU.mult))

            @block.tensor
            def _(pe):
                pe.wait_ge(loaded, after(16 * 7))
                for k in range(2):
                    for m in range(4):
                        mm = pe.transpose(turn[k][:, m * P:(m + 1) * P], wx[:, k, m * P:(m + 1) * P], g.ident[:, :])
                    mm.then_inc(turned, 1)
                pe.wait_ge(ready, after(2))
                for h in range(SH):
                    pe.matmul(bias_ps[:, h * SG:(h + 1) * SG], bxw[:, h, :], wsl[0:SD, :], start=True, stop=True)
                pe.wait_ge(copied, after(1))
                for o in range(2):
                    half = slice(o * SD, (o + 1) * SD)
                    for k in range(2):
                        for m in range(4):
                            c = (k * 4 + m) * SG
                            mm = pe.matmul(both[o][:, c:c + SG], wxt[half, k, m, :], wsl[half, :], start=True, stop=True)
                mm.then_inc(folded, 1)


def slice_tokens(nc, g, a, io):
    HW = SH * SG
    with ExitStack() as ctx:
        s = Space(nc, ctx, "tok")
        xs = [s.sb(f"xs{i}", [P, D + 1]) for i in range(2)]
        xt = [s.sb(f"xt{i}", [P, 2, P]) for i in range(2)]
        sw = [s.sb(f"sw{i}", [P, HW]) for i in range(2)]
        peak, total = s.sb("peak", [P, SH]), s.sb("total", [P, SH])
        zero = s.sb("zero", [P, P])
        norm = Norm(s)
        turned, flipped = s.ps("turned"), s.ps("flipped")
        lg = [s.ps(f"lg{i}") for i in range(2)]
        tok = [s.ps(f"tok{m}") for m in range(4)]
        bn, linked, summed, zeroed = s.sem("bn"), s.sem("linked"), s.sem("summed"), s.sem("zeroed")
        fed, t_done, t_copied, m_done, m_read, shifted, expd, soft, tok_done = (
            [s.sem(f"{n}{i}") for i in range(2)] for n in (
                "fed", "t_done", "t_copied", "m_done", "m_read", "shifted", "expd", "soft", "tok_done"))
        f_done, f_copied = s.sem("f_done"), s.sem("f_copied")
        heads = lambda t: t.rearrange("p (h s) -> p h s", h=SH)
        wide = lambda t: t[:, :].unsqueeze(2).to_broadcast([P, SH, SG])
        with s.block() as block:
            @block.vector
            def _(dve):
                norm.on_vector(dve, bn, a.x)
                dve.tensor_tensor(norm.rstd[:, :], norm.rstd[:, :], a.valid[:, :], ALU.mult).then_inc(zeroed, 1)
                dve.memset(zero[:, :], 0.0).then_inc(zeroed, 1)
                dve.wait_ge(zeroed, after(2))

                def feed(b, i, j):
                    dve.wait_ge(tok_done[i], after(j))
                    dve.tensor_copy(xs[i][:, D:D + 1], at(a.valid, b))
                    norm.block(dve, xs[i][:, 0:D], a.x, b).then_inc(fed[i], 1)

                def step(block, following):
                    b, i, j = block
                    link = Linked(dve, linked, 6 * b)
                    w = heads(sw[i][:, :])
                    dve.wait_ge(m_done[i], after(j + 1))
                    link(dve.tensor_tensor(sw[i][:, :], lg[i][:, :], a.bias[:, :], ALU.add))
                    dve.sem_inc(m_read[i], 1)
                    link(dve.tensor_reduce(peak[:, :], w, AX, ALU.max))
                    link(dve.tensor_tensor(w, w, wide(peak), ALU.subtract))
                    dve.sem_inc(shifted[i], 1)
                    if following:
                        feed(*following)
                    dve.wait_ge(expd[i], after(j + 1))
                    link(dve.tensor_reduce(total[:, :], w, AX, ALU.add))
                    link(dve.reciprocal(total[:, :], total[:, :]))
                    link(dve.tensor_tensor(w, w, wide(total), ALU.mult))
                    dve.sem_inc(soft[i], 1)

                feed(0, 0, 0)
                lagged(dve, step)
                dve.wait_ge(summed, after(1))
                for m in range(4):
                    dve.tensor_copy(a.tok[:, m, 0:D + 1], tok[m][:, 0:D + 1])

            @block.scalar
            def _(act):
                norm.on_scalar(act)

                def turn_copy(b, i, j):
                    act.wait_ge(t_done[i], after(j + 1))
                    act.wait_ge(m_done[i], after(j))
                    act.activation(xt[i][:, :, :].rearrange("p k n -> p (k n)"),
                                   turned[:, i * D:(i + 1) * D], ACT.Copy).then_inc(t_copied[i], 1)

                def step(block, following):
                    b, i, j = block
                    act.wait_ge(shifted[i], after(j + 1))
                    act.activation(sw[i][:, :], sw[i][:, :], ACT.Exp).then_inc(expd[i], 1)
                    if following:
                        turn_copy(*following)
                    act.wait_ge(f_done, after(b + 1))
                    act.activation(at(a.swt, b), flipped[:, :], ACT.Copy).then_inc(f_copied, 1)

                turn_copy(0, 0, 0)
                lagged(act, step)

            @block.tensor
            def _(pe):
                pe.wait_ge(zeroed, after(2))
                for m in range(4):
                    pe.matmul(tok[m][:, 0:D + 1], zero[:, :], a.x[:, 0:2, :].rearrange("p b d -> p (b d)")[:, 0:D + 1],
                              start=True, stop=False, skip_group_check=True)

                def logits(b, i, j):
                    pe.wait_ge(fed[i], after(j + 1))
                    pe.wait_ge(t_copied[1 - i], after(j + i))
                    for k in range(2):
                        mm = pe.transpose(turned[:, i * D + k * P:i * D + (k + 1) * P], xs[i][:, k:D:2], g.ident[:, :])
                    mm.then_inc(t_done[i], 1)
                    pe.wait_ge(t_copied[i], after(j + 1))
                    pe.wait_ge(m_read[i], after(j))
                    for k in range(2):
                        mm = pe.matmul(lg[i][:, :], xt[i][:, k, :], a.wxs[:, k, :], start=(k == 0), stop=(k == 1))
                    mm.then_inc(m_done[i], 1)

                def step(block, following):
                    b, i, j = block
                    if following:
                        logits(*following)
                    pe.wait_ge(soft[i], after(j + 1))
                    pe.wait_ge(f_copied, after(b))
                    for m in range(4):
                        mm = pe.transpose(flipped[:, m * P:(m + 1) * P], sw[i][:, m * P:(m + 1) * P], g.ident[:, :])
                    mm.then_inc(f_done, 1)
                    for m in range(4):
                        mm = pe.matmul(tok[m][:, 0:D + 1], sw[i][:, m * P:(m + 1) * P], xs[i][:, :], start=False,
                                       stop=False, skip_group_check=True)
                    mm.then_inc(tok_done[i], 1)

                logits(0, 0, 0)
                lagged(pe, step)
                for m in range(4):
                    mm = pe.matmul(tok[m][:, 0:P], zero[:, :], zero[:, :], start=False, stop=True, skip_group_check=True)
                mm.then_inc(summed, 1)


def slice_attention(nc, g, a, io):
    with ExitStack() as ctx:
        s = Space(nc, ctx, "att")
        HW = SH * SD
        wfx, bfx = s.sb("wfx", [P, 2, HW]), s.sb("bfx", [1, HW])
        wq, wk, wv = (s.sb(n, [SD, SD]) for n in ("wq", "wk", "wv"))
        wo = s.sb("wo", [SD, SH, D])
        inv = s.sb("inv", [P, 4])
        tokt, normt = s.sb("tokt", [P, 2, 4 * P]), s.sb("normt", [1, 4 * P])
        st, qt, kt, v, at_, att, ot = (s.sb(n, [SD, SH, SG]) for n in ("st", "qt", "kt", "v", "at", "att", "ot"))
        peak = s.sb("peak", [SG, SH])
        A, B, C, Dd = (s.ps(n) for n in "ABCD")
        O = [s.ps(f"O{m}") for m in range(4)]
        loaded, linked, vec, ten, expd = (s.sem(n) for n in ("loaded", "linked", "vec", "ten", "expd"))
        nm = lambda n: io[f"L1_ffn_{n}"]
        fl = lambda t: t[:, :, :].rearrange("p h g -> p (h g)")
        wide = lambda t: t[:, :].unsqueeze(2).to_broadcast([SG, SH, SG])
        with s.block() as block:
            @block.sync
            def _(sp):
                sp.dma_start(wfx[:, :, :], nm("W_fx").rearrange("(k p) n -> p k n", p=P)).then_inc(loaded, 16)
                sp.dma_start(bfx[:, :], nm("b_fx").rearrange("(a n) -> a n", a=1)).then_inc(loaded, 16)
                for w, n in ((wq, "W_q"), (wk, "W_k"), (wv, "W_v")):
                    sp.dma_start(w[:, :], nm(n)).then_inc(loaded, 16)
                sp.dma_start(wo[:, :, :], nm("W_out").rearrange("(h c) d -> c h d", h=SH)).then_inc(loaded, 16)

            @block.vector
            def _(dve):
                link = Linked(dve, linked)
                link(dve.tensor_scalar(inv[:, :], a.tok[:, :, D], 1e-5, None, ALU.add))
                link(dve.reciprocal(inv[:, :], inv[:, :]))
                link(dve.tensor_tensor(a.tok[:, :, 0:D + 1], a.tok[:, :, 0:D + 1],
                                       inv[:, :].unsqueeze(2).to_broadcast([P, 4, D + 1]), ALU.mult))
                dve.sem_inc(vec, 1)
                dve.wait_ge(ten, after(1))
                for k, src in enumerate((A, B)):
                    link(dve.tensor_copy(tokt[:, k, :], src[:, :]))
                link(dve.tensor_copy(normt[:, :], C[0:1, :]))
                dve.sem_inc(vec, 1)
                dve.wait_ge(ten, after(2))
                for h in range(SH):
                    m, o = h // 2, h % 2
                    link(dve.tensor_copy(st[:, h, :], Dd[o * SD:(o + 1) * SD, m * P + o * SG:m * P + (o + 1) * SG]))
                dve.sem_inc(vec, 1)
                dve.wait_ge(ten, after(3))
                for dst, src in ((qt, A), (kt, B), (v, C)):
                    link(dve.tensor_copy(fl(dst), src[0:SD, :]))
                dve.sem_inc(vec, 1)
                dve.wait_ge(ten, after(4))
                link(dve.tensor_copy(fl(at_), Dd[0:SD, :]))
                link(dve.tensor_reduce(peak[:, :], at_[:, :, :], AX, ALU.max))
                link(dve.tensor_tensor(at_[:, :, :], at_[:, :, :], wide(peak), ALU.subtract))
                dve.sem_inc(vec, 1)
                dve.wait_ge(expd, after(1))
                link(dve.tensor_reduce(peak[:, :], at_[:, :, :], AX, ALU.add))
                link(dve.reciprocal(peak[:, :], peak[:, :]))
                link(dve.tensor_tensor(at_[:, :, :], at_[:, :, :], wide(peak), ALU.mult))
                dve.sem_inc(vec, 1)
                dve.wait_ge(ten, after(5))
                link(dve.tensor_copy(fl(att), A[0:SD, :]))
                dve.sem_inc(vec, 1)
                dve.wait_ge(ten, after(6))
                link(dve.tensor_copy(fl(ot), B[0:SD, :]))
                dve.sem_inc(vec, 1)
                dve.wait_ge(ten, after(7))
                for h in range(SH):
                    m, o = h // 2, h % 2
                    link(dve.tensor_copy(a.v2[o * SG:(o + 1) * SG, m, :], O[m][0:SG, o * D:(o + 1) * D]))

            @block.scalar
            def _(act):
                act.wait_ge(vec, after(5))
                act.activation(fl(at_), fl(at_), ACT.Exp, scale=float(SD) ** -0.5).then_inc(expd, 1)

            @block.tensor
            def _(pe):
                pe.wait_ge(loaded, after(16 * 6))
                pe.wait_ge(vec, after(1))
                for m in range(4):
                    for k, dst in enumerate((A, B)):
                        pe.transpose(dst[:, m * P:(m + 1) * P], a.tok[:, m, k * P:(k + 1) * P], g.ident[:, :])
                    mm = pe.transpose(C[0:1, m * P:(m + 1) * P], a.tok[:, m, D:D + 1], g.ident[:, :])
                mm.then_inc(ten, 1)
                pe.wait_ge(vec, after(2))
                for m in range(4):
                    cols = slice(m * P, (m + 1) * P)
                    for k in range(2):
                        pe.matmul(Dd[:, cols], wfx[:, k, cols], tokt[:, k, cols], start=(k == 0), stop=False)
                    mm = pe.matmul(Dd[:, cols], bfx[0:1, cols], normt[0:1, cols], start=False, stop=True)
                mm.then_inc(ten, 1)
                pe.wait_ge(vec, after(3))
                pe.matmul(A[0:SD, :], wq[:, :], fl(st), start=True, stop=True)
                pe.matmul(B[0:SD, :], wk[:, :], fl(st), start=True, stop=True)
                each = lambda dst, lhs, rhs: [pe.matmul(dst[0:SD, h * SG:(h + 1) * SG], lhs(h), rhs(h), start=True,
                                                        stop=True) for h in range(SH)][-1]
                each(C, lambda h: st[:, h, :], lambda h: wv[:, :]).then_inc(ten, 1)
                pe.wait_ge(vec, after(4))
                each(Dd, lambda h: qt[:, h, :], lambda h: kt[:, h, :]).then_inc(ten, 1)
                pe.wait_ge(vec, after(6))
                for h in range(SH):
                    mm = pe.transpose(A[0:SD, h * SG:(h + 1) * SG], at_[:, h, :], g.ident[0:SG, 0:SG])
                mm.then_inc(ten, 1)
                pe.wait_ge(vec, after(7))
                each(B, lambda h: v[:, h, :], lambda h: att[:, h, :]).then_inc(ten, 1)
                pe.wait_ge(vec, after(8))
                for h in range(SH):
                    m, o = h // 2, h % 2
                    mm = pe.matmul(O[m][0:SG, o * D:(o + 1) * D], ot[:, h, :], wo[:, h, :], start=True, stop=True)
                mm.then_inc(ten, 1)


def slice_output(nc, g, a, io, out):
    with ExitStack() as ctx:
        s = Space(nc, ctx, "out")
        now = [s.sb(f"now{i}", [P, SH * SG]) for i in range(2)]
        y = [s.sb(f"y{i}", [P, D]) for i in range(2)]
        bias = s.sb("bias", [P, D])
        acc = [s.ps(f"acc{i}") for i in range(2)]
        loaded, linked = s.sem("loaded"), s.sem("linked")
        copied, done, made, stored = ([s.sem(f"{n}{i}") for i in range(2)] for n in ("copied", "done", "made", "stored"))
        with s.block() as block:
            @block.sync
            def _(sp):
                sp.dma_start(bias[:, :], across(io["L1_ffn_b_out"], D)).then_inc(loaded, 16)

                def body(blocks):
                    for b, i, j in blocks:
                        sp.wait_ge(made[i], after(j + 1))
                        sp.dma_start(out[bass.ds(b * P, P), :], y[i][:, :]).then_inc(stored[i], 16)
                pairs(sp, body)
                for i in range(2):
                    sp.wait_ge(stored[i], after(16 * TURNS[i]))

            @block.scalar
            def _(act):
                def body(blocks):
                    for b, i, j in blocks:
                        act.wait_ge(done[i], after(j))
                        act.activation(now[i][:, :], at(a.swt, b), ACT.Copy).then_inc(copied[i], 1)
                pairs(act, body)

            @block.tensor
            def _(pe):
                def body(blocks):
                    for b, i, j in blocks:
                        pe.wait_ge(copied[i], after(j + 1))
                        pe.wait_ge(made[i], after(j))
                        for m in range(4):
                            mm = pe.matmul(acc[i][:, 0:D], now[i][:, m * P:(m + 1) * P], a.v2[:, m, :], start=(m == 0),
                                           stop=(m == 3))
                        mm.then_inc(done[i], 1)
                pairs(pe, body)

            @block.vector
            def _(dve):
                dve.wait_ge(loaded, after(16))

                def body(blocks):
                    for b, i, j in blocks:
                        link = Linked(dve, linked, b)
                        dve.wait_ge(done[i], after(j + 1))
                        dve.wait_ge(stored[i], after(16 * j))
                        link(dve.tensor_tensor(y[i][:, :], acc[i][:, 0:D], bias[:, :], ALU.add))
                        dve.tensor_tensor(y[i][:, :], y[i][:, :], at(a.x, b), ALU.add).then_inc(made[i], 1)
                pairs(dve, body)


def main_program(nc, io, out):
    with ExitStack() as whole:
        g = Space(nc, whole, "all")
        dram = lambda name, shape, dt=F32: nc.dram_tensor(name, shape, dt, kind="Internal").ap()
        g.edge_fill, g.edge_scan = dram("edge_fill", [EP, SW]), dram("edge_scan", [EP, SW])
        g.edge_w = dram("edge_w", [EP * 4])
        g.edge_terms = dram("edge_terms", [sum(HEADS), EP])
        g.hx_rows, g.small = dram("hx_rows", [NP, ROW]), dram("small", [NP, SW])
        g.expert_in, g.expert_out = dram("expert_in", [NE * SLOTS, D]), dram("expert_out", [NE * SLOTS, D])
        g.x_norm, g.x_mid, g.x_gnn, g.x_moe, g.x_gcn = (
            dram(n, [NP, D]) for n in ("x_norm", "x_mid", "x_gnn", "x_moe", "x_gcn"))
        g.hop_parts = dram("hop_parts", [2 * NP, 3 * D], BF16)
        g.ident, g.count, g.ones = g.sb("ident", [P, P]), g.sb("count", [P, P]), g.sb("ones", [P, P])
        g.tri_upto, g.tri_below = g.sb("tri_upto", [P, P]), g.sb("tri_below", [P, P])
        g.dis, g.share = g.sb("dis", [P, NB]), g.sb("share", [P, NB])
        g.slot_in, g.slot_out = g.sb("slot_in", [P, NB], I32), g.sb("slot_out", [P, NB], I32)
        constants(nc, g)
        with ExitStack() as counted:
            g.counts = counted.enter_context(nc.sbuf_tensor("counts", [P, NB, NP], F16))
            with ExitStack() as graph:
                sb = lambda n, shape, dt=F32: graph.enter_context(nc.sbuf_tensor(n, shape, dt))
                g.src_i, g.dst_f = sb("src_i", [P, ET], I32), sb("dst_f", [P, ET])
                g.indeg, g.inv_deg, g.has, g.minus_base = (sb(n, [P, NB]) for n in ("indeg", "inv_deg", "has", "minus_base"))
                g.seg_start, g.seg_end = sb("seg_start", [P, NB], I32), sb("seg_end", [P, NB], I32)
                g.tiles, g.tile_pairs = sb("tiles", [P, NB + 1], I32), sb("tile_pairs", [P, NB + 1], I32)
                g.small_sb = sb("small_sb", [P, NB, SW])
                g.node_d, g.w_self = sb("node_d", [P, NB, 4]), sb("w_self", [P, NB, 4])
                graph_tables(nc, g, io)
                project_nodes(nc, g, io, 0, io["x"], True)
                c_space = Space(nc, graph, "count")
                c_sems = [c_space.sem(n) for n in ("hot", "used", "summed", "act_read", "dve_read")]
                c_space.arm()
                for layer, target in enumerate((g.x_mid, g.x_gnn)):
                    if layer:
                        project_nodes(nc, g, io, layer, g.x_mid, False)
                    with ExitStack() as held:
                        words = max(ET * (SW + 1), ET * SW + 2 * NB * SW, RING * ROW)
                        room = held.enter_context(nc.sbuf_tensor(f"room{layer}", [P, words], F32))
                        g.per_edge = room[:, 0:ET * SW].rearrange("p (j c) -> p j c", c=SW)
                        g.ids = room[:, ET * SW:ET * (SW + 1)].bitcast(I32)
                        g.spare = room[:, ET * SW:ET * SW + 2 * NB * SW].rearrange("p (n b c) -> p n b c", n=2, c=SW)
                        g.ring = room[:, 0:RING * ROW].rearrange("p (k c) -> p k c", c=ROW)
                        counts_and_gather(nc, g, io, c_sems, ((0, SPLIT), (SPLIT, NB))[layer], layer == 0)
                        g.w_cols = held.enter_context(nc.sbuf_tensor(f"w_cols{layer}", [P, ET, 4], F32))
                        edge_weights(nc, g, io, layer)
                        aggregate(nc, g, io, layer, target)
            route(nc, g, io)
            experts(nc, g, io)
            combine(nc, g, io)
            hops_start(nc, g, io)
            hops(nc, g, io)
        with ExitStack() as slices:
            a = Space(nc, slices, "slc")
            a.x, a.swt = a.sb("x", [P, NB, D]), a.sb("swt", [P, NB, SH * SG])
            a.wxs, a.bias, a.valid = a.sb("wxs", [P, 2, SH * SG]), a.sb("bias", [P, SH * SG]), a.sb("valid", [P, NB])
            a.tok, a.v2 = a.sb("tok", [P, 4, D + 1]), a.sb("v2", [P, 4, D])
            slice_weights(nc, g, a, io)
            slice_tokens(nc, g, a, io)
            slice_attention(nc, g, a, io)
            slice_output(nc, g, a, io, out)


def kernel(**inputs):
    import numpy as np
    import concourse.bacc as bacc
    from concourse.bass_utils import run_bass_kernel_spmd

    a = {k: np.ascontiguousarray(v) for k, v in inputs.items()}
    pad = lambda v, n, fill=0: np.concatenate([v, np.full((n - len(v), *v.shape[1:]), fill, v.dtype)])
    x, src, dst, ea = a.pop("x"), a.pop("src"), a.pop("dst"), a.pop("edge_attr_32")
    src, dst, ea = pad(src, EP, NP - 1), pad(dst, EP, NP - 1), pad(ea, EP)
    arrays = {
        "x": pad(x, NP),
        "src_cols": src.reshape(ET, P).T, "dst_cols": dst.reshape(ET, P).T,
        "src_rows": src.reshape(P, ET),
        "dst_after": np.concatenate([np.full(1, -1, dst.dtype), dst]),
        "edge_attr": ea.T,
        **a,
    }
    arrays = {"in_" + k: np.ascontiguousarray(v).reshape(v.shape or (1,)) for k, v in arrays.items()}
    nc = bacc.Bacc("TRN2", target_bir_lowering=False, num_devices=1)
    io = {k[3:]: nc.dram_tensor(k, v.shape, mybir.dt.from_np(v.dtype), kind="ExternalInput").ap()
          for k, v in arrays.items()}
    out = nc.dram_tensor("out_0_dram", (NP, D), F32, kind="ExternalOutput").ap()
    main_program(nc, io, out)
    r = run_bass_kernel_spmd(nc, [arrays], core_ids=[0])
    return r.results[0]["out_0_dram"][:N]
```
